# Optimizing a Trainium2 kernel written in Bass

```python
import numpy as np
import jax
import jax.numpy as jnp

def _softmax(x, axis=-1):
    return jax.nn.softmax(x, axis=axis)

def _gelu(x):
    return jax.nn.gelu(x, approximate=True)

def _silu(x):
    return jax.nn.silu(x)

def _sigmoid(x):
    return jax.nn.sigmoid(x)

def _layernorm(x, axis=-1, eps=1e-05):
    m = jnp.mean(x, axis=axis, keepdims=True)
    v = jnp.var(x, axis=axis, keepdims=True)
    return (x - m) / jnp.sqrt(v + eps)

def _scatter_add(tgt, idx, src, axis=0):
    return tgt.at[idx].add(src)

def _segment_sum(src, seg, n):
    return jax.ops.segment_sum(src, seg, n)
kernel_name = 'mk_flamingo_gated_d2_seqx_r4_729998'

def setup_inputs(seed: int=0):
    np.random.seed(seed)
    _w = jnp.asarray

    def _rec_inputs():
        import jax
        import jax.numpy as jnp
        _rk = jax.random.key(seed)
        x = -0.0002928 + 1 * jax.random.normal(jax.random.fold_in(_rk, 1), (16, 128, 256), jnp.float32)
        _lenS = 128 - jax.random.randint(jax.random.fold_in(_rk, 7), (16,), 0, max(1, 128 // 4) + 1, jnp.int32)
        _lenS2 = 128 - jax.random.randint(jax.random.fold_in(_rk, 8), (16,), 0, max(1, 128 // 4) + 1, jnp.int32)
        _ctx_1024P = jax.random.normal(jax.random.fold_in(_rk, 11), (16, 16, 256), jnp.float32)
        _ctx_1024c = jax.random.dirichlet(jax.random.fold_in(_rk, 511), 0.3 * jnp.ones((16,), jnp.float32), (16, 128))
        _ctx_1024t = jnp.einsum('bsk,bkd->bsd', _ctx_1024c, _ctx_1024P)
        _ctx_1024t = _ctx_1024t * jax.lax.rsqrt(jnp.mean(jnp.square(_ctx_1024t)) + 1e-12) * 0.953939
        ctx_1024 = -1.39393e-06 + 0.999914 * (_ctx_1024t + 0.3 * jax.random.normal(jax.random.fold_in(_rk, 611), (16, 128, 256), jnp.float32))
        _validS = jnp.arange(128)[None, :] < _lenS[:, None]
        _validS2 = jnp.arange(128)[None, :] < _lenS2[:, None]
        _causal = jnp.tril(jnp.ones((128, 128), dtype=bool))
        mask_1x1xSxS2_if1 = jnp.where(jnp.ones((1, 1, 128, 128), dtype=bool), 1, 0).astype(jnp.int32)
        mask_BxSxS2_fk0 = jnp.where(jnp.broadcast_to(_validS2[:, None, :], (16, 128, 128)), 0.0, 1.0).astype(jnp.float32)
        _g = jax.random.normal(jax.random.fold_in(_rk, 9001), (2, 2), jnp.float32)
        _g = jnp.sign(_g) * jnp.maximum(jnp.abs(_g), 1.0) + (_g == 0) * 1.0
        g_xattn = _g[0]
        g_ffn = _g[1]
        return (x, ctx_1024, mask_1x1xSxS2_if1, mask_BxSxS2_fk0, g_xattn, g_ffn)
    x, ctx_1024, mask_1x1xSxS2_if1, mask_BxSxS2_fk0, g_xattn, g_ffn = _rec_inputs()

    def _L0_xattn_setup():
        import jax, jax.numpy as jnp
        import numpy as np
        D_MODEL = 256
        H = 16
        D_K = D_MODEL // H
        B, S = (2, 512)
        NEG = -1000000000.0

        def _split_heads(x):
            b, s, _ = x.shape
            return x.reshape(b, s, H, D_K).transpose(0, 2, 1, 3)
        key = jax.random.key(seed)
        ks = jax.random.split(key, 8)
        scale = 1.0 / np.sqrt(D_MODEL)
        return {'q': jax.random.normal(ks[0], (B, S, D_MODEL), jnp.float32), 'k': jax.random.normal(ks[1], (B, S, D_MODEL), jnp.float32), 'v': jax.random.normal(ks[2], (B, S, D_MODEL), jnp.float32), 'mask': jnp.ones((1, 1, S, S), jnp.int32), 'Wq': jax.random.normal(ks[3], (D_MODEL, D_MODEL), jnp.float32) * scale, 'bq': jnp.zeros((D_MODEL,), jnp.float32), 'Wk': jax.random.normal(ks[4], (D_MODEL, D_MODEL), jnp.float32) * scale, 'bk': jnp.zeros((D_MODEL,), jnp.float32), 'Wv': jax.random.normal(ks[5], (D_MODEL, D_MODEL), jnp.float32) * scale, 'bv': jnp.zeros((D_MODEL,), jnp.float32), 'Wo': jax.random.normal(ks[6], (D_MODEL, D_MODEL), jnp.float32) * scale, 'bo': jnp.zeros((D_MODEL,), jnp.float32)}
    _L0_xattn_all = _L0_xattn_setup()
    _L0_xattn_in = {k: v for k, v in _L0_xattn_all.items() if k in ('Wq', 'bq', 'Wk', 'bk', 'Wv', 'bv', 'Wo', 'bo')}
    del _L0_xattn_all

    def _L0_ffn_setup():
        import jax, jax.numpy as jnp
        import numpy as np
        import math
        GOLDEN_CENTER = 1.0 / math.e
        GOLDEN_LOWER = 0.5 - math.log(4.0 / 3.0)
        GOLDEN_UPPER = 0.5
        B, T, D = (4, 512, 256)
        E = 8
        I = 1024 // (E // 2)

        def _routing_weights(x, Wr, temperature):
            inh = jax.nn.sigmoid(x @ Wr / temperature)
            in_zone = (inh >= GOLDEN_LOWER) & (inh <= GOLDEN_UPPER)
            dist = jnp.abs(inh - GOLDEN_CENTER)
            w = jnp.exp(-dist / 0.1) * in_zone.astype(x.dtype)
            wsum = w.sum(axis=-1, keepdims=True)
            no_expert = wsum < 1e-08
            fb = jnp.exp(-dist / 0.3)
            _, top2 = jax.lax.top_k(fb, 2)
            fb_mask = jax.nn.one_hot(top2, E, dtype=x.dtype).sum(axis=-2)
            fb_w = fb * fb_mask
            fb_w = fb_w / jnp.clip(fb_w.sum(axis=-1, keepdims=True), 1e-08)
            w = jnp.where(no_expert, fb_w, w)
            wsum = w.sum(axis=-1, keepdims=True)
            return w / jnp.clip(wsum, 1e-08)
        key = jax.random.key(seed)
        k = jax.random.split(key, 6)
        s_d = 1.0 / math.sqrt(D)
        s_i = 1.0 / math.sqrt(I)
        return {'x': jax.random.normal(k[0], (B, T, D), jnp.float32), 'Wg': jax.random.normal(k[1], (E, D, I), jnp.float32) * s_d, 'Wu': jax.random.normal(k[2], (E, D, I), jnp.float32) * s_d, 'Wd': jax.random.normal(k[3], (E, I, D), jnp.float32) * s_i, 'Wr': jax.random.normal(k[4], (D, E), jnp.float32) * s_d, 'temperature': jnp.ones((1,), jnp.float32)}
    _L0_ffn_all = _L0_ffn_setup()
    _L0_ffn_in = {k: v for k, v in _L0_ffn_all.items() if k in ('Wg', 'Wu', 'Wd', 'Wr', 'temperature')}
    del _L0_ffn_all

    def _L1_xattn_setup():
        import jax, jax.numpy as jnp
        import numpy as np
        INPUT_DIM, ATTN_DIM, OUTPUT_DIM = (256, 256, 256)
        B, LQ, LKV = (4, 512, 512)
        key = jax.random.key(seed)
        ks = jax.random.split(key, 10)
        s = 1.0 / np.sqrt(INPUT_DIM)
        return {'primary': jax.random.normal(ks[0], (B, LQ, INPUT_DIM), jnp.float32), 'context_sequence': jax.random.normal(ks[1], (B, LKV, INPUT_DIM), jnp.float32), 'mask': jax.random.randint(ks[2], (B, LQ, LKV), 0, 2).astype(jnp.float32), 'Wq': jax.random.uniform(ks[3], (INPUT_DIM, ATTN_DIM), jnp.float32, -s, s), 'bq': jax.random.uniform(ks[4], (ATTN_DIM,), jnp.float32, -s, s), 'Wk': jax.random.uniform(ks[5], (INPUT_DIM, ATTN_DIM), jnp.float32, -s, s), 'bk': jax.random.uniform(ks[6], (ATTN_DIM,), jnp.float32, -s, s), 'Wv': jax.random.uniform(ks[7], (INPUT_DIM, OUTPUT_DIM), jnp.float32, -s, s), 'bv': jax.random.uniform(ks[8], (OUTPUT_DIM,), jnp.float32, -s, s)}
    _L1_xattn_all = _L1_xattn_setup()
    _L1_xattn_in = {k: v for k, v in _L1_xattn_all.items() if k in ('Wq', 'bq', 'Wk', 'bk', 'Wv', 'bv')}
    del _L1_xattn_all

    def _L1_ffn_setup():
        import jax, jax.numpy as jnp
        import numpy as np
        CAPACITY_FACTOR = 1.0

        def _top1_gate(x2d, wg):
            S, _ = x2d.shape
            E = wg.shape[1]
            C = int(CAPACITY_FACTOR * S / E)
            logits = x2d @ wg
            gates = jax.nn.softmax(logits, axis=-1)
            idx = jnp.argmax(gates, axis=-1)
            mask = jax.nn.one_hot(idx, E, dtype=jnp.int32)
            loc = jnp.cumsum(mask, axis=0) - 1
            me = jnp.mean(gates, axis=0)
            ce = jnp.mean(mask.astype(gates.dtype), axis=0)
            l_aux = E * jnp.sum(me * ce)
            mask = mask * (loc < C).astype(jnp.int32)
            gate_s = jnp.sum(gates * mask, axis=-1)
            loc_s = jnp.sum(loc * mask, axis=-1)
            loc_oh = jax.nn.one_hot(loc_s, C, dtype=gates.dtype)
            combine = (gate_s[:, None] * mask.astype(gates.dtype))[:, :, None] * loc_oh[:, None, :]
            dispatch = (combine > 0).astype(gates.dtype)
            return (l_aux, combine, dispatch)
        key = jax.random.key(seed)
        k1, k2, k3, k4 = jax.random.split(key, 4)
        s, b, m, E, ffn = (512, 4, 256, 8, 1024)
        x = jax.random.normal(k1, (s, b, m), dtype=jnp.float32)
        wg = jax.random.normal(k2, (m, E), dtype=jnp.float32) * 0.02
        w1 = jax.random.normal(k3, (E, m, ffn), dtype=jnp.float32) * 0.02
        w2 = jax.random.normal(k4, (E, ffn, m), dtype=jnp.float32) * 0.02
        return {'x': x, 'wg': wg, 'w1': w1, 'w2': w2}
    _L1_ffn_all = _L1_ffn_setup()
    _L1_ffn_in = {k: v for k, v in _L1_ffn_all.items() if k in ('wg', 'w1', 'w2')}
    del _L1_ffn_all
    return {'x': x, 'ctx_1024': ctx_1024, 'mask_1x1xSxS2_if1': mask_1x1xSxS2_if1, 'mask_BxSxS2_fk0': mask_BxSxS2_fk0, 'g_xattn': g_xattn, 'g_ffn': g_ffn, 'L0_xattn_Wq': _L0_xattn_in['Wq'], 'L0_xattn_bq': _L0_xattn_in['bq'], 'L0_xattn_Wk': _L0_xattn_in['Wk'], 'L0_xattn_bk': _L0_xattn_in['bk'], 'L0_xattn_Wv': _L0_xattn_in['Wv'], 'L0_xattn_bv': _L0_xattn_in['bv'], 'L0_xattn_Wo': _L0_xattn_in['Wo'], 'L0_xattn_bo': _L0_xattn_in['bo'], 'L0_ffn_Wg': _L0_ffn_in['Wg'], 'L0_ffn_Wu': _L0_ffn_in['Wu'], 'L0_ffn_Wd': _L0_ffn_in['Wd'], 'L0_ffn_Wr': _L0_ffn_in['Wr'], 'L0_ffn_temperature': _L0_ffn_in['temperature'], 'L1_xattn_Wq': _L1_xattn_in['Wq'], 'L1_xattn_bq': _L1_xattn_in['bq'], 'L1_xattn_Wk': _L1_xattn_in['Wk'], 'L1_xattn_bk': _L1_xattn_in['bk'], 'L1_xattn_Wv': _L1_xattn_in['Wv'], 'L1_xattn_bv': _L1_xattn_in['bv'], 'L1_ffn_wg': _L1_ffn_in['wg'], 'L1_ffn_w1': _L1_ffn_in['w1'], 'L1_ffn_w2': _L1_ffn_in['w2']}

def reference(x, ctx_1024, mask_1x1xSxS2_if1, mask_BxSxS2_fk0, g_xattn, g_ffn, L0_xattn_Wq, L0_xattn_bq, L0_xattn_Wk, L0_xattn_bk, L0_xattn_Wv, L0_xattn_bv, L0_xattn_Wo, L0_xattn_bo, L0_ffn_Wg, L0_ffn_Wu, L0_ffn_Wd, L0_ffn_Wr, L0_ffn_temperature, L1_xattn_Wq, L1_xattn_bq, L1_xattn_Wk, L1_xattn_bk, L1_xattn_Wv, L1_xattn_bv, L1_ffn_wg, L1_ffn_w1, L1_ffn_w2):
    import jax
    import jax.numpy as jnp

    def _L0_xattn_ref(q, k, v, mask, Wq, bq, Wk, bk, Wv, bv, Wo, bo):
        import jax, jax.numpy as jnp
        import numpy as np
        D_MODEL = 256
        H = 16
        D_K = D_MODEL // H
        B, S = (2, 512)
        NEG = -1000000000.0

        def _split_heads(x):
            b, s, _ = x.shape
            return x.reshape(b, s, H, D_K).transpose(0, 2, 1, 3)
        query = _split_heads(q @ Wq.T + bq)
        key_ = _split_heads(k @ Wk.T + bk)
        value = _split_heads(v @ Wv.T + bv)
        scores = jnp.einsum('bhqd,bhkd->bhqk', query, key_) / jnp.sqrt(jnp.asarray(D_K, query.dtype))
        scores = jnp.where(mask == 0, jnp.asarray(NEG, scores.dtype), scores)
        attn = jax.nn.softmax(scores, axis=-1)
        ctx = jnp.einsum('bhqk,bhkd->bhqd', attn, value)
        ctx = ctx.transpose(0, 2, 1, 3).reshape(q.shape[0], -1, D_MODEL)
        return ctx @ Wo.T + bo

    def _L0_ffn_ref(x, Wg, Wu, Wd, Wr, temperature):
        import jax, jax.numpy as jnp
        import numpy as np
        import math
        GOLDEN_CENTER = 1.0 / math.e
        GOLDEN_LOWER = 0.5 - math.log(4.0 / 3.0)
        GOLDEN_UPPER = 0.5
        B, T, D = (4, 512, 256)
        E = 8
        I = 1024 // (E // 2)

        def _routing_weights(x, Wr, temperature):
            inh = jax.nn.sigmoid(x @ Wr / temperature)
            in_zone = (inh >= GOLDEN_LOWER) & (inh <= GOLDEN_UPPER)
            dist = jnp.abs(inh - GOLDEN_CENTER)
            w = jnp.exp(-dist / 0.1) * in_zone.astype(x.dtype)
            wsum = w.sum(axis=-1, keepdims=True)
            no_expert = wsum < 1e-08
            fb = jnp.exp(-dist / 0.3)
            _, top2 = jax.lax.top_k(fb, 2)
            fb_mask = jax.nn.one_hot(top2, E, dtype=x.dtype).sum(axis=-2)
            fb_w = fb * fb_mask
            fb_w = fb_w / jnp.clip(fb_w.sum(axis=-1, keepdims=True), 1e-08)
            w = jnp.where(no_expert, fb_w, w)
            wsum = w.sum(axis=-1, keepdims=True)
            return w / jnp.clip(wsum, 1e-08)
        weights = _routing_weights(x, Wr, temperature)
        gate = jnp.einsum('btd,edi->beti', x, Wg)
        up = jnp.einsum('btd,edi->beti', x, Wu)
        h = jax.nn.silu(gate) * up
        e_out = jnp.einsum('beti,eid->betd', h, Wd)
        out = jnp.einsum('bte,betd->btd', weights, e_out)
        return out

    def _L1_xattn_ref(primary, context_sequence, mask, Wq, bq, Wk, bk, Wv, bv):
        import jax, jax.numpy as jnp
        import numpy as np
        INPUT_DIM, ATTN_DIM, OUTPUT_DIM = (256, 256, 256)
        B, LQ, LKV = (4, 512, 512)
        q = primary @ Wq + bq
        k = context_sequence @ Wk + bk
        v = context_sequence @ Wv + bv
        score = jnp.einsum('bqd,bkd->bqk', q, k) / jnp.sqrt(jnp.float32(ATTN_DIM))
        score = score + mask * -1000000000.0
        attn = jax.nn.softmax(score, axis=-1)
        return jnp.einsum('bqk,bkd->bqd', attn, v)

    def _L1_ffn_ref(x, wg, w1, w2):
        import jax, jax.numpy as jnp
        import numpy as np
        CAPACITY_FACTOR = 1.0

        def _top1_gate(x2d, wg):
            S, _ = x2d.shape
            E = wg.shape[1]
            C = int(CAPACITY_FACTOR * S / E)
            logits = x2d @ wg
            gates = jax.nn.softmax(logits, axis=-1)
            idx = jnp.argmax(gates, axis=-1)
            mask = jax.nn.one_hot(idx, E, dtype=jnp.int32)
            loc = jnp.cumsum(mask, axis=0) - 1
            me = jnp.mean(gates, axis=0)
            ce = jnp.mean(mask.astype(gates.dtype), axis=0)
            l_aux = E * jnp.sum(me * ce)
            mask = mask * (loc < C).astype(jnp.int32)
            gate_s = jnp.sum(gates * mask, axis=-1)
            loc_s = jnp.sum(loc * mask, axis=-1)
            loc_oh = jax.nn.one_hot(loc_s, C, dtype=gates.dtype)
            combine = (gate_s[:, None] * mask.astype(gates.dtype))[:, :, None] * loc_oh[:, None, :]
            dispatch = (combine > 0).astype(gates.dtype)
            return (l_aux, combine, dispatch)
        s, b, m = x.shape
        x2d = x.reshape(-1, m)
        l_aux, combine, dispatch = _top1_gate(x2d, wg)
        combine = combine[:, None]
        dispatch = dispatch[:, None]
        xr = x2d[:, None, :]
        dispatched = jnp.einsum('szfc,szm->zfcm', dispatch, xr)
        E = w1.shape[0]
        di = dispatched.reshape(E, -1, m)
        h = jax.nn.relu(jnp.einsum('ecm,emh->ech', di, w1))
        eo = jnp.einsum('ech,ehm->ecm', h, w2)
        eo = eo[None]
        out = jnp.einsum('szfc,zfcm->sm', combine, eo)
        return out.reshape(s, b, m)
    x = x + jnp.tanh(g_xattn[0]) * _L0_xattn_ref(_layernorm(x, axis=-1), ctx_1024, ctx_1024, mask_1x1xSxS2_if1, L0_xattn_Wq, L0_xattn_bq, L0_xattn_Wk, L0_xattn_bk, L0_xattn_Wv, L0_xattn_bv, L0_xattn_Wo, L0_xattn_bo)
    x = x + jnp.tanh(g_ffn[0]) * _L0_ffn_ref(_layernorm(x, axis=-1), L0_ffn_Wg, L0_ffn_Wu, L0_ffn_Wd, L0_ffn_Wr, L0_ffn_temperature)
    x = x + jnp.tanh(g_xattn[1]) * _L1_xattn_ref(_layernorm(x, axis=-1), ctx_1024, mask_BxSxS2_fk0, L1_xattn_Wq, L1_xattn_bq, L1_xattn_Wk, L1_xattn_bk, L1_xattn_Wv, L1_xattn_bv)
    x = x + jnp.tanh(g_ffn[1]) * _L1_ffn_ref(_layernorm(x, axis=-1), L1_ffn_wg, L1_ffn_w1, L1_ffn_w2)
    return x

_drawn_inputs = setup_inputs


def setup_inputs(seed=0):
    import zlib

    import numpy as np

    out = dict(_drawn_inputs(seed))
    spreads = {'g_ffn': (-1.0, 0.6),
     'L0_xattn_bq': (0.0, 0.1),
     'L0_xattn_bk': (0.0, 0.8),
     'L0_xattn_bv': (0.0, 0.1),
     'L0_xattn_bo': (0.0, 0.1)}
    factors = {'L1_xattn_bq': 8.0,
     'L1_xattn_bk': 8.0,
     'L1_ffn_wg': 3.203,
     'L1_ffn_w1': 3.601,
     'L1_ffn_w2': 2.99}
    for name, (base, spread) in spreads.items():
        noise = np.random.default_rng([zlib.crc32(name.encode()), seed]).standard_normal(out[name].shape)
        drawn = base * np.exp(spread * noise) if base else spread * noise
        out[name] = jnp.asarray(drawn.astype(out[name].dtype))
    for name, factor in factors.items():
        out[name] = (out[name] * factor).astype(out[name].dtype)
    return out
```

```python
import math
from contextlib import ExitStack

import numpy as np

import concourse.bass as bass
from concourse import mybir

ALU = mybir.AluOpType
ACT = mybir.ActivationFunctionType
AX = mybir.AxisListType
F32 = mybir.dt.float32
F32R = mybir.dt.float32r
BF16 = mybir.dt.bfloat16
I32 = mybir.dt.int32

P = 128
B, S, D = 16, 128, 256
K2 = D // P
H, DH = 16, 16
T = B * S
GB = 4
G = B // GB
GT = GB * S
UNITS = 2 * GB
E = 8
I0 = 256
W2C = 6 * I0
F1 = 1024
CAP = T // E
ROW = D + 4
EPS = 1e-5
RSQ = 12
VS1 = 2 * GB + RSQ + (2 + RSQ) * GB + GB
DS3 = 69
GOLD = 1.0 / math.e
GOLD_LO = 0.5 - math.log(4.0 / 3.0)
Z_LO = math.log(GOLD_LO / (1.0 - GOLD_LO))
NEG = -1000000000.0
C_ID, C_TRI, C_ODD, C_IDX, C_REV, C_TOK, C_OWN = 0, 128, 256, 257, 257 + 128, 257 + 256, 257 + 260
C_N = 257 + 264


def constants():
    p = np.arange(P)
    c = np.zeros((P, C_N), np.float32)
    c[:, C_ID:C_ID + P] = np.eye(P)
    c[:, C_TRI:C_TRI + P] = p[:, None] < p[None, :]
    c[:, C_ODD] = (p // DH) % 2
    c[:, C_IDX:C_IDX + P] = np.tile(np.arange(E), P // E)
    c[:, C_REV:C_REV + P] = E - np.tile(np.arange(E), P // E)
    c[:, C_TOK:C_TOK + GB] = p[:, None] + S * np.arange(GB)
    c[:, C_OWN:C_OWN + GB] = T + p[:, None] + S * np.arange(GB)
    return c


class Signal:

    def __init__(self, sem, per):
        self.sem, self.per = sem, per

    def credit(self, eng):
        eng.sem_inc(self.sem, self.per)

    def now(self, g, n):
        return g * self.per + (self.per + n)

    def before(self, g, n):
        return g * self.per + n

    def total(self, turns):
        return (turns + 1) * self.per


class Steps(Signal):

    def __init__(self, sem, per):
        super().__init__(sem, per)
        self.last = 0

    def done(self, ins):
        ins.then_inc(self.sem, 1)
        self.last += 1
        return self.last


def block_kernel(nc, x, ctxT, maskf, gx, gf, wa0, bcols, bv0, bo0, w0, wrs, temp, wa1, bv1,
                 w1, w2, const, out, slots, stop_after=4):
    with ExitStack() as ctx:
        def sem(name):
            return ctx.enter_context(nc.semaphore(name))

        def sb(name, cols, dt=F32):
            return ctx.enter_context(nc.sbuf_tensor(name, [P, cols], dt))

        psum = ctx.enter_context(nc.psum_tensor("psum", [P, 8, 512], F32))

        x_all = sb("x_all", B * ROW).rearrange("p (t c) -> p t c", c=ROW)
        cst = sb("cst", C_N)
        ident = cst[:, C_ID:C_ID + P]
        neg_ident = sb("neg_ident", P)
        parity = sb("parity", 2)
        ones_r = sb("ones_r", P, F32R)
        ones_b = sb("ones_b", P, BF16)
        tri_b = sb("tri_b", P, BF16)
        biasc = sb("biasc", 8)
        biasr = sb("biasr", 3 * D)
        bv0r, bo0r, bv1r = (biasr[:, i * D:(i + 1) * D] for i in range(3))
        scal = sb("scal", 8)
        scratch = sb("scratch", GB)
        wr_raw = sb("wr_raw", 2 * K2 * E).rearrange("p (l k n) -> p l k n", l=2, k=K2)
        fill = sb("fill", ROW)
        bq1s = sb("bq1s", 2)
        w_exp = sb("w_exp", E * B).rearrange("p (e t) -> p e t", e=E)
        w_cur = [sb(f"w_cur{i}", B) for i in range(2)]
        tgate = sb("tgate", 4)
        arena = sb("arena", 36352, F32R)
        at = [0]

        def cut(cols):
            at[0] += cols
            assert at[0] <= 36352
            return arena[:, at[0] - cols:at[0]]

        def pair(cols):
            return cut(cols), cut(cols)

        wa = pair(4 * K2 * D)
        wa = [w.rearrange("p (m k n) -> p m k n", m=4, k=K2) for w in wa]
        xnT_all = [w.rearrange("p (k t) -> p k t", k=K2) for w in pair(K2 * T)]
        w2_both = pair(2 * W2C)
        w2s = [[w[:, i * W2C:(i + 1) * W2C] for w in w2_both] for i in range(2)]
        wr = [w.rearrange("p (l k n) -> p l k n", l=2, k=K2) for w in pair(2 * K2 * P)]
        mark = at[0]
        cT = [w.rearrange("p (k t) -> p k t", k=K2) for w in pair(K2 * GT)]
        xnT = [w.rearrange("p (k t) -> p k t", k=K2) for w in pair(K2 * GT)]
        kT = [w.rearrange("p (m t) -> p m t", m=2) for w in pair(2 * GT)]
        kM = cut(4 * GT).rearrange("p (m r t) -> p m r t", m=2, r=2)
        qT = [w.rearrange("p (m t) -> p m t", m=2) for w in pair(2 * GT)]
        qM = [w.rearrange("p (m r t) -> p m r t", m=2, r=2) for w in pair(4 * GT)]
        diag = [cut(8 * P).rearrange("p (h q) -> p h q", h=8) for _ in range(2)]
        oT = [w.rearrange("p (k t) -> p k t", k=K2) for w in pair(K2 * P)]
        at[0] = mark
        hT = [[w.rearrange("p (k t) -> p k t", k=2) for w in pair(2 * GT)] for _ in range(2)]
        at[0] = 0
        w4 = [[w.rearrange("p (a n) -> p a n", a=2) for w in pair(2 * 2048)] for _ in range(2)]
        diT = [[w.rearrange("p (k c) -> p k c", k=K2) for w in pair(K2 * CAP)] for _ in range(2)]
        h4 = [[w.rearrange("p (f c) -> p f c", f=8) for w in pair(8 * CAP)] for _ in range(2)]

        work = sb("work", 9728)
        wat = [0]

        def fcut(cols):
            wat[0] += cols
            assert wat[0] <= 9728, wat
            return work[:, wat[0] - cols:wat[0]]

        raw_both = fcut(2 * W2C)
        raw = [raw_both[:, i * W2C:(i + 1) * W2C] for i in range(2)]
        c_in = fcut(K2 * GT).rearrange("p (k t) -> p k t", k=K2)
        fmark = wat[0]
        v0 = fcut(GB * H * 32).rearrange("p (b h d) -> p b h d", b=GB, h=H)
        probs = [fcut(8 * P).rearrange("p (h q) -> p h q", h=8) for _ in range(2)]
        oT_raw = fcut(512).rearrange("p (c q) -> p c q", c=4)
        o_tok = fcut(D)
        xn = [fcut(D) for _ in range(2)]
        stats = fcut(2 * 6 * GB).rearrange("p (n s) -> p n s", s=6)
        mv = fcut(2 * 2 * GB).rearrange("p (n s) -> p n s", s=2)
        rstd, newton = fcut(2 * GB), fcut(2 * GB)
        mx = [fcut(8) for _ in range(2)]
        rden = fcut(H)

        wat[0] = fmark
        lgT = fcut(T)
        gu_s = [fcut(GT) for _ in range(2)]
        gu_h = [fcut(GT) for _ in range(2)]
        rt = [fcut(P) for _ in range(9)]
        rs = [fcut(B) for _ in range(4)]
        wat[0] = fmark
        wa1_raw = fcut(3 * K2 * D).rearrange("p (m k n) -> p m k n", m=3, k=K2)
        wat[0] = fmark + 2048
        k1 = fcut(2 * GT).rearrange("p (m t) -> p m t", m=2)
        q1 = fcut(2 * GT).rearrange("p (m t) -> p m t", m=2)
        p3mark = wat[0]
        wat[0] = fmark
        v1 = fcut(GB * D).rearrange("p (b n) -> p b n", b=GB)
        sc1 = fcut(GT).rearrange("p (b k) -> p b k", b=GB)
        p1T = fcut(GT).rearrange("p (b q) -> p b q", b=GB)
        wat[0] = 0
        mask = fcut(GT).rearrange("p (b k) -> p b k", b=GB)
        pay = fcut(GB * ROW).rearrange("p (b c) -> p b c", b=GB)
        lg1T = fcut(GT)
        r3 = [fcut(GB * E).rearrange("p (b e) -> p b e", b=GB) for _ in range(6)]
        r3s = [fcut(GB) for _ in range(10)]
        assert wat[0] <= 2 * W2C
        wat[0] = p3mark
        xn3 = [fcut(D) for _ in range(2)]
        st3 = fcut(2 * 6 * GB).rearrange("p (n s) -> p n s", s=6)
        mv3 = fcut(2 * 2 * GB).rearrange("p (n s) -> p n s", s=2)
        rstd3, newton3 = fcut(2 * GB), fcut(2 * GB)
        nmax, sum1, gsc = fcut(GB), fcut(GB), fcut(GB)
        tok_idx = sb("tok_idx", GB, I32)
        ones_before = sb("ones_before", E)
        oh_b = sb("oh_b", 2 * GB * E, BF16).rearrange("p (a b e) -> p a b e", a=2, b=GB)
        tokn = sb("tokn", 2 * GB)
        wat[0] = 0
        raw4 = [fcut(4096).rearrange("p (a n) -> p a n", a=2) for _ in range(2)]
        xd = [fcut(D) for _ in range(2)]
        yo = [[fcut(D) for j in range(2)] for i in range(2)]
        out_idx = [sb(f"out_idx{i}", 2, I32) for i in range(2)]
        xs = x_all

        ps = psum

        s_passed = sem("wait_passed")

        def reciprocal_root(dve, step, var, r, t):
            step(dve.tensor_scalar(t, var, EPS, None, ALU.add))
            step(dve.tensor_scalar(r.bitcast(I32), t.bitcast(I32), 1, None, ALU.logical_shift_right))
            step(dve.tensor_scalar(r.bitcast(I32), r.bitcast(I32), -1.0, float(0x5f3759df), ALU.mult, ALU.add))
            for _ in range(3):
                step(dve.tensor_tensor(u := scratch[:, 0:r.shape[1]], r, r, ALU.mult))
                step(dve.scalar_tensor_tensor(u, u, -0.5, t, ALU.mult, ALU.mult))
                step(dve.scalar_tensor_tensor(r, u, 1.5, r, ALU.add, ALU.mult))

        def alone(eng):
            eng.sem_inc(s_passed, 1)

        s_const, s_small = sem("const_loaded"), sem("small_loaded")
        s_waraw = sem("attn_weights_loaded")
        s_x, s_c = sem("x_loaded"), sem("ctx_loaded")
        s_setup = Steps(sem("vector_setup_step"), 0)
        s_wa_hi, s_wa_lo = sem("attn_weights_high"), sem("attn_weights_low")
        s_bo = sem("bias_gated")
        s_tanh, s_fill = sem("tanh_ready"), sem("fill_ready")
        sg = {}

        def signal(name, per):
            sg[name] = Signal(sem(name), per)
            return sg[name]

        c_hi, c_lo = signal("ctx_high", 1), signal("ctx_low", 1)
        ln0 = signal("xn_ready", GB)
        xt_tr = signal("xn_transposed", GB)
        xt_hi, xt_lo = signal("xnT_high", 2), signal("xnT_low", 2)
        pj_k, pj_v, pj_q = signal("k_projected", 2), signal("v_projected", 2), signal("q_projected", 2)
        k_hi, k_lo, k_m = signal("k_high", 2), signal("k_low", 2), signal("k_masked", 2)
        v_ok = signal("v_ready", 2 * 2)
        q_hi, q_lo, q_m = signal("q_high", 2), signal("q_low", 2), signal("q_masked", 8)
        sc_q = signal("scores_for_max", UNITS)
        mx_ok, dg = signal("max_ready", UNITS), signal("diag_ready", UNITS)
        sc_k = signal("scores_shifted", UNITS)
        ex = signal("exp_ready", UNITS)
        pv = signal("pv_done", UNITS)
        o_raw = signal("oT_copied", GB)
        o_tr = signal("o_transposed", GB)
        o_n = signal("o_normalised", GB)
        o_nt = signal("o_back", GB)
        oT_hi, oT_lo = signal("oT_high", GB), signal("oT_low", GB)
        wo = signal("wo_done", GB)
        x1 = signal("x_after_attn", GB)
        ln1 = signal("xn1_ready", GB)
        x1t = signal("xn1_transposed", GB)
        x1_hi, x1_lo = signal("xn1T_high", GB), signal("xn1T_low", GB)
        xb_ok = signal("x_with_bias", GB)
        vs = Steps(sem("vector_step"), VS1)


        NC2, NH2 = 2 * G, 4 * G
        lg, lgc, lgt = sem("logits_ready"), sem("logits_copied"), sem("logits_transposed")
        s_wexp = sem("routing_weights_ready")
        re_step = Steps(sem("routing_step"), 0)
        s_inh, s_fb = sem("sigmoid_exp_ready"), sem("zone_exp_ready")
        s_raw2 = [sem(f"expert_weights_loaded{i}") for i in range(2)]
        w2q_hi, w2q_lo = signal("first_experts_high", 1), signal("first_experts_low", 1)
        w2_hi, w2_lo = signal("expert_high", 2), signal("expert_low", 2)
        gt, up = signal("gate_ready", NH2), signal("up_ready", NH2)
        sl, hm = signal("silu_ready", NH2), signal("h_ready", NH2)
        hh, hl = signal("h_high", NH2), signal("h_low", NH2)
        dn, ac = signal("down_ready", NC2), signal("x_accumulated", NC2)
        wcur = signal("expert_weight_picked", 2)
        as2 = Steps(sem("vector_step2"), 3 * NC2)

        s_c3, s_m3, s_wa1, s_base = sem("ctx3_loaded"), sem("mask_loaded"), sem("wa1_loaded"), sem("base_out_written")
        s_wa1_hi, s_wa1_lo = sem("wa1_high"), sem("wa1_low")
        s_fillw, s_disp = sem("slots_filled"), sem("rows_dispatched")
        c3_hi, c3_lo = signal("ctx3_high", 1), signal("ctx3_low", 1)
        n3 = signal("xn3_ready", 2 * GB)
        n3t = signal("xn3_transposed", 2 * GB)
        n3_hi, n3_lo = signal("xn3T_high", 4), signal("xn3T_low", 4)
        pk3, pv3, pq3 = signal("k1_projected", 2), signal("v1_projected", 2), signal("q1_projected", 2)
        k1_ok, v1_ok, q1_ok = signal("k1_ready", 2), signal("v1_ready", 2), signal("q1_ready", 2)
        s1 = signal("scores1_ready", 1)
        s1m, m1 = signal("scores1_masked", 1), signal("max1_ready", 1)
        e1 = signal("probs1_ready", GB)
        t1 = signal("probs1_transposed", 1)
        p1_ok = signal("probs1T_ready", 1)
        a1 = signal("attn1_ready", 2)
        x3 = signal("x3_ready", GB)
        l1, l1c, l1t = signal("logits1_ready", 1), signal("logits1_copied", 1), signal("logits1_transposed", 1)
        ex1, r1e = signal("gate_shift_ready", 1), signal("gate_exp_ready", 1)
        oh1, loc1 = signal("onehot_ready", 1), signal("places_ready", 1)
        dest = signal("rows_ready", 1)
        ds3 = Steps(sem("vector_step3"), DS3)

        s_xs = sem("slots_loaded")
        s_raw4 = [sem(f"expert1_weights_loaded{i}") for i in range(2)]
        w4_hi, w4_l1, w4_l2 = signal("expert1_high", 4), signal("expert1_w1_low", 2), signal("expert1_w2_low", 2)
        xd_ok = signal("slots_normalised", 4)
        xd_t = signal("slots_transposed", 2)
        di_hi, di_lo = signal("slotsT_high", 2), signal("slotsT_low", 2)
        h1, h1_hi, h1_lo = signal("hidden_ready", 16), signal("hidden_high", 16), signal("hidden_low", 16)
        d4 = signal("expert1_out_ready", 2)
        y4 = signal("rows_out_ready", 2)
        idx4 = signal("row_numbers_ready", 2)
        rows_left, out_left = signal("rows_left", 1), signal("rows_out_left", 2)
        s_sc = [sem(f"rows_scattered{i}") for i in range(2)]
        ds4 = Steps(sem("vector_step4"), 2)

        block = ctx.enter_context(nc.Block())

        def two_seqs(t, c):
            return t[:, :, 2 * c * P:(2 * c + 2) * P].rearrange("p k (b t) -> p b k t", b=2)

        def slot_cols(t):
            return t.rearrange("p k (b t) -> p b k t", b=2)

        def in_bank(i):
            return ps[:, i, :].rearrange("p (b k t) -> p b k t", b=2, k=K2)

        @block.sync
        def _(sp):
            sp.dma_start(cst[:, :], const).then_inc(s_const, 16)
            sp.dma_start(x_all[:, 0:GB, 0:D], x[0:GB].rearrange("b s d -> s b d")).then_inc(s_x, 16)
            sp.dma_start(probs_raw := work[:, fmark:fmark + 4 * K2 * D].rearrange("p (m k n) -> p m k n", m=4, k=K2),
                         wa0.rearrange("m (k p) n -> p m k n", p=P)).then_inc(s_waraw, 16)
            sp.dma_start(c_in, ctxT[:, 0:GT].rearrange("(k p) t -> p k t", p=P)).then_inc(s_c, 16)
            sp.dma_start(biasc[:, :], bcols).then_inc(s_small, 16)
            for i, b in enumerate((bv0, bo0, bv1)):
                sp.dma_start(biasr[:, i * D:(i + 1) * D], b.rearrange("(a d) -> a d", a=1).to_broadcast([P, D])
                             ).then_inc(s_small, 16)
            sp.dma_start(wr_raw, wrs.rearrange("l (k p) e -> p l k e", p=P)).then_inc(s_small, 16)
            for a, i, n in ((gx, 0, 2), (gf, 2, 2), (temp, 4, 1)):
                sp.dma_start(scal[:, i:i + n], a.rearrange("(a d) -> a d", a=1).to_broadcast([P, n])
                             ).then_inc(s_small, 16)
            for i in range(2):
                sp.dma_start(raw[i], w0[i:i + 1].rearrange("e p n -> p (e n)")).then_inc(s_raw2[i], 16)
            with sp.Fori(0, G - 1) as g:
                sp.wait_ge(s_x, g * 16 + 16)
                alone(sp)
                sp.wait_ge(c_hi.sem, c_hi.now(g, 1))
                alone(sp)
                sp.wait_ge(c_lo.sem, c_lo.now(g, 1))
                alone(sp)
                sp.dma_start(x_all[:, bass.ds(g * GB + GB, GB), 0:D],
                             x[bass.ds(g * GB + GB, GB)].rearrange("b s d -> s b d")).then_inc(s_x, 16)
                sp.dma_start(c_in, ctxT[:, bass.ds(g * GT + GT, GT)].rearrange("(k p) t -> p k t", p=P)
                             ).then_inc(s_c, 16)
            sp.sem_inc(s_base, 16)
            with sp.Fori(1, E // 2) as g:
                for i in range(2):
                    sp.wait_ge(w2_lo.sem, w2_lo.before(g, i + 1))
                    alone(sp)
                    sp.dma_start(raw[i], w0[bass.ds(2 * g + i, 1)].rearrange("e p n -> p (e n)")).then_inc(s_raw2[i], 16)
            sp.wait_ge(s_wexp, 1)
            sp.dma_start(wa1_raw, wa1.rearrange("m (k p) n -> p m k n", p=P)).then_inc(s_wa1, 16)
            sp.wait_ge(w2_lo.sem, w2_lo.total(E // 2))
            with sp.Fori(0, G) as g:
                sp.wait_ge(c3_lo.sem, c3_lo.before(g, 1))
                alone(sp)
                sp.wait_ge(c3_hi.sem, c3_hi.before(g, 1))
                alone(sp)
                sp.dma_start(c_in, ctxT[:, bass.ds(g * GT, GT)].rearrange("(k p) t -> p k t", p=P)).then_inc(s_c3, 16)
                sp.wait_ge(s1m.sem, s1m.before(g, 1))
                alone(sp)
                sp.dma_start(mask, maskf[bass.ds(g * GB, GB)].rearrange("b q k -> q b k")).then_inc(s_m3, 16)
                sp.wait_ge(x3.sem, x3.now(g, GB))
                alone(sp)
                sp.dma_start(out[bass.ds(g * GB, GB)].rearrange("b s d -> s b d"), pay[:, :, 0:D]).then_inc(s_base, 16)
            sp.wait_ge(s_disp, 16 * B)
            sp.wait_ge(s_base, 16 * (1 + G))

            def load4(i, e):
                sp.dma_start(raw4[i][:, 0, :].rearrange("p (k n) -> p k n", k=K2),
                             w1[e].rearrange("e (k p) n -> p (e k) n", p=P)).then_inc(s_raw4[i], 16)
                sp.dma_start(raw4[i][:, 1, :].rearrange("p (f n) -> p f n", f=8),
                             w2[e].rearrange("e (f p) n -> p (e f) n", p=P)).then_inc(s_raw4[i], 16)
            load4(0, slice(0, 1))
            sp.dma_start(xs[:, :, :], slots[0:T, :].rearrange("(t p) c -> p t c", p=P)).then_inc(s_xs, 16)
            load4(1, slice(1, 2))
            with sp.Fori(0, E // 2 - 1) as g:
                for i in range(2):
                    sp.wait_ge(w4_hi.sem, w4_hi.now(g, 2 * i + 2))
                    alone(sp)
                    sp.wait_ge(w4_l1.sem, w4_l1.now(g, i + 1))
                    alone(sp)
                    sp.wait_ge(w4_l2.sem, w4_l2.now(g, i + 1))
                    alone(sp)
                    load4(i, bass.ds(2 * g + 2 + i, 1))

        @block.scalar
        def _(act):
            wraw = work[:, fmark:fmark + 4 * K2 * D].rearrange("p (m k n) -> p m k n", m=4, k=K2)
            for s in (c_hi, xt_hi, k_hi, q_hi, ex, o_raw, oT_hi, x1_hi):
                s.credit(act)
            act.wait_ge(s_waraw, 16)
            act.activation(wa[0][:, :, :, :], wraw, ACT.Copy).then_inc(s_wa_hi, 1)
            act.wait_ge(s_small, 16 * 8)
            act.activation(tgate[:, :], scal[:, 0:4], ACT.Tanh).then_inc(s_tanh, 1)
            act.wait_ge(s_wa_lo, 1)
            with act.Fori(0, G) as g:
                act.wait_ge(s_c, g * 16 + 16)
                act.wait_ge(pj_k.sem, pj_k.before(g, 2))
                act.wait_ge(pj_v.sem, pj_v.before(g, 2))
                act.activation(cT[0], c_in, ACT.Copy).then_inc(c_hi.sem, 1)
                for m in range(2):
                    act.wait_ge(pj_k.sem, pj_k.now(g, m + 1))
                    act.wait_ge(sc_k.sem, sc_k.before(g, UNITS))
                    act.wait_ge(k_m.sem, k_m.before(g, 2))
                    act.activation(kT[0][:, m, :], ps[:, m, :], ACT.Identity, bias=biasc[:, 2 + m:3 + m]
                                   ).then_inc(k_hi.sem, 1)
                for c in range(2):
                    act.wait_ge(xt_tr.sem, xt_tr.now(g, 2 * c + 2))
                    act.activation(two_seqs(xnT[0], c), in_bank(6 + c), ACT.Copy).then_inc(xt_hi.sem, 1)
                for m in range(2):
                    act.wait_ge(pj_q.sem, pj_q.now(g, m + 1))
                    act.activation(qT[0][:, m, :], ps[:, 4 + m, :], ACT.Identity, bias=biasc[:, m:m + 1]
                                   ).then_inc(q_hi.sem, 1)

                def tail_a(b):
                    act.wait_ge(pv.sem, pv.now(g, 2 * b + 2))
                    act.wait_ge(o_tr.sem, o_tr.now(g, b) if b else o_tr.before(g, GB))
                    act.activation(oT_raw, ps[:, 6, :].rearrange("p (c q) -> p c q", c=4), ACT.Copy).then_inc(o_raw.sem, 1)

                def tail_b(b):
                    act.wait_ge(o_nt.sem, o_nt.now(g, b + 1))
                    act.wait_ge(wo.sem, wo.now(g, b) if b else wo.before(g, GB))
                    act.activation(oT[0], ps[:, 7, 0:256].rearrange("p (k t) -> p k t", k=K2), ACT.Copy
                                   ).then_inc(oT_hi.sem, 1)

                def tail_c(b):
                    act.wait_ge(x1t.sem, x1t.now(g, b + 1))
                    act.activation(xnT_all[0][:, :, bass.ds(g * GT + b * P, P)],
                                   ps[:, 7, 0:256].rearrange("p (k t) -> p k t", k=K2), ACT.Copy).then_inc(x1_hi.sem, 1)

                for u in range(UNITS):
                    if u >= 3 and u % 2:
                        tail_b(u // 2 - 1)
                    if u >= 4 and u % 2 == 0:
                        tail_c(u // 2 - 2)
                    act.wait_ge(sc_k.sem, sc_k.now(g, u + 1))
                    act.wait_ge(pv.sem, pv.now(g, u - 1) if u >= 2 else pv.before(g, UNITS - 1 + u))
                    act.activation(probs[u % 2], ps[:, 2 + 2 * (u % 2):4 + 2 * (u % 2), :].rearrange("p j (h q) -> p (j h) q", q=P),
                                   ACT.Exp, scale=DH ** -0.5).then_inc(ex.sem, 1)
                    if u >= 2 and u % 2 == 0:
                        tail_a(u // 2 - 1)
                tail_c(GB - 2)
                tail_a(GB - 1)
                tail_b(GB - 1)
                tail_c(GB - 1)

            act.wait_ge(pv.sem, pv.total(G))
            for n in range(G):
                act.wait_ge(lg, n + 1)
                act.activation(lgT[0:E, n * GT:(n + 1) * GT], ps[0:E, n, :], ACT.Copy).then_inc(lgc, 1)
            act.wait_ge(s_inh, 1)
            act.activation(rt[2], rt[1], ACT.Exp, scale=-1.0).then_inc(s_inh, 1)
            act.wait_ge(s_fb, 1)
            act.activation(rt[4], rt[3], ACT.Exp, scale=-1.0 / 0.1).then_inc(s_fb, 1)
            act.wait_ge(s_fb, 2)
            act.activation(rt[5], rt[3], ACT.Exp, scale=-1.0 / 0.3).then_inc(s_fb, 1)

            for s in (sl, hh):
                s.credit(act)
            with act.Fori(0, E // 2) as g:
                def high(i):
                    act.wait_ge(hm.sem, hm.now(g, i + 1))
                    c = i // 2
                    act.wait_ge(dn.sem, dn.now(g, c - 1) if c >= 2 else dn.before(g, NC2 - 1 + c))
                    act.activation(hT[c % 2][0][:, i % 2, :], gu_h[i % 2], ACT.Copy).then_inc(hh.sem, 1)
                for i in range(NH2):
                    act.wait_ge(gt.sem, gt.now(g, i + 1))
                    act.wait_ge(hm.sem, hm.now(g, i - 1) if i >= 2 else hm.before(g, NH2 - 1 + i))
                    act.activation(gu_s[i % 2], ps[:, i % 2, :], ACT.Silu).then_inc(sl.sem, 1)
                    if i:
                        high(i - 1)
                high(NH2 - 1)

            act.wait_ge(dn.sem, dn.total(E // 2))
            for s in (c3_hi, n3_hi, k1_ok, q1_ok, e1, p1_ok, l1c, r1e):
                s.credit(act)
            with act.Fori(0, G) as g:
                def high3(c):
                    act.wait_ge(n3t.sem, n3t.now(g, 2 * c + 2))
                    act.activation(two_seqs(xnT[0], c % 2), in_bank(6 + c % 2), ACT.Copy).then_inc(n3_hi.sem, 1)

                act.wait_ge(s_c3, g * 16 + 16)
                act.wait_ge(pv3.sem, pv3.before(g, 2))
                act.activation(cT[0], c_in, ACT.Copy).then_inc(c3_hi.sem, 1)
                for m in range(2):
                    act.wait_ge(pk3.sem, pk3.now(g, m + 1))
                    act.wait_ge(s1.sem, s1.before(g, 1))
                    act.activation(k1[:, m, :], ps[:, m, :], ACT.Identity, bias=biasc[:, 6 + m:7 + m]).then_inc(k1_ok.sem, 1)
                act.wait_ge(l1.sem, l1.before(g, 1))
                for c in range(2):
                    high3(c)
                for m in range(2):
                    act.wait_ge(pq3.sem, pq3.now(g, m + 1))
                    act.activation(q1[:, m, :], ps[:, 4 + m, :], ACT.Identity, bias=bq1s[:, m:m + 1], scale=1.0 / 16
                                   ).then_inc(q1_ok.sem, 1)
                act.wait_ge(m1.sem, m1.now(g, 1))
                act.wait_ge(x3.sem, x3.before(g, GB))
                for b in range(GB):
                    act.activation(sc1[:, b, :], sc1[:, b, :], ACT.Exp, bias=nmax[:, b:b + 1], accum_out=sum1[:, b:b + 1]
                                   ).then_inc(e1.sem, 1)
                act.wait_ge(t1.sem, t1.now(g, 1))
                act.activation(p1T, ps[:, 7, :].rearrange("p (b q) -> p b q", b=GB), ACT.Copy).then_inc(p1_ok.sem, 1)
                for c in range(2, 4):
                    high3(c)
                act.wait_ge(l1.sem, l1.now(g, 1))
                act.activation(lg1T[0:E, :], ps[0:E, 2, :], ACT.Copy).then_inc(l1c.sem, 1)
                act.wait_ge(ex1.sem, ex1.now(g, 1))
                act.activation(r3[5], r3[4], ACT.Exp).then_inc(r1e.sem, 1)

            for s in (w4_hi, di_hi, h1_hi):
                s.credit(act)

            def split(g, i, a):
                act.wait_ge(s_raw4[i], 32 * g + 32)
                act.wait_ge(d4.sem, d4.before(g, i + 1))
                act.activation(w4[i][0][:, a, :], raw4[i][:, a, :], ACT.Copy).then_inc(w4_hi.sem, 1)

            def slots_high(g, i):
                act.wait_ge(xd_t.sem, xd_t.now(g, i + 1))
                act.wait_ge(h1.sem, h1.before(g, 8 * i + 8))
                act.activation(slot_cols(diT[i][0]), in_bank(6 + i), ACT.Copy).then_inc(di_hi.sem, 1)

            def hidden(g, i, f):
                if f == 0:
                    act.wait_ge(d4.sem, d4.before(g, i + 1))
                act.wait_ge(h1.sem, h1.now(g, 8 * i + f + 1))
                act.activation(h4[i][0][:, f, :], ps[:, f % 4, 0:CAP], ACT.Relu).then_inc(h1_hi.sem, 1)

            def turn(g, last):
                for i in range(2):
                    nxt = (g, 1) if i == 0 else (g + 1, 0)
                    more = i == 0 or not last
                    for f in range(8):
                        hidden(g, i, f)
                        if more and f in (1, 4):
                            split(*nxt, f // 3)
                    if more:
                        slots_high(*nxt)
            act.wait_ge(a1.sem, a1.total(G))
            act.wait_ge(l1.sem, l1.total(G))
            for a in range(2):
                split(0, 0, a)
            slots_high(0, 0)
            with act.Fori(0, E // 2 - 1) as g:
                turn(g, False)
            turn(E // 2 - 1, True)

        @block.vector
        def _(dve):
            su = s_setup
            for s in (ln0, xt_lo, k_lo, v_ok, q_lo, q_m, mx_ok, o_n, oT_lo, x1, ln1, x1_lo, vs):
                s.credit(dve)
            wraw = work[:, fmark:fmark + 4 * K2 * D].rearrange("p (m k n) -> p m k n", m=4, k=K2)
            dve.wait_ge(s_const, 16)
            su.done(dve.tensor_scalar(neg_ident[:, :], ident, -1.0, None, ALU.mult))
            su.done(dve.tensor_copy(parity[:, 1:2], cst[:, C_ODD:C_ODD + 1]))
            su.done(dve.tensor_scalar(parity[:, 0:1], cst[:, C_ODD:C_ODD + 1], -1.0, 1.0, ALU.mult, ALU.add))
            su.done(dve.memset(ones_b[:, :], 1.0))
            su.done(dve.tensor_scalar(ones_r[:, :], ident, 0.0, 1.0, ALU.mult, ALU.add))
            su.done(dve.tensor_copy(tri_b[:, :], cst[:, C_TRI:C_TRI + P]))
            dve.wait_ge(s_wa_hi, 1)
            dve.tensor_tensor(wa[1][:, :, :, :], wraw, wa[0][:, :, :, :], ALU.subtract).then_inc(s_wa_lo, 1)
            dve.wait_ge(s_wa_lo, 1)
            su.done(dve.memset(v0, 0.0))
            dve.wait_ge(su.sem, su.last)
            su.done(dve.memset(v0[:, :, :, DH:DH + 1], 1.0))
            dve.wait_ge(s_tanh, 1)
            dve.wait_ge(s_small, 16 * 8)
            for i in range(2):
                su.done(dve.memset(wr[i].bitcast(F32), 0.0))
            su.done(dve.memset(fill[:, 0:ROW - 1], 0.0))
            dve.memset(fill[:, ROW - 1:ROW], float(2 * T)).then_inc(s_fill, 1)
            dve.wait_ge(su.sem, su.last)
            su.done(dve.tensor_copy(wr[0][:, :, :, 0:E], wr_raw))
            su.done(dve.memset(ones_before[:, :], 0.0))
            su.done(dve.tensor_copy(tokn[:, :], cst[:, C_TOK:C_TOK + 2 * GB]))
            su.done(dve.tensor_scalar(bq1s[:, :], biasc[:, 4:6], 1.0 / 16, None, ALU.mult))
            su.done(dve.reciprocal(scal[:, 5:6], scal[:, 4:5]))
            dve.wait_ge(su.sem, su.last)
            su.done(dve.tensor_tensor(wr[1][:, :, :, 0:E], wr_raw, wr[0][:, :, :, 0:E], ALU.subtract))
            dve.tensor_scalar(bo0r, bo0r, tgate[:, 0:1], None, ALU.mult).then_inc(s_bo, 1)
            dve.wait_ge(su.sem, su.last)
            with dve.Fori(0, G) as g:
                vs.last = 0

                def own(n=None):
                    dve.wait_ge(vs.sem, vs.now(g, vs.last if n is None else n))

                def x_of(b):
                    return x_all[:, bass.ds(g * GB + b, 1), 0:D].rearrange("p a d -> p (a d)")

                def step(ins):
                    vs.done(ins)
                    own()

                def statistics(n, b):
                    alone(dve)
                    step(dve.bn_stats(stats[:, n, :], x_of(b)))
                    alone(dve)
                    step(dve.bn_aggr(mv[:, n, :], stats[:, n, :]))

                def normalise(n, b, dst, sig):
                    dve.tensor_scalar(dst, x_of(b), mv[:, n, 0:1], rstd[:, n:n + 1], ALU.subtract, ALU.mult
                                      ).then_inc(sig.sem, 1)

                dve.wait_ge(s_x, g * 16 + 16)
                dve.wait_ge(ln1.sem, ln1.before(g, GB))
                for b in range(GB):
                    statistics(b, b)
                reciprocal_root(dve, step, mv[:, 0:GB, 1:2].rearrange("p n o -> p (n o)"), rstd[:, 0:GB], newton[:, 0:GB])
                for b in range(GB):
                    if b >= 2:
                        dve.wait_ge(xt_tr.sem, xt_tr.now(g, b - 1))
                    else:
                        dve.wait_ge(x1t.sem, x1t.before(g, GB - 1 + b))
                    normalise(b, b, xn[b % 2], ln0)
                for c in range(2):
                    dve.wait_ge(xt_hi.sem, xt_hi.now(g, c + 1))
                    dve.tensor_tensor(two_seqs(xnT[1], c), in_bank(6 + c), two_seqs(xnT[0], c), ALU.subtract
                                      ).then_inc(xt_lo.sem, 1)
                for m in range(2):
                    dve.wait_ge(k_hi.sem, k_hi.now(g, m + 1))
                    dve.scalar_tensor_tensor(kT[1][:, m, :], ps[:, m, :], biasc[:, 2 + m:3 + m], kT[0][:, m, :],
                                             ALU.add, ALU.subtract).then_inc(k_lo.sem, 1)
                for c in range(2):
                    dve.wait_ge(pj_v.sem, pj_v.now(g, c + 1))
                    dve.wait_ge(pv.sem, pv.before(g, UNITS))
                    for i in range(2):
                        dve.tensor_tensor(v0[:, 2 * c + i, :, 0:DH],
                                          ps[:, 2 + c, i * D:(i + 1) * D].rearrange("p (h d) -> p h d", d=DH),
                                          bv0r.rearrange("p (h d) -> p h d", d=DH), ALU.add).then_inc(v_ok.sem, 1)
                for m in range(2):
                    dve.wait_ge(q_hi.sem, q_hi.now(g, m + 1))
                    dve.scalar_tensor_tensor(qT[1][:, m, :], ps[:, 4 + m, :], biasc[:, m:m + 1], qT[0][:, m, :],
                                             ALU.add, ALU.subtract).then_inc(q_lo.sem, 1)
                    dve.wait_ge(sc_k.sem, sc_k.before(g, UNITS))
                    dve.wait_ge(q_lo.sem, q_lo.now(g, m + 1))
                    for i in range(2):
                        for r in range(2):
                            dve.tensor_scalar(qM[i][:, m, r, :], qT[i][:, m, :], parity[:, r:r + 1], None, ALU.mult
                                              ).then_inc(q_m.sem, 1)

                def tail_a(b):
                    o_ps = ps[:, 7, :].rearrange("p (h d) -> p h d", d=32)
                    dve.wait_ge(o_tr.sem, o_tr.now(g, b + 1))
                    vs.done(dve.reciprocal(rden[:, :].rearrange("p (h o) -> p h o", o=1), o_ps[:, :, DH:DH + 1]))
                    own()
                    dve.tensor_tensor(o_tok.rearrange("p (h d) -> p h d", d=DH), o_ps[:, :, 0:DH],
                                      rden[:, :].rearrange("p (h o) -> p h o", o=1).to_broadcast([P, H, DH]), ALU.mult
                                      ).then_inc(o_n.sem, 1)

                def tail_b(b):
                    dve.wait_ge(oT_hi.sem, oT_hi.now(g, b + 1))
                    dve.tensor_tensor(oT[1], ps[:, 7, 0:256].rearrange("p (k t) -> p k t", k=K2), oT[0], ALU.subtract
                                      ).then_inc(oT_lo.sem, 1)

                def tail_c(b):
                    dve.wait_ge(wo.sem, wo.now(g, b + 1))
                    dve.wait_ge(xb_ok.sem, xb_ok.now(g, b + 1))
                    dve.scalar_tensor_tensor(x_of(b), ps[:, 7, 256:512], tgate[:, 0:1], x_of(b), ALU.mult, ALU.add
                                             ).then_inc(x1.sem, 1)
                    dve.wait_ge(x1.sem, x1.now(g, b + 1))
                    statistics(GB + b, b)
                    reciprocal_root(dve, step, mv[:, GB + b, 1:2], rstd[:, GB + b:GB + b + 1], newton[:, GB + b:GB + b + 1])
                    if b >= 2:
                        dve.wait_ge(x1t.sem, x1t.now(g, b - 1))
                    else:
                        dve.wait_ge(xt_tr.sem, xt_tr.now(g, 3 + b))
                    normalise(GB + b, b, xn[b % 2], ln1)

                def tail_d(b):
                    dve.wait_ge(x1_hi.sem, x1_hi.now(g, b + 1))
                    dve.tensor_tensor(xnT_all[1][:, :, bass.ds(g * GT + b * P, P)],
                                      ps[:, 7, 0:256].rearrange("p (k t) -> p k t", k=K2),
                                      xnT_all[0][:, :, bass.ds(g * GT + b * P, P)], ALU.subtract).then_inc(x1_lo.sem, 1)

                for u in range(UNITS):
                    dve.wait_ge(sc_q.sem, sc_q.now(g, u + 1))
                    dve.wait_ge(dg.sem, dg.now(g, u - 1) if u >= 2 else dg.before(g, UNITS - 1 + u))
                    dve.tensor_reduce(mx[u % 2], ps[:, 0:2, :].rearrange("p j (h k) -> p (j h) k", k=P), AX.X, ALU.max
                                      ).then_inc(mx_ok.sem, 1)
                    if u >= 3 and u % 2:
                        tail_a(u // 2 - 1)
                        tail_b(u // 2 - 1)
                    if u >= 4 and u % 2 == 0:
                        tail_c(u // 2 - 2)
                        tail_d(u // 2 - 2)
                tail_c(GB - 2)
                tail_d(GB - 2)
                tail_a(GB - 1)
                tail_b(GB - 1)
                tail_c(GB - 1)
                tail_d(GB - 1)
                assert vs.last == vs.per, vs.last

            r = [t.rearrange("p (t e) -> p t e", e=E) for t in rt]
            rev = cst[:, C_REV:C_REV + P].rearrange("p (t e) -> p t e", e=E)

            def over_e(col):
                return col.rearrange("p (t o) -> p t o", o=1).to_broadcast([P, B, E])

            def seq(ins):
                dve.wait_ge(re_step.sem, re_step.done(ins))

            dve.wait_ge(lgt, 1)
            dve.tensor_scalar(rt[1], ps[:, 4, 0:P], scal[:, 5:6], -80.0, ALU.mult, ALU.max).then_inc(s_inh, 1)
            dve.wait_ge(s_inh, 2)
            seq(dve.tensor_scalar(rt[2], rt[2], 1.0, None, ALU.add))
            seq(dve.reciprocal(rt[2], rt[2]))
            seq(dve.tensor_scalar(rt[2], rt[2], -GOLD, None, ALU.add))
            dve.scalar_tensor_tensor(rt[3], rt[2], -1.0, rt[2], ALU.mult, ALU.max).then_inc(s_fb, 1)
            seq(dve.tensor_scalar(rt[6], rt[1], Z_LO, None, ALU.is_ge))
            seq(dve.scalar_tensor_tensor(rt[6], rt[1], 0.0, rt[6], ALU.is_le, ALU.mult))
            dve.wait_ge(s_fb, 3)
            seq(dve.tensor_tensor(rt[4], rt[4], rt[6], ALU.mult))
            seq(dve.tensor_reduce(rs[0], r[4], AX.X, ALU.add))
            seq(dve.tensor_scalar(rs[1], rs[0], 1e-8, None, ALU.is_lt))

            def first_of_max(src, dst):
                seq(dve.tensor_reduce(rs[2], src, AX.X, ALU.max))
                seq(dve.tensor_tensor(dst, src, over_e(rs[2]), ALU.is_equal))
                seq(dve.tensor_tensor(dst, dst, rev, ALU.mult))
                seq(dve.tensor_reduce(rs[3], dst, AX.X, ALU.max))
                seq(dve.tensor_tensor(dst, dst, over_e(rs[3]), ALU.is_equal))

            first_of_max(r[5], r[8])
            seq(dve.scalar_tensor_tensor(rt[1], rt[8], -4.0, rt[5], ALU.mult, ALU.add))
            first_of_max(r[1], r[7])
            seq(dve.tensor_tensor(rt[7], rt[7], rt[8], ALU.add))
            seq(dve.tensor_tensor(rt[7], rt[7], rt[5], ALU.mult))

            def divide_by_sum(t, i):
                seq(dve.tensor_reduce(rs[2], r[i], AX.X, ALU.add))
                seq(dve.tensor_scalar(rs[2], rs[2], 1e-8, None, ALU.max))
                seq(dve.reciprocal(rs[2], rs[2]))
                seq(dve.tensor_tensor(r[i], r[i], over_e(rs[2]), ALU.mult))

            divide_by_sum(rt[7], 7)
            seq(dve.tensor_tensor(r[7], r[7], over_e(rs[1]), ALU.mult))
            seq(dve.tensor_tensor(rt[4], rt[4], rt[7], ALU.add))
            divide_by_sum(rt[4], 4)
            dve.tensor_scalar(w_exp.rearrange("p e t -> p t e"), r[4], tgate[:, 2:3], None, ALU.mult).then_inc(s_wexp, 1)
            dve.wait_ge(s_wexp, 1)

            for s in (hm, hl, ac, wcur, as2):
                s.credit(dve)
            with dve.Fori(0, E // 2) as g:
                as2.last = 0

                def multiply(i):
                    dve.wait_ge(sl.sem, sl.now(g, i + 1))
                    dve.wait_ge(up.sem, up.now(g, i + 1))
                    dve.wait_ge(hl.sem, hl.now(g, i - 1) if i >= 2 else hl.before(g, NH2 - 1 + i))
                    dve.tensor_tensor(gu_h[i % 2], gu_s[i % 2], ps[:, 2 + i % 2, :], ALU.mult).then_inc(hm.sem, 1)

                def low(i):
                    dve.wait_ge(hh.sem, hh.now(g, i + 1))
                    dve.tensor_tensor(hT[i // 2 % 2][1][:, i % 2, :], gu_h[i % 2], hT[i // 2 % 2][0][:, i % 2, :],
                                      ALU.subtract).then_inc(hl.sem, 1)

                def accumulate(c):
                    e, n = c // 4, c % 4
                    if n == 0:
                        dve.wait_ge(ac.sem, ac.before(g, 4 * e + 4))
                        dve.tensor_copy(w_cur[e][:, :], w_exp[:, bass.ds(2 * g + e, 1), :].rearrange("p e t -> p (e t)")
                                        ).then_inc(wcur.sem, 1)
                        dve.wait_ge(wcur.sem, wcur.now(g, e + 1))
                    dve.wait_ge(dn.sem, dn.now(g, c + 1))
                    dve.wait_ge(ac.sem, ac.now(g, c - 3) if c >= 4 else ac.before(g, NC2 - 3 + c))
                    if as2.last:
                        dve.wait_ge(as2.sem, as2.now(g, as2.last))
                    for j in range(4):
                        t = 4 * n + j
                        ins = dve.scalar_tensor_tensor(x_all[:, t, 0:D], ps[:, 4 + 2 * (c % 2) + j // 2, (j % 2) * D:(j % 2 + 1) * D],
                                                       w_cur[e][:, t:t + 1], x_all[:, t, 0:D], ALU.mult, ALU.add)
                        if j < 3:
                            as2.done(ins)
                        else:
                            ins.then_inc(ac.sem, 1)

                for i in range(NH2):
                    if i == 0:
                        dve.wait_ge(as2.sem, as2.before(g, as2.per))
                    multiply(i)
                    if i:
                        low(i - 1)
                    if i >= 4 and i % 2 == 0:
                        accumulate(i // 2 - 2)
                low(NH2 - 1)
                accumulate(NC2 - 2)
                accumulate(NC2 - 1)
                assert as2.last == as2.per

            for s in (n3, n3_lo, v1_ok, s1m, m1, x3, ex1, oh1, dest, ds3):
                s.credit(dve)
            dve.wait_ge(as2.sem, as2.total(E // 2))
            dve.wait_ge(ac.sem, ac.total(E // 2))
            with dve.Fori(0, G) as g:
                ds3.last = 0

                def seq3(ins):
                    dve.wait_ge(ds3.sem, ds3.now(g, ds3.done(ins)))

                def x3_of(n):
                    b = n % GB
                    if n < GB:
                        return x_all[:, bass.ds(g * GB + b, 1), 0:D].rearrange("p a d -> p (a d)")
                    return pay[:, b, 0:D]

                def statistics(n):
                    alone(dve)
                    seq3(dve.bn_stats(st3[:, n, :], x3_of(n)))
                    alone(dve)
                    seq3(dve.bn_aggr(mv3[:, n, :], st3[:, n, :]))

                def root3(half):
                    sel = slice(half * GB, (half + 1) * GB)
                    reciprocal_root(dve, seq3, mv3[:, sel, 1:2].rearrange("p n o -> p (n o)"), rstd3[:, sel], newton3[:, sel])

                def normalise(n):
                    dve.wait_ge(n3t.sem, n3t.now(g, n - 1) if n >= 2 else n3t.before(g, 2 * GB - 1 + n))
                    dve.tensor_scalar(xn3[n % 2], x3_of(n), mv3[:, n, 0:1], rstd3[:, n:n + 1], ALU.subtract, ALU.mult
                                      ).then_inc(n3.sem, 1)

                def low3(c):
                    dve.wait_ge(n3_hi.sem, n3_hi.now(g, c + 1))
                    dve.tensor_tensor(two_seqs(xnT[1], c % 2), in_bank(6 + c % 2), two_seqs(xnT[0], c % 2), ALU.subtract
                                      ).then_inc(n3_lo.sem, 1)

                dve.wait_ge(n3.sem, n3.before(g, 2 * GB))
                for b in range(GB):
                    statistics(b)
                root3(0)
                for b in range(GB):
                    normalise(b)
                for c in range(2):
                    dve.wait_ge(pv3.sem, pv3.now(g, c + 1))
                    dve.wait_ge(a1.sem, a1.before(g, 2))
                    dve.tensor_tensor(v1[:, 2 * c:2 * c + 2, :], ps[:, 2 + c, :].rearrange("p (b n) -> p b n", b=2),
                                      bv1r.rearrange("p (o n) -> p o n", o=1).to_broadcast([P, 2, D]), ALU.add
                                      ).then_inc(v1_ok.sem, 1)
                for c in range(2):
                    low3(c)
                dve.wait_ge(s1.sem, s1.now(g, 1))
                dve.wait_ge(s_m3, 16 * g + 16)
                dve.wait_ge(t1.sem, t1.before(g, 1))
                dve.scalar_tensor_tensor(sc1, mask, NEG, ps[:, 6, :].rearrange("p (b k) -> p b k", b=GB), ALU.mult, ALU.add
                                         ).then_inc(s1m.sem, 1)
                dve.wait_ge(s1m.sem, s1m.now(g, 1))
                dve.wait_ge(e1.sem, e1.before(g, GB))
                seq3(dve.tensor_reduce(nmax, sc1, AX.X, ALU.max))
                dve.tensor_scalar(nmax, nmax, -1.0, None, ALU.mult).then_inc(m1.sem, 1)
                dve.wait_ge(e1.sem, e1.now(g, GB))
                seq3(dve.reciprocal(gsc, sum1))
                seq3(dve.tensor_scalar(gsc, gsc, tgate[:, 1:2], None, ALU.mult))
                dve.wait_ge(rows_left.sem, rows_left.before(g, 1))
                dve.wait_ge(s_base, 16 * g + 16)
                for b in range(GB):
                    dve.wait_ge(a1.sem, a1.now(g, b // 2 + 1))
                    dve.scalar_tensor_tensor(pay[:, b, 0:D], ps[:, b // 2, (b % 2) * D:(b % 2 + 1) * D], gsc[:, b:b + 1],
                                             x3_of(b), ALU.mult, ALU.add).then_inc(x3.sem, 1)
                for b in range(GB):
                    dve.wait_ge(x3.sem, x3.now(g, b + 1))
                    statistics(GB + b)
                root3(1)
                for b in range(GB):
                    normalise(GB + b)
                seq3(dve.tensor_copy(pay[:, :, D:D + 1], rstd3[:, GB:2 * GB].rearrange("p (b o) -> p b o", o=1)))
                seq3(dve.scalar_tensor_tensor(pay[:, :, D + 1:D + 2], mv3[:, GB:2 * GB, 0:1], -1.0,
                                              rstd3[:, GB:2 * GB].rearrange("p (b o) -> p b o", o=1), ALU.mult, ALU.mult))
                for c in range(2, 4):
                    low3(c)
                dve.wait_ge(l1t.sem, l1t.now(g, 1))
                lp = ps[:, 3, 0:GB * E].rearrange("p (b e) -> p b e", e=E)

                def over8(col):
                    return col.rearrange("p (t o) -> p t o", o=1).to_broadcast([P, GB, E])
                seq3(dve.tensor_reduce(r3s[0], lp, AX.X, ALU.max))
                dve.wait_ge(r1e.sem, r1e.before(g, 1))
                dve.tensor_tensor(r3[4], lp, over8(r3s[0]), ALU.subtract).then_inc(ex1.sem, 1)
                seq3(dve.tensor_tensor(r3[0], lp, over8(r3s[0]), ALU.is_equal))
                seq3(dve.tensor_tensor(r3[0], r3[0], cst[:, C_REV:C_REV + GB * E].rearrange("p (b e) -> p b e", e=E), ALU.mult))
                seq3(dve.tensor_reduce(r3s[1], r3[0], AX.X, ALU.max))
                seq3(dve.tensor_tensor(r3[0], r3[0], over8(r3s[1]), ALU.is_equal))
                seq3(dve.tensor_copy(r3[1][:, 0, :], ones_before[:, :]))
                for b in range(1, GB):
                    seq3(dve.tensor_tensor(r3[1][:, b, :], r3[1][:, b - 1, :], r3[0][:, b - 1, :], ALU.add))
                seq3(dve.tensor_tensor(ones_before[:, :], r3[1][:, GB - 1, :], r3[0][:, GB - 1, :], ALU.add))
                dve.wait_ge(loc1.sem, loc1.before(g, 1))
                seq3(dve.tensor_copy(oh_b[:, 0, :, :], r3[0]))
                dve.tensor_copy(oh_b[:, 1, :, :], r3[1]).then_inc(oh1.sem, 1)
                dve.wait_ge(r1e.sem, r1e.now(g, 1))
                seq3(dve.tensor_reduce(r3s[2], r3[5], AX.X, ALU.add))
                seq3(dve.reciprocal(r3s[2], r3s[2]))
                seq3(dve.tensor_scalar(pay[:, :, D + 2:D + 3], r3s[2].rearrange("p (b o) -> p b o", o=1), tgate[:, 3:4], None, ALU.mult))
                seq3(dve.tensor_copy(pay[:, :, D + 3:D + 4], tokn[:, 0:GB].rearrange("p (b o) -> p b o", o=1)))
                seq3(dve.tensor_tensor(r3[3], r3[0], cst[:, C_IDX:C_IDX + GB * E].rearrange("p (b e) -> p b e", e=E), ALU.mult))
                seq3(dve.tensor_reduce(r3s[4], r3[3], AX.X, ALU.add))
                dve.wait_ge(loc1.sem, loc1.now(g, 1))
                seq3(dve.tensor_tensor(r3[2], ps[:, 3, GB * E:2 * GB * E].rearrange("p (b e) -> p b e", e=E), r3[0], ALU.mult))
                seq3(dve.tensor_reduce(r3s[3], r3[2], AX.X, ALU.add))
                seq3(dve.scalar_tensor_tensor(r3s[5], r3s[4], float(CAP), r3s[3], ALU.mult, ALU.add))
                seq3(dve.tensor_tensor(r3s[5], r3s[5], tokn[:, GB:2 * GB], ALU.subtract))
                seq3(dve.scalar_tensor_tensor(r3s[5], r3s[3], float(CAP), r3s[5], ALU.is_lt, ALU.mult))
                seq3(dve.tensor_tensor(r3s[5], r3s[5], tokn[:, GB:2 * GB], ALU.add))
                seq3(dve.tensor_scalar(tokn[:, :], tokn[:, :], float(GT), None, ALU.add))
                dve.tensor_copy(tok_idx[:, :], r3s[5]).then_inc(dest.sem, 1)
                assert ds3.last == DS3, ds3.last

            for s in (xd_ok, di_lo, w4_l2, h1_lo, y4, ds4, idx4):
                s.credit(dve)

            def slots_norm(g, i):
                for j in range(2):
                    row = xs[:, bass.ds(4 * g + 2 * i + j, 1), :].rearrange("p a c -> p (a c)") if not isinstance(g, int) \
                        else xs[:, 4 * g + 2 * i + j, :]
                    dve.wait_ge(xd_t.sem, xd_t.now(g, 1) if i else xd_t.before(g, 2))
                    dve.tensor_scalar(xd[j], row[:, 0:D], row[:, D:D + 1], row[:, D + 1:D + 2], ALU.mult, ALU.add
                                      ).then_inc(xd_ok.sem, 1)

            def slots_low(g, i):
                dve.wait_ge(di_hi.sem, di_hi.now(g, i + 1))
                dve.tensor_tensor(slot_cols(diT[i][1]), in_bank(6 + i), slot_cols(diT[i][0]), ALU.subtract
                                  ).then_inc(di_lo.sem, 1)

            def split_w2(g, i):
                dve.wait_ge(w4_hi.sem, w4_hi.now(g, 2 * i + 2))
                dve.tensor_tensor(w4[i][1][:, 1, :], raw4[i][:, 1, :], w4[i][0][:, 1, :], ALU.subtract).then_inc(w4_l2.sem, 1)

            def hidden_low(g, i, f):
                dve.wait_ge(h1_hi.sem, h1_hi.now(g, 8 * i + f + 1))
                dve.scalar_tensor_tensor(h4[i][1][:, f, :], ps[:, f % 4, 0:CAP], 0.0, h4[i][0][:, f, :], ALU.max, ALU.subtract
                                         ).then_inc(h1_lo.sem, 1)

            def rows_out(g, i):
                dve.wait_ge(d4.sem, d4.now(g, i + 1))
                dve.wait_ge(out_left.sem, out_left.before(g, i + 1))
                t = 4 * g + 2 * i
                sel = slice(t, t + 2) if isinstance(g, int) else bass.ds(t, 2)
                dve.tensor_copy(out_idx[i][:, :].rearrange("p (a o) -> p a o", o=1), xs[:, sel, D + 3:D + 4]).then_inc(idx4.sem, 1)
                for j in range(2):
                    row = xs[:, t + j, :] if isinstance(g, int) else xs[:, bass.ds(t + j, 1), :].rearrange("p a c -> p (a c)")
                    ins = dve.scalar_tensor_tensor(yo[i][j], ps[:, 4 + i, j * D:(j + 1) * D], row[:, D + 2:D + 3],
                                                   row[:, 0:D], ALU.mult, ALU.add)
                    ins.then_inc(y4.sem if j else ds4.sem, 1)

            def turn(g, last):
                for i in range(2):
                    nxt = (g, 1) if i == 0 else (g + 1, 0)
                    more = i == 0 or not last
                    if more:
                        slots_norm(*nxt)
                    for f in range(8):
                        hidden_low(g, i, f)
                        if more and f == 5:
                            split_w2(*nxt)
                    if more:
                        slots_low(*nxt)
                    rows_out(g, i)
            dve.wait_ge(s_xs, 16)
            slots_norm(0, 0)
            split_w2(0, 0)
            slots_low(0, 0)
            with dve.Fori(0, E // 2 - 1) as g:
                turn(g, False)
            turn(E // 2 - 1, True)

        @block.tensor
        def _(pe):
            for s in (xt_tr, pj_k, pj_v, pj_q, sc_q, sc_k, pv, o_tr, o_nt, wo, x1t):
                s.credit(pe)
            THREE = ((0, 0), (0, 1), (1, 0))

            def product(dst, left, right, last_of=None):
                n = 0
                for k in range(K2):
                    for i, j in THREE:
                        mm = pe.matmul(dst, left(i, k), right(j, k), start=(n == 0), stop=(n == 3 * K2 - 1))
                        n += 1
                return mm

            pe.wait_ge(s_const, 16)
            pe.wait_ge(s_wa_hi, 1)
            pe.wait_ge(s_wa_lo, 1)
            with pe.Fori(0, G) as g:
                pe.wait_ge(c_hi.sem, c_hi.now(g, 1))
                pe.wait_ge(c_lo.sem, c_lo.now(g, 1))
                pe.wait_ge(mx_ok.sem, mx_ok.before(g, UNITS))
                for m in range(2):
                    product(ps[:, m, :], lambda i, k: wa[i][:, 1, k, m * P:(m + 1) * P], lambda j, k: cT[j][:, k, :]
                            ).then_inc(pj_k.sem, 1)
                pe.wait_ge(ex.sem, ex.before(g, UNITS))
                for c in range(2):
                    for i in range(2):
                        b = 2 * c + i
                        mm = product(ps[:, 2 + c, i * D:(i + 1) * D], lambda i, k: cT[i][:, k, b * P:(b + 1) * P],
                                     lambda j, k: wa[j][:, 2, k, :])
                    mm.then_inc(pj_v.sem, 1)
                for b in range(GB):
                    pe.wait_ge(ln0.sem, ln0.now(g, b + 1))
                    if b == 0:
                        pe.wait_ge(x1_lo.sem, x1_lo.before(g, GB))
                        pe.wait_ge(x1_hi.sem, x1_hi.before(g, GB))
                    for k in range(K2):
                        mm = pe.transpose(ps[:, 6 + b // 2, (b % 2) * 256 + k * P:(b % 2) * 256 + (k + 1) * P],
                                          xn[b % 2][:, k * P:(k + 1) * P], ident)
                    mm.then_inc(xt_tr.sem, 1)
                pe.wait_ge(xt_hi.sem, xt_hi.now(g, 2))
                pe.wait_ge(xt_lo.sem, xt_lo.now(g, 2))
                for m in range(2):
                    product(ps[:, 4 + m, :], lambda i, k: wa[i][:, 0, k, m * P:(m + 1) * P], lambda j, k: xnT[j][:, k, :]
                            ).then_inc(pj_q.sem, 1)

                def scores_for_max(u):
                    b, gp = u // 2, u % 2
                    if u == 0:
                        pe.wait_ge(k_m.sem, k_m.now(g, 2))
                        pe.wait_ge(k_lo.sem, k_lo.now(g, 2))
                        pe.wait_ge(q_hi.sem, q_hi.now(g, 2))
                    else:
                        pe.wait_ge(mx_ok.sem, mx_ok.now(g, u))
                    for m in range(2):
                        for j in range(2):
                            r = 32 * (2 * gp + j)
                            mm = pe.matmul(ps[:, j, m * 256:(m + 1) * 256], qT[0][r:r + 32, m, b * P:(b + 1) * P],
                                           kM[r:r + 32, m, :, b * P:(b + 1) * P], start=True, stop=True,
                                           skip_group_check=True)
                    mm.then_inc(sc_q.sem, 1)

                def scores_shifted(u):
                    b, gp, bank = u // 2, u % 2, 2 + 2 * (u % 2)
                    if u == 0:
                        pe.wait_ge(q_m.sem, q_m.now(g, 8))
                        pe.wait_ge(v_ok.sem, v_ok.now(g, 4))
                    if u == 1:
                        pe.wait_ge(q_lo.sem, q_lo.now(g, 2))
                    if u >= 2:
                        pe.wait_ge(ex.sem, ex.now(g, u - 1))
                    n = 0
                    for i, jj in THREE:
                        for m in range(2):
                            for j in range(2):
                                r = 32 * (2 * gp + j)
                                pe.matmul(ps[:, bank + j, m * 256:(m + 1) * 256], kT[i][r:r + 32, m, b * P:(b + 1) * P],
                                          qM[jj][r:r + 32, m, :, b * P:(b + 1) * P], start=(n < 2), stop=False,
                                          skip_group_check=True)
                                n += 1

                def shift(u):
                    bank = 2 + 2 * (u % 2)
                    pe.wait_ge(dg.sem, dg.now(g, u + 1))
                    for j in range(2):
                        mm = pe.matmul(ps[:, bank + j, :], ones_r[:, :], diag[u % 2][:, 4 * j:4 * j + 4, :],
                                       start=False, stop=True, skip_group_check=True)
                    mm.then_inc(sc_k.sem, 1)

                def values(u):
                    b, gp = u // 2, u % 2
                    pe.wait_ge(ex.sem, ex.now(g, u + 1))
                    if gp == 0:
                        if b == 0:
                            pe.wait_ge(o_raw.sem, o_raw.before(g, GB))
                        else:
                            pe.wait_ge(o_raw.sem, o_raw.now(g, b))
                    for j in range(2):
                        c = 2 * gp + j
                        for s in range(4):
                            h = (s // 2) * 8 + c * 2 + s % 2
                            mm = pe.matmul(ps[32 * s:32 * s + 32, 6, c * P:(c + 1) * P], v0[:, b, h, :],
                                           probs[u % 2][:, 4 * j + s, :], start=True, stop=True, skip_group_check=True)
                    mm.then_inc(pv.sem, 1)

                def tail(b, step):
                    if step == 0:
                        pe.wait_ge(o_raw.sem, o_raw.now(g, b + 1))
                        pe.wait_ge(x1_lo.sem, x1_lo.now(g, b) if b else x1_lo.before(g, GB))
                        if b == 0:
                            pe.wait_ge(xt_lo.sem, xt_lo.now(g, 2))
                        for c in range(4):
                            mm = pe.transpose(ps[:, 7, c * P:(c + 1) * P], oT_raw[:, c, :], ident)
                        mm.then_inc(o_tr.sem, 1)
                    if step == 1:
                        pe.wait_ge(o_n.sem, o_n.now(g, b + 1))
                        for k in range(K2):
                            mm = pe.transpose(ps[:, 7, k * P:(k + 1) * P], o_tok[:, k * P:(k + 1) * P], ident)
                        mm.then_inc(o_nt.sem, 1)
                    if step == 2:
                        pe.wait_ge(oT_hi.sem, oT_hi.now(g, b + 1))
                        pe.wait_ge(oT_lo.sem, oT_lo.now(g, b + 1))
                        product(ps[:, 7, 256:512], lambda i, k: oT[i][:, k, :], lambda j, k: wa[j][:, 3, k, :]
                                ).then_inc(wo.sem, 1)
                    if step == 3:
                        pe.wait_ge(ln1.sem, ln1.now(g, b + 1))
                        for k in range(K2):
                            mm = pe.transpose(ps[:, 7, k * P:(k + 1) * P], xn[b % 2][:, k * P:(k + 1) * P], ident)
                        mm.then_inc(x1t.sem, 1)

                steps = []
                scores_for_max(0)
                for u in range(UNITS):
                    if u + 1 < UNITS:
                        scores_for_max(u + 1)
                    if steps:
                        tail(*steps.pop(0))
                    scores_shifted(u)
                    if steps:
                        tail(*steps.pop(0))
                    shift(u)
                    if u >= 1:
                        values(u - 1)
                        if u % 2 == 0:
                            steps += [(u // 2 - 1, i) for i in range(4)]
                values(UNITS - 1)
                steps += [(GB - 1, i) for i in range(4)]
                for s in steps:
                    tail(*s)

            pe.wait_ge(mx_ok.sem, mx_ok.total(G))
            pe.wait_ge(ex.sem, ex.total(G))
            pe.wait_ge(x1_lo.sem, x1_lo.total(G))
            for n in range(G):
                product(ps[:, n, :], lambda i, k: wr[i][:, 0, k, :], lambda j, k: xnT_all[j][:, k, n * GT:(n + 1) * GT]
                        ).then_inc(lg, 1)
            pe.wait_ge(lgc, G)
            for t in range(B):
                mm = pe.transpose(ps[:, 4, t * E:(t + 1) * E], lgT[0:E, t * P:(t + 1) * P], ident[0:E, 0:E])
            mm.then_inc(lgt, 1)
            pe.wait_ge(s_inh, 1)

            for s in (gt, up, dn):
                s.credit(pe)
            with pe.Fori(0, E // 2) as g:
                def gate_up(i):
                    e, n, m = i // 8, i // 2 % 4, i % 2
                    if i % 8 == 0:
                        pe.wait_ge(w2_hi.sem, w2_hi.now(g, e + 1))
                        pe.wait_ge(w2_lo.sem, w2_lo.now(g, e + 1))
                    for bank, at0, prior, done in ((0, 0, sl, gt), (2, 2 * I0, hm, up)):
                        pe.wait_ge(prior.sem, prior.now(g, i - 1) if i >= 2 else prior.before(g, NH2 - 1 + i))
                        product(ps[:, bank + i % 2, :],
                                lambda a, k: w2s[e][a][:, at0 + k * I0 + m * P:at0 + k * I0 + (m + 1) * P],
                                lambda b, k: xnT_all[b][:, k, n * GT:(n + 1) * GT]).then_inc(done.sem, 1)

                def down(c):
                    e = c // 4
                    pe.wait_ge(hh.sem, hh.now(g, 2 * c + 2))
                    pe.wait_ge(hl.sem, hl.now(g, 2 * c + 2))
                    pe.wait_ge(ac.sem, ac.now(g, c - 1) if c >= 2 else ac.before(g, NC2 - 1 + c))
                    for j in range(4):
                        mm = product(ps[:, 4 + 2 * (c % 2) + j // 2, (j % 2) * D:(j % 2 + 1) * D],
                                     lambda a, k: hT[c % 2][a][:, k, j * P:(j + 1) * P],
                                     lambda b, k: w2s[e][b][:, 4 * I0 + k * D:4 * I0 + (k + 1) * D])
                    mm.then_inc(dn.sem, 1)

                for c in range(NC2):
                    gate_up(2 * c)
                    gate_up(2 * c + 1)
                    if c:
                        down(c - 1)
                down(NC2 - 1)

            for s in (n3t, pk3, pv3, pq3, s1, t1, a1, l1, l1t, loc1):
                s.credit(pe)
            pe.wait_ge(ac.sem, ac.total(E // 2))
            pe.wait_ge(s_wa1_lo, 1)
            with pe.Fori(0, G) as g:
                def transposes3(n):
                    pe.wait_ge(n3.sem, n3.now(g, n + 1))
                    for k in range(K2):
                        mm = pe.transpose(ps[:, 6 + n // 2 % 2, (n % 2) * 256 + k * P:(n % 2) * 256 + (k + 1) * P],
                                          xn3[n % 2][:, k * P:(k + 1) * P], ident)
                    mm.then_inc(n3t.sem, 1)

                pe.wait_ge(c3_hi.sem, c3_hi.now(g, 1))
                pe.wait_ge(c3_lo.sem, c3_lo.now(g, 1))
                pe.wait_ge(x3.sem, x3.before(g, GB))
                for m in range(2):
                    product(ps[:, m, :], lambda i, k: wa[i][:, 1, k, m * P:(m + 1) * P], lambda j, k: cT[j][:, k, :]
                            ).then_inc(pk3.sem, 1)
                pe.wait_ge(dest.sem, dest.before(g, 1))
                pe.wait_ge(l1c.sem, l1c.before(g, 1))
                for c in range(2):
                    for i in range(2):
                        b = 2 * c + i
                        mm = product(ps[:, 2 + c, i * D:(i + 1) * D], lambda i, k: cT[i][:, k, b * P:(b + 1) * P],
                                     lambda j, k: wa[j][:, 2, k, :])
                    mm.then_inc(pv3.sem, 1)
                pe.wait_ge(n3_lo.sem, n3_lo.before(g, 4))
                for b in range(GB):
                    transposes3(b)
                pe.wait_ge(n3_hi.sem, n3_hi.now(g, 2))
                pe.wait_ge(n3_lo.sem, n3_lo.now(g, 2))
                pe.wait_ge(q1_ok.sem, q1_ok.before(g, 2))
                for m in range(2):
                    product(ps[:, 4 + m, :], lambda i, k: wa[i][:, 0, k, m * P:(m + 1) * P], lambda j, k: xnT[j][:, k, :]
                            ).then_inc(pq3.sem, 1)
                pe.wait_ge(k1_ok.sem, k1_ok.now(g, 2))
                pe.wait_ge(q1_ok.sem, q1_ok.now(g, 2))
                for b in range(GB):
                    for k in range(2):
                        mm = pe.matmul(ps[:, 6, b * P:(b + 1) * P], q1[:, k, b * P:(b + 1) * P], k1[:, k, b * P:(b + 1) * P],
                                       start=(k == 0), stop=(k == 1))
                mm.then_inc(s1.sem, 1)
                for b in range(GB):
                    pe.wait_ge(e1.sem, e1.now(g, b + 1))
                    mm = pe.transpose(ps[:, 7, b * P:(b + 1) * P], sc1[:, b, :], ident)
                mm.then_inc(t1.sem, 1)
                pe.wait_ge(p1_ok.sem, p1_ok.now(g, 1))
                pe.wait_ge(v1_ok.sem, v1_ok.now(g, 2))
                for b in range(GB):
                    mm = pe.matmul(ps[:, b // 2, (b % 2) * D:(b % 2 + 1) * D], p1T[:, b, :], v1[:, b, :], start=True, stop=True)
                    if b % 2:
                        mm.then_inc(a1.sem, 1)
                for n in range(GB, 2 * GB):
                    transposes3(n)
                pe.wait_ge(n3_hi.sem, n3_hi.now(g, 4))
                pe.wait_ge(n3_lo.sem, n3_lo.now(g, 4))
                product(ps[:, 2, :], lambda i, k: wr[i][:, 1, k, :], lambda j, k: xnT[j][:, k, :]).then_inc(l1.sem, 1)
                pe.wait_ge(l1c.sem, l1c.now(g, 1))
                alone(pe)
                for b in range(GB):
                    mm = pe.transpose(ps[:, 3, b * E:(b + 1) * E], lg1T[0:E, b * P:(b + 1) * P], ident[0:E, 0:E])
                mm.then_inc(l1t.sem, 1)
                pe.wait_ge(oh1.sem, oh1.now(g, 1))
                pe.matmul(ps[:, 3, GB * E:2 * GB * E], tri_b[:, :], oh_b[:, 0, :, :], start=True, stop=False)
                pe.matmul(ps[:, 3, GB * E:2 * GB * E], ones_b[:, :], oh_b[:, 1, :, :], start=False, stop=True
                          ).then_inc(loc1.sem, 1)

            for s in (xd_t, h1, d4):
                s.credit(pe)

            def slots_transposed(g, i):
                pe.wait_ge(xd_ok.sem, xd_ok.now(g, 2 * i + 2))
                pe.wait_ge(di_lo.sem, di_lo.before(g, i + 1))
                for j in range(2):
                    for k in range(K2):
                        mm = pe.transpose(ps[:, 6 + i, j * 256 + k * P:j * 256 + (k + 1) * P], xd[j][:, k * P:(k + 1) * P], ident)
                mm.then_inc(xd_t.sem, 1)

            def hidden(g, i, f):
                n = 8 * i + f
                if f == 0:
                    pe.wait_ge(di_hi.sem, di_hi.now(g, i + 1))
                    pe.wait_ge(di_lo.sem, di_lo.now(g, i + 1))
                    pe.wait_ge(w4_hi.sem, w4_hi.now(g, 2 * i + 1))
                    pe.wait_ge(w4_l1.sem, w4_l1.now(g, i + 1))
                pe.wait_ge(h1_lo.sem, h1_lo.now(g, n - 3) if n >= 4 else h1_lo.before(g, 16 - 3 + n))
                product(ps[:, f % 4, 0:CAP], lambda a, k: w4[i][a][:, 0, k * F1 + f * P:k * F1 + (f + 1) * P],
                        lambda b, k: diT[i][b][:, k, :]).then_inc(h1.sem, 1)

            def down4(g, i):
                pe.wait_ge(w4_hi.sem, w4_hi.now(g, 2 * i + 2))
                pe.wait_ge(w4_l2.sem, w4_l2.now(g, i + 1))
                pe.wait_ge(y4.sem, y4.before(g, i + 1))
                for j in range(2):
                    for f in range(8):
                        if j == 0:
                            pe.wait_ge(h1_lo.sem, h1_lo.now(g, 8 * i + f + 1))
                        for n, (a, b) in enumerate(THREE):
                            mm = pe.matmul(ps[:, 4 + i, j * D:(j + 1) * D], h4[i][a][:, f, j * P:(j + 1) * P],
                                           w4[i][b][:, 1, f * D:(f + 1) * D], start=(f == 0 and n == 0), stop=(f == 7 and n == 2))
                mm.then_inc(d4.sem, 1)

            def turn(g, last):
                for i in range(2):
                    for f in range(8):
                        hidden(g, i, f)
                    if i == 0 or not last:
                        slots_transposed(*((g, 1) if i == 0 else (g + 1, 0)))
                    down4(g, i)
            slots_transposed(0, 0)
            with pe.Fori(0, E // 2 - 1) as g:
                turn(g, False)
            turn(E // 2 - 1, True)

        @block.gpsimd
        def _(pool):
            for s in (c_lo, k_m, dg, xb_ok, w2q_hi, w2q_lo, w2_hi, w2_lo, c3_lo, w4_l1, rows_left, out_left):
                s.credit(pool)
            pool.wait_ge(s_fill, 1)
            pool.dma_start(slots[0:T, :].rearrange("(t p) c -> p t c", p=P),
                           fill[:, :].rearrange("p (o c) -> p o c", o=1).to_broadcast([P, T // P, ROW])).then_inc(s_fillw, 16)
            pool.wait_ge(s_bo, 1)
            pool.wait_ge(s_setup.sem, s_setup.last)
            for i in range(2):
                pool.wait_ge(s_raw2[i], 16)
            with pool.Fori(0, G) as g:
                pool.wait_ge(c_hi.sem, c_hi.now(g, 1))
                pool.tensor_tensor(cT[1], c_in, cT[0], ALU.subtract).then_inc(c_lo.sem, 1)
                quarter = bass.ds(g * (W2C // 2), W2C // 2)
                pool.tensor_copy(w2_both[0][:, quarter], raw_both[:, quarter]).then_inc(w2q_hi.sem, 1)
                for m in range(2):
                    pool.wait_ge(k_hi.sem, k_hi.now(g, m + 1))
                    pool.tensor_tensor(kM[:, m, :, :], kT[0][:, m:m + 1, :].to_broadcast([P, 2, GT]),
                                       parity[:, :].rearrange("p (r o) -> p r o", o=1).to_broadcast([P, 2, GT]), ALU.mult
                                       ).then_inc(k_m.sem, 1)
                pool.wait_ge(w2q_hi.sem, w2q_hi.now(g, 1))
                alone(pool)
                pool.tensor_tensor(w2_both[1][:, quarter], raw_both[:, quarter], w2_both[0][:, quarter], ALU.subtract
                                   ).then_inc(w2q_lo.sem, 1)
                for u in range(UNITS):
                    pool.wait_ge(mx_ok.sem, mx_ok.now(g, u + 1))
                    pool.wait_ge(sc_k.sem, sc_k.now(g, u - 1) if u >= 2 else sc_k.before(g, UNITS - 1 + u))
                    pool.tensor_tensor(diag[u % 2], neg_ident[:, :].rearrange("p (o q) -> p o q", o=1).to_broadcast([P, 8, P]),
                                       mx[u % 2].rearrange("p (h o) -> p h o", o=1).to_broadcast([P, 8, P]), ALU.mult
                                       ).then_inc(dg.sem, 1)
                    if u % 2:
                        b = u // 2
                        pool.wait_ge(ln0.sem, ln0.now(g, b + 1))
                        alone(pool)
                        xo = x_all[:, bass.ds(g * GB + b, 1), 0:D].rearrange("p a d -> p (a d)")
                        pool.tensor_tensor(xo, xo, bo0r, ALU.add).then_inc(xb_ok.sem, 1)
            pool.wait_ge(w2q_lo.sem, w2q_lo.total(G))
            pool.sem_inc(w2_hi.sem, 2)
            pool.sem_inc(w2_lo.sem, 2)
            with pool.Fori(1, E // 2) as g:
                for i in range(2):
                    pool.wait_ge(s_raw2[i], 16 * g + 16)
                    pool.wait_ge(dn.sem, dn.before(g, 4 * i + 4))
                    alone(pool)
                    pool.tensor_copy(w2s[i][0], raw[i]).then_inc(w2_hi.sem, 1)
                    pool.wait_ge(w2_hi.sem, w2_hi.now(g, i + 1))
                    pool.tensor_tensor(w2s[i][1], raw[i], w2s[i][0], ALU.subtract).then_inc(w2_lo.sem, 1)
            pool.wait_ge(s_wa1, 16)
            pool.wait_ge(wo.sem, wo.total(G))
            pool.tensor_copy(wa[0][:, 0:3, :, :], wa1_raw).then_inc(s_wa1_hi, 1)
            pool.wait_ge(s_wa1_hi, 1)
            pool.tensor_tensor(wa[1][:, 0:3, :, :], wa1_raw, wa[0][:, 0:3, :, :], ALU.subtract).then_inc(s_wa1_lo, 1)
            pool.wait_ge(s_fillw, 16)
            with pool.Fori(0, G) as g:
                pool.wait_ge(c3_hi.sem, c3_hi.now(g, 1))
                pool.tensor_tensor(cT[1], c_in, cT[0], ALU.subtract).then_inc(c3_lo.sem, 1)
                pool.wait_ge(dest.sem, dest.now(g, 1))
                alone(pool)
                for b in range(GB):
                    pool.indirect_dma_start(out=slots[:, :], out_offset=bass.IndirectOffsetOnAxis(ap=tok_idx[:, b:b + 1], axis=0),
                                            in_=pay[:, b, :], in_offset=None).then_inc(s_disp, 16)
                pool.wait_ge(s_disp, 16 * GB * g + 16 * GB)
                alone(pool)
                pool.sem_inc(rows_left.sem, 1)

            def split_w1(g, i):
                pool.wait_ge(w4_hi.sem, w4_hi.now(g, 2 * i + 1))
                pool.tensor_tensor(w4[i][1][:, 0, :], raw4[i][:, 0, :], w4[i][0][:, 0, :], ALU.subtract).then_inc(w4_l1.sem, 1)

            def scatter(g, i):
                pool.wait_ge(y4.sem, y4.now(g, i + 1))
                pool.wait_ge(ds4.sem, ds4.now(g, i + 1))
                pool.wait_ge(idx4.sem, idx4.now(g, i + 1))
                alone(pool)
                for j in range(2):
                    pool.indirect_dma_start(out=out.rearrange("b s d -> (b s) d"),
                                            out_offset=bass.IndirectOffsetOnAxis(ap=out_idx[i][:, j:j + 1], axis=0),
                                            in_=yo[i][j], in_offset=None, bounds_check=T - 1, oob_is_err=False
                                            ).then_inc(s_sc[i], 16)
                pool.wait_ge(s_sc[i], 32 * g + 32)
                alone(pool)
                pool.sem_inc(out_left.sem, 1)

            def turn(g, last):
                for i in range(2):
                    if i == 0 or not last:
                        split_w1(*((g, 1) if i == 0 else (g + 1, 0)))
                    scatter(g, i)
            split_w1(0, 0)
            with pool.Fori(0, E // 2 - 1) as g:
                turn(g, False)
            turn(E // 2 - 1, True)
            for i in range(2):
                pool.wait_ge(s_sc[i], 32 * (E // 2))


def layout(inputs):
    a = {k: np.asarray(v) for k, v in inputs.items()}
    rows = np.arange(D).reshape(2, 4, 2, DH).transpose(1, 0, 2, 3).reshape(-1)
    return {
        "x": a["x"], "ctxT": np.ascontiguousarray(a["ctx_1024"].reshape(T, D).T), "maskf": a["mask_BxSxS2_fk0"],
        "gx": a["g_xattn"], "gf": a["g_ffn"],
        "wa0": np.stack([a["L0_xattn_Wq"].T, a["L0_xattn_Wk"].T, a["L0_xattn_Wv"].T, a["L0_xattn_Wo"].T[rows]]),
        "bcols": np.concatenate([a[n].reshape(2, P).T for n in ("L0_xattn_bq", "L0_xattn_bk", "L1_xattn_bq", "L1_xattn_bk")], axis=1),
        "bv0": a["L0_xattn_bv"], "bo0": a["L0_xattn_bo"],
        "w0": np.concatenate([a[f"L0_ffn_{n}"].reshape(E, K2, P, 256).transpose(0, 2, 1, 3).reshape(E, P, 512)
                              for n in ("Wg", "Wu", "Wd")], axis=2),
        "wrs": np.stack([a["L0_ffn_Wr"], a["L1_ffn_wg"]]), "temp": a["L0_ffn_temperature"],
        "wa1": np.stack([a["L1_xattn_Wq"], a["L1_xattn_Wk"], a["L1_xattn_Wv"]]),
        "bv1": a["L1_xattn_bv"],
        "w1": a["L1_ffn_w1"], "w2": a["L1_ffn_w2"], "const": constants(),
    }


def kernel(**inputs):
    from concourse import bacc
    from concourse.bass_utils import run_bass_kernel_spmd

    nc = bacc.Bacc("TRN2", target_bir_lowering=False, num_devices=1)
    arrays, args = {}, []
    for name, a in layout(inputs).items():
        a = np.ascontiguousarray(a)
        arrays[f"in_{name}"] = a
        args.append(nc.dram_tensor(f"in_{name}", a.shape, mybir.dt.from_np(a.dtype), kind="ExternalInput").ap())
    out = nc.dram_tensor("out", (B, S, D), F32, kind="ExternalOutput").ap()
    slots = nc.dram_tensor("slots", (2 * T, ROW), F32, kind="Internal").ap()
    block_kernel(nc, *args, out, slots)
    r = run_bass_kernel_spmd(nc, [arrays], core_ids=[0])
    return r.results[0]["out"]
```

```python
import math
from contextlib import ExitStack

import numpy as np

import concourse.bass as bass
from concourse import mybir

ALU = mybir.AluOpType
ACT = mybir.ActivationFunctionType
AX = mybir.AxisListType
F32 = mybir.dt.float32
F32R = mybir.dt.float32r
BF16 = mybir.dt.bfloat16
I32 = mybir.dt.int32

P = 128
B, S, D = 16, 128, 256
K2 = D // P
H, DH = 16, 16
T = B * S
GB = 4
G = B // GB
GT = GB * S
UNITS = 2 * GB
E = 8
I0 = 256
W2C = 6 * I0
F1 = 1024
CAP = T // E
ROW = D + 4
EPS = 1e-5
RSQ = 11
VS1 = 2 * GB + RSQ + (2 + RSQ) * GB + GB
DSA, DSB = 9, 29
GOLD = 1.0 / math.e
GOLD_LO = 0.5 - math.log(4.0 / 3.0)
Z_LO = math.log(GOLD_LO / (1.0 - GOLD_LO))
NEG = -1000000000.0
C_ID, C_TRI, C_ODD, C_IDX, C_REV, C_TOK, C_OWN = 0, 128, 256, 257, 257 + 128, 257 + 256, 257 + 260
C_N = 257 + 264


def constants():
    p = np.arange(P)
    c = np.zeros((P, C_N), np.float32)
    c[:, C_ID:C_ID + P] = np.eye(P)
    c[:, C_TRI:C_TRI + P] = p[:, None] < p[None, :]
    c[:, C_ODD] = (p // DH) % 2
    c[:, C_IDX:C_IDX + P] = np.tile(np.arange(E), P // E)
    c[:, C_REV:C_REV + P] = E - np.tile(np.arange(E), P // E)
    c[:, C_TOK:C_TOK + GB] = p[:, None] + S * np.arange(GB)
    c[:, C_OWN:C_OWN + GB] = T + p[:, None] + S * np.arange(GB)
    return c


class Signal:

    def __init__(self, sem, per):
        self.sem, self.per = sem, per

    def credit(self, eng):
        eng.sem_inc(self.sem, self.per)

    def now(self, g, n):
        return g * self.per + (self.per + n)

    def before(self, g, n):
        return g * self.per + n

    def total(self, turns):
        return (turns + 1) * self.per


class Steps(Signal):

    def __init__(self, sem, per):
        super().__init__(sem, per)
        self.last = 0

    def done(self, ins):
        ins.then_inc(self.sem, 1)
        self.last += 1
        return self.last


def block_kernel(nc, x, ctxT, maskf, gx, gf, wa0, bcols, bv0, bo0, w0, wrs, temp, wa1, bv1,
                 w1, w2, const, out, slots, stop_after=4):
    with ExitStack() as ctx:
        def sem(name):
            return ctx.enter_context(nc.semaphore(name))

        def sb(name, cols, dt=F32):
            return ctx.enter_context(nc.sbuf_tensor(name, [P, cols], dt))

        psum = ctx.enter_context(nc.psum_tensor("psum", [P, 8, 512], F32))

        x_all = sb("x_all", B * ROW).rearrange("p (t c) -> p t c", c=ROW)
        cst = sb("cst", C_N)
        ident = cst[:, C_ID:C_ID + P]
        neg_ident = sb("neg_ident", P)
        parity = sb("parity", 2)
        ones_r = sb("ones_r", P, F32R)
        ones_b = sb("ones_b", P, BF16)
        tri_b = sb("tri_b", P, BF16)
        biasc = sb("biasc", 8)
        biasr = sb("biasr", 3 * D)
        bv0r, bo0r, bv1r = (biasr[:, i * D:(i + 1) * D] for i in range(3))
        scal = sb("scal", 8)
        scratch = sb("scratch", 2 * GB)
        wr_raw = sb("wr_raw", 2 * K2 * E).rearrange("p (l k n) -> p l k n", l=2, k=K2)
        fill = sb("fill", ROW)
        bq1s = sb("bq1s", 2)
        w_exp = sb("w_exp", E * B).rearrange("p (e t) -> p e t", e=E)
        w_cur = [sb(f"w_cur{i}", B) for i in range(2)]
        tgate = sb("tgate", 4)
        arena = sb("arena", 36352, F32R)
        at = [0]

        def cut(cols):
            at[0] += cols
            assert at[0] <= 36352
            return arena[:, at[0] - cols:at[0]]

        def pair(cols):
            return cut(cols), cut(cols)

        wa = pair(4 * K2 * D)
        wa = [w.rearrange("p (m k n) -> p m k n", m=4, k=K2) for w in wa]
        xnT_all = [w.rearrange("p (k t) -> p k t", k=K2) for w in pair(K2 * T)]
        w2_both = pair(2 * W2C)
        w2s = [[w[:, i * W2C:(i + 1) * W2C] for w in w2_both] for i in range(2)]
        wr = [w.rearrange("p (l k n) -> p l k n", l=2, k=K2) for w in pair(2 * K2 * P)]
        mark = at[0]
        cT = [w.rearrange("p (k t) -> p k t", k=K2) for w in pair(K2 * GT)]
        xnT = [w.rearrange("p (k t) -> p k t", k=K2) for w in pair(K2 * GT)]
        kT_at = at[0]
        kT = [w.rearrange("p (m t) -> p m t", m=2) for w in pair(2 * GT)]
        kM = cut(4 * GT).rearrange("p (m r t) -> p m r t", m=2, r=2)
        qT = [w.rearrange("p (m t) -> p m t", m=2) for w in pair(2 * GT)]
        qM = [w.rearrange("p (m r t) -> p m r t", m=2, r=2) for w in pair(4 * GT)]
        diag = [cut(8 * P).rearrange("p (h q) -> p h q", h=8) for _ in range(2)]
        oT = [w.rearrange("p (k t) -> p k t", k=K2) for w in pair(K2 * P)]
        at[0] = kT_at
        xnT_b = [w.rearrange("p (k t) -> p k t", k=K2) for w in pair(K2 * GT)]
        at[0] = mark
        hT = [[w.rearrange("p (k t) -> p k t", k=2) for w in pair(2 * GT)] for _ in range(2)]
        at[0] = 0
        w4 = [[w.rearrange("p (a n) -> p a n", a=2) for w in pair(2 * 2048)] for _ in range(2)]
        diT = [[w.rearrange("p (k c) -> p k c", k=K2) for w in pair(K2 * CAP)] for _ in range(2)]
        h4 = [[w.rearrange("p (f c) -> p f c", f=8) for w in pair(8 * CAP)] for _ in range(2)]

        work = sb("work", 9728)
        wat = [0]

        def fcut(cols):
            wat[0] += cols
            assert wat[0] <= 9728, wat
            return work[:, wat[0] - cols:wat[0]]

        raw_both = fcut(2 * W2C)
        raw = [raw_both[:, i * W2C:(i + 1) * W2C] for i in range(2)]
        c_in = fcut(K2 * GT).rearrange("p (k t) -> p k t", k=K2)
        fmark = wat[0]
        v0 = fcut(GB * H * 32).rearrange("p (b h d) -> p b h d", b=GB, h=H)
        probs = [fcut(8 * P).rearrange("p (h q) -> p h q", h=8) for _ in range(2)]
        oT_raw = fcut(512).rearrange("p (c q) -> p c q", c=4)
        o_tok = fcut(D)
        xn = [fcut(D) for _ in range(2)]
        stats = fcut(2 * 6 * GB).rearrange("p (n s) -> p n s", s=6)
        mv = fcut(2 * 2 * GB).rearrange("p (n s) -> p n s", s=2)
        rstd, newton = fcut(2 * GB), fcut(2 * GB)
        mx = [fcut(8) for _ in range(2)]
        rden = fcut(H)

        wat[0] = fmark
        lgT = fcut(T)
        gu_s = [fcut(GT) for _ in range(2)]
        gu_h = [fcut(GT) for _ in range(2)]
        rt = [fcut(P) for _ in range(9)]
        rs = [fcut(B) for _ in range(4)]
        wat[0] = 0
        k1 = fcut(2 * GT).rearrange("p (m t) -> p m t", m=2)
        q1 = fcut(2 * GT).rearrange("p (m t) -> p m t", m=2)
        mask = fcut(GT).rearrange("p (b k) -> p b k", b=GB)
        assert wat[0] <= 2 * W2C
        wat[0] = fmark
        wa1_raw = fcut(3 * K2 * D).rearrange("p (m k n) -> p m k n", m=3, k=K2)
        wat[0] = fmark
        v1 = fcut(GB * D).rearrange("p (b n) -> p b n", b=GB)
        sc1 = fcut(GT).rearrange("p (b k) -> p b k", b=GB)
        p1T = fcut(GT).rearrange("p (b q) -> p b q", b=GB)
        lg1T = fcut(GT)
        r3 = [fcut(GB * E).rearrange("p (b e) -> p b e", b=GB) for _ in range(4)]
        r3s = [fcut(GB) for _ in range(6)]
        counted = fcut(E)
        xn_a, xn_b = [fcut(D) for _ in range(GB)], [fcut(D) for _ in range(GB)]
        st3 = fcut(2 * 6 * GB).rearrange("p (n s) -> p n s", s=6)
        mv3 = fcut(2 * 2 * GB).rearrange("p (n s) -> p n s", s=2)
        rstd3, newton3 = fcut(2 * GB), fcut(2 * GB)
        nmax, sum1, gsc = fcut(GB), fcut(GB), fcut(GB)
        tok_idx = sb("tok_idx", B, I32)
        ones_before = sb("ones_before", E, BF16)
        oh_b = sb("oh_b", GB * E, BF16).rearrange("p (b e) -> p b e", b=GB)
        tokn = sb("tokn", 2 * GB)
        wat[0] = 0
        raw4 = [fcut(4096).rearrange("p (a n) -> p a n", a=2) for _ in range(2)]
        xd = [fcut(D) for _ in range(2)]
        yo = [[fcut(D) for j in range(2)] for i in range(2)]
        out_idx = [sb(f"out_idx{i}", 2, I32) for i in range(2)]
        xs = x_all

        ps = psum

        s_passed = sem("wait_passed")

        def reciprocal_root(dve, step, var, r, t):
            step(dve.tensor_scalar(t, var, EPS, None, ALU.add))
            step(dve.tensor_scalar(r.bitcast(I32), t.bitcast(I32), -0.5, float(0x5f3759df), ALU.mult, ALU.add))
            for _ in range(3):
                step(dve.tensor_tensor(u := scratch[:, 0:r.shape[1]], r, r, ALU.mult))
                step(dve.scalar_tensor_tensor(u, u, -0.5, t, ALU.mult, ALU.mult))
                step(dve.scalar_tensor_tensor(r, u, 1.5, r, ALU.add, ALU.mult))

        def alone(eng):
            eng.sem_inc(s_passed, 1)

        s_const, s_small = sem("const_loaded"), sem("small_loaded")
        s_waraw = sem("attn_weights_loaded")
        s_x, s_c = sem("x_loaded"), sem("ctx_loaded")
        s_setup = Steps(sem("vector_setup_step"), 0)
        s_wa_hi, s_wa_lo = sem("attn_weights_high"), sem("attn_weights_low")
        s_bo = sem("bias_gated")
        s_tanh, s_fill = sem("tanh_ready"), sem("fill_ready")
        sg = {}

        def signal(name, per):
            sg[name] = Signal(sem(name), per)
            return sg[name]

        c_hi, c_lo = signal("ctx_high", 1), signal("ctx_low", 1)
        ln0 = signal("xn_ready", GB)
        xt_tr = signal("xn_transposed", GB)
        xt_hi, xt_lo = signal("xnT_high", 2), signal("xnT_low", 2)
        pj_k, pj_v, pj_q = signal("k_projected", 2), signal("v_projected", 2), signal("q_projected", 2)
        k_hi, k_lo, k_m = signal("k_high", 2), signal("k_low", 2), signal("k_masked", 2)
        v_ok = signal("v_ready", 2 * 2)
        q_hi, q_lo, q_m = signal("q_high", 2), signal("q_low", 2), signal("q_masked", 8)
        sc_q = signal("scores_for_max", UNITS)
        mx_ok, dg = signal("max_ready", UNITS), signal("diag_ready", UNITS)
        sc_k = signal("scores_shifted", UNITS)
        ex = signal("exp_ready", UNITS)
        pv = signal("pv_done", UNITS)
        o_raw = signal("oT_copied", GB)
        o_tr = signal("o_transposed", GB)
        o_n = signal("o_normalised", GB)
        o_nt = signal("o_back", GB)
        oT_hi, oT_lo = signal("oT_high", GB), signal("oT_low", GB)
        wo = signal("wo_done", GB)
        x1 = signal("x_after_attn", GB)
        ln1 = signal("xn1_ready", GB)
        x1t = signal("xn1_transposed", GB)
        x1_hi, x1_lo = signal("xn1T_high", GB), signal("xn1T_low", GB)
        xb_ok = signal("x_with_bias", GB)
        vs = Steps(sem("vector_step"), VS1)


        NC2, NH2 = 2 * G, 4 * G
        lg, lgc, lgt = sem("logits_ready"), sem("logits_copied"), sem("logits_transposed")
        s_wexp = sem("routing_weights_ready")
        re_step = Steps(sem("routing_step"), 0)
        s_inh, s_fb = sem("sigmoid_exp_ready"), sem("zone_exp_ready")
        s_raw2 = [sem(f"expert_weights_loaded{i}") for i in range(2)]
        w2q_hi, w2q_lo = signal("first_experts_high", 1), signal("first_experts_low", 1)
        w2_hi, w2_lo = signal("expert_high", 2), signal("expert_low", 2)
        gt, up = signal("gate_ready", NH2), signal("up_ready", NH2)
        sl, hm = signal("silu_ready", NH2), signal("h_ready", NH2)
        hh, hl = signal("h_high", NH2), signal("h_low", NH2)
        dn, ac = signal("down_ready", NC2), signal("x_accumulated", NC2)
        wcur = signal("expert_weight_picked", 2)
        as2 = Steps(sem("vector_step2"), 3 * NC2)

        s_c3, s_m3, s_wa1, s_base = sem("ctx3_loaded"), sem("mask_loaded"), sem("wa1_loaded"), sem("base_out_written")
        s_wa1_hi, s_wa1_lo = sem("wa1_high"), sem("wa1_low")
        s_disp = sem("rows_dispatched")
        c3_hi, c3_lo = signal("ctx3_high", 1), signal("ctx3_low", 1)
        na, nat = signal("xn2_ready", GB), signal("xn2_transposed", GB)
        na_hi, na_lo = signal("xn2T_high", 2), signal("xn2T_low", 2)
        nb, nbt = signal("xn3_ready", GB), signal("xn3_transposed", GB)
        nb_hi, nb_lo = signal("xn3T_high", 2), signal("xn3T_low", 2)
        pk3, pv3, pq3 = signal("k1_projected", 2), signal("v1_projected", 2), signal("q1_projected", 2)
        k1_ok, v1_ok, q1_ok = signal("k1_ready", 2), signal("v1_ready", 2), signal("q1_ready", 2)
        s1 = signal("scores1_ready", 1)
        s1m, m1 = signal("scores1_masked", 1), signal("max1_ready", 1)
        e1 = signal("probs1_ready", GB)
        t1 = signal("probs1_transposed", 1)
        p1_ok = signal("probs1T_ready", 1)
        a1 = signal("attn1_ready", 2)
        x3 = signal("x3_ready", GB)
        l1, l1c, l1t = signal("logits1_ready", 1), signal("logits1_copied", 1), signal("logits1_transposed", 1)
        ex1, r1e = signal("gate_shift_ready", 1), signal("gate_exp_ready", 1)
        oh1, loc1 = signal("onehot_ready", 1), signal("places_ready", 1)
        dest = signal("rows_ready", 1)
        dsa, dsb = Steps(sem("vector_step3a"), DSA), Steps(sem("vector_step3b"), DSB)
        dsr = Steps(sem("vector_root_step3"), RSQ)

        s_xs = [sem("first_slots_loaded"), sem("other_slots_loaded")]
        s_raw4 = [sem(f"expert1_weights_loaded{i}") for i in range(2)]
        w4_hi, w4_l1, w4_l2 = signal("expert1_high", 4), signal("expert1_w1_low", 2), signal("expert1_w2_low", 2)
        xd_ok = signal("slots_normalised", 4)
        xd_t = signal("slots_transposed", 2)
        di_hi, di_lo = signal("slotsT_high", 2), signal("slotsT_low", 2)
        h1, h1_hi, h1_lo = signal("hidden_ready", 16), signal("hidden_high", 16), signal("hidden_low", 16)
        d4 = signal("expert1_out_ready", 2)
        y4 = signal("rows_out_ready", 2)
        idx4 = signal("row_numbers_ready", 2)
        out_left = signal("rows_out_left", 2)
        s_sc = [sem(f"rows_scattered{i}") for i in range(2)]
        ds4 = Steps(sem("vector_step4"), 2)

        block = ctx.enter_context(nc.Block())

        def two_seqs(t, c):
            return t[:, :, 2 * c * P:(2 * c + 2) * P].rearrange("p k (b t) -> p b k t", b=2)

        def slot_cols(t):
            return t.rearrange("p k (b t) -> p b k t", b=2)

        def in_bank(i):
            return ps[:, i, :].rearrange("p (b k t) -> p b k t", b=2, k=K2)

        @block.sync
        def _(sp):
            sp.dma_start(cst[:, :], const).then_inc(s_const, 16)
            sp.dma_start(x_all[:, 0:GB, 0:D], x[0:GB].rearrange("b s d -> s b d")).then_inc(s_x, 16)
            sp.dma_start(probs_raw := work[:, fmark:fmark + 4 * K2 * D].rearrange("p (m k n) -> p m k n", m=4, k=K2),
                         wa0.rearrange("m (k p) n -> p m k n", p=P)).then_inc(s_waraw, 16)
            sp.dma_start(c_in, ctxT[:, 0:GT].rearrange("(k p) t -> p k t", p=P)).then_inc(s_c, 16)
            sp.dma_start(biasc[:, :], bcols).then_inc(s_small, 16)
            for i, b in enumerate((bv0, bo0, bv1)):
                sp.dma_start(biasr[:, i * D:(i + 1) * D], b.rearrange("(a d) -> a d", a=1).to_broadcast([P, D])
                             ).then_inc(s_small, 16)
            sp.dma_start(wr_raw, wrs.rearrange("l (k p) e -> p l k e", p=P)).then_inc(s_small, 16)
            for a, i, n in ((gx, 0, 2), (gf, 2, 2), (temp, 4, 1)):
                sp.dma_start(scal[:, i:i + n], a.rearrange("(a d) -> a d", a=1).to_broadcast([P, n])
                             ).then_inc(s_small, 16)
            for i in range(2):
                sp.dma_start(raw[i], w0[i:i + 1].rearrange("e p n -> p (e n)")).then_inc(s_raw2[i], 16)
            with sp.Fori(0, G - 1) as g:
                sp.wait_ge(s_x, g * 16 + 16)
                alone(sp)
                sp.wait_ge(c_hi.sem, c_hi.now(g, 1))
                alone(sp)
                sp.wait_ge(c_lo.sem, c_lo.now(g, 1))
                alone(sp)
                sp.dma_start(x_all[:, bass.ds(g * GB + GB, GB), 0:D],
                             x[bass.ds(g * GB + GB, GB)].rearrange("b s d -> s b d")).then_inc(s_x, 16)
                sp.dma_start(c_in, ctxT[:, bass.ds(g * GT + GT, GT)].rearrange("(k p) t -> p k t", p=P)
                             ).then_inc(s_c, 16)
            sp.sem_inc(s_base, 16)
            with sp.Fori(1, E // 2) as g:
                for i in range(2):
                    sp.wait_ge(w2_lo.sem, w2_lo.before(g, i + 1))
                    alone(sp)
                    sp.dma_start(raw[i], w0[bass.ds(2 * g + i, 1)].rearrange("e p n -> p (e n)")).then_inc(s_raw2[i], 16)
            sp.wait_ge(s_wexp, 1)
            sp.dma_start(wa1_raw, wa1.rearrange("m (k p) n -> p m k n", p=P)).then_inc(s_wa1, 16)
            sp.wait_ge(w2_lo.sem, w2_lo.total(E // 2))
            def loads(g):
                sp.wait_ge(c3_lo.sem, c3_lo.before(g, 1))
                alone(sp)
                sp.wait_ge(c3_hi.sem, c3_hi.before(g, 1))
                alone(sp)
                sp.dma_start(c_in, ctxT[:, bass.ds(g * GT, GT)].rearrange("(k p) t -> p k t", p=P)).then_inc(s_c3, 16)
                sp.wait_ge(s1m.sem, s1m.before(g, 1))
                alone(sp)
                sp.dma_start(mask, maskf[bass.ds(g * GB, GB)].rearrange("b q k -> q b k")).then_inc(s_m3, 16)

            def base_out(g):
                sp.wait_ge(x3.sem, x3.now(g, GB))
                alone(sp)
                sp.dma_start(out[bass.ds(g * GB, GB)].rearrange("b s d -> s b d"), x_all[:, bass.ds(g * GB, GB), 0:D]
                             ).then_inc(s_base, 16)
            def load4(i, e):
                sp.dma_start(raw4[i][:, 0, :].rearrange("p (k n) -> p k n", k=K2),
                             w1[e].rearrange("e (k p) n -> p (e k) n", p=P)).then_inc(s_raw4[i], 16)
                sp.dma_start(raw4[i][:, 1, :].rearrange("p (f n) -> p f n", f=8),
                             w2[e].rearrange("e (f p) n -> p (e f) n", p=P)).then_inc(s_raw4[i], 16)

            loads(0)
            with sp.Fori(0, G - 1) as g:
                loads(g + 1)
                base_out(g)
            sp.wait_ge(c3_lo.sem, c3_lo.total(G))
            sp.wait_ge(s1m.sem, s1m.total(G))
            load4(0, slice(0, 1))
            base_out(G - 1)
            sp.wait_ge(s_disp, 16 * B + 16)
            sp.wait_ge(s_base, 16 * (1 + G))
            sp.wait_ge(dsb.sem, dsb.total(G))

            for n, tiles in enumerate((slice(0, 4), slice(4, B))):
                sp.dma_start(xs[:, tiles, :], slots[tiles.start * P:tiles.stop * P, :].rearrange("(t p) c -> p t c", p=P)
                             ).then_inc(s_xs[n], 16)
                if n == 0:
                    load4(1, slice(1, 2))
            with sp.Fori(0, E // 2 - 1) as g:
                for i in range(2):
                    sp.wait_ge(w4_hi.sem, w4_hi.now(g, 2 * i + 2))
                    alone(sp)
                    sp.wait_ge(w4_l1.sem, w4_l1.now(g, i + 1))
                    alone(sp)
                    sp.wait_ge(w4_l2.sem, w4_l2.now(g, i + 1))
                    alone(sp)
                    load4(i, bass.ds(2 * g + 2 + i, 1))

        @block.scalar
        def _(act):
            wraw = work[:, fmark:fmark + 4 * K2 * D].rearrange("p (m k n) -> p m k n", m=4, k=K2)
            for s in (c_hi, xt_hi, k_hi, q_hi, ex, o_raw, oT_hi, x1_hi):
                s.credit(act)
            act.wait_ge(s_waraw, 16)
            act.activation(wa[0][:, :, :, :], wraw, ACT.Copy).then_inc(s_wa_hi, 1)
            act.wait_ge(s_small, 16 * 8)
            act.activation(tgate[:, :], scal[:, 0:4], ACT.Tanh).then_inc(s_tanh, 1)
            act.wait_ge(s_wa_lo, 1)
            with act.Fori(0, G) as g:
                act.wait_ge(s_c, g * 16 + 16)
                act.wait_ge(pj_k.sem, pj_k.before(g, 2))
                act.wait_ge(pj_v.sem, pj_v.before(g, 2))
                act.activation(cT[0], c_in, ACT.Copy).then_inc(c_hi.sem, 1)
                for m in range(2):
                    act.wait_ge(pj_k.sem, pj_k.now(g, m + 1))
                    act.wait_ge(sc_k.sem, sc_k.before(g, UNITS))
                    act.wait_ge(k_m.sem, k_m.before(g, 2))
                    act.activation(kT[0][:, m, :], ps[:, m, :], ACT.Identity, bias=biasc[:, 2 + m:3 + m]
                                   ).then_inc(k_hi.sem, 1)
                for c in range(2):
                    act.wait_ge(xt_tr.sem, xt_tr.now(g, 2 * c + 2))
                    act.activation(two_seqs(xnT[0], c), in_bank(6 + c), ACT.Copy).then_inc(xt_hi.sem, 1)
                for m in range(2):
                    act.wait_ge(pj_q.sem, pj_q.now(g, m + 1))
                    act.activation(qT[0][:, m, :], ps[:, 4 + m, :], ACT.Identity, bias=biasc[:, m:m + 1]
                                   ).then_inc(q_hi.sem, 1)

                def tail_a(b):
                    act.wait_ge(pv.sem, pv.now(g, 2 * b + 2))
                    act.wait_ge(o_tr.sem, o_tr.now(g, b) if b else o_tr.before(g, GB))
                    act.activation(oT_raw, ps[:, 6, :].rearrange("p (c q) -> p c q", c=4), ACT.Copy).then_inc(o_raw.sem, 1)

                def tail_b(b):
                    act.wait_ge(o_nt.sem, o_nt.now(g, b + 1))
                    act.wait_ge(wo.sem, wo.now(g, b) if b else wo.before(g, GB))
                    act.activation(oT[0], ps[:, 7, 0:256].rearrange("p (k t) -> p k t", k=K2), ACT.Copy
                                   ).then_inc(oT_hi.sem, 1)

                def tail_c(b):
                    act.wait_ge(x1t.sem, x1t.now(g, b + 1))
                    act.activation(xnT_all[0][:, :, bass.ds(g * GT + b * P, P)],
                                   ps[:, 7, 0:256].rearrange("p (k t) -> p k t", k=K2), ACT.Copy).then_inc(x1_hi.sem, 1)

                for u in range(UNITS):
                    if u >= 3 and u % 2:
                        tail_b(u // 2 - 1)
                    if u >= 4 and u % 2 == 0:
                        tail_c(u // 2 - 2)
                    act.wait_ge(sc_k.sem, sc_k.now(g, u + 1))
                    act.wait_ge(pv.sem, pv.now(g, u - 1) if u >= 2 else pv.before(g, UNITS - 1 + u))
                    act.activation(probs[u % 2], ps[:, 2 + 2 * (u % 2):4 + 2 * (u % 2), :].rearrange("p j (h q) -> p (j h) q", q=P),
                                   ACT.Exp, scale=DH ** -0.5).then_inc(ex.sem, 1)
                    if u >= 2 and u % 2 == 0:
                        tail_a(u // 2 - 1)
                tail_c(GB - 2)
                tail_a(GB - 1)
                tail_b(GB - 1)
                tail_c(GB - 1)

            act.wait_ge(pv.sem, pv.total(G))
            for n in range(G):
                act.wait_ge(lg, n + 1)
                act.activation(lgT[0:E, n * GT:(n + 1) * GT], ps[0:E, n, :], ACT.Copy).then_inc(lgc, 1)
            act.wait_ge(s_inh, 1)
            act.activation(rt[2], rt[1], ACT.Exp, scale=-1.0).then_inc(s_inh, 1)
            act.wait_ge(s_fb, 1)
            act.activation(rt[4], rt[3], ACT.Exp, scale=-1.0 / 0.1).then_inc(s_fb, 1)
            act.wait_ge(s_fb, 2)
            act.activation(rt[5], rt[3], ACT.Exp, scale=-1.0 / 0.3).then_inc(s_fb, 1)

            for s in (sl, hh):
                s.credit(act)
            with act.Fori(0, E // 2) as g:
                def high(i):
                    act.wait_ge(hm.sem, hm.now(g, i + 1))
                    c = i // 2
                    act.wait_ge(dn.sem, dn.now(g, c - 1) if c >= 2 else dn.before(g, NC2 - 1 + c))
                    act.activation(hT[c % 2][0][:, i % 2, :], gu_h[i % 2], ACT.Copy).then_inc(hh.sem, 1)
                for i in range(NH2):
                    act.wait_ge(gt.sem, gt.now(g, i + 1))
                    act.wait_ge(hm.sem, hm.now(g, i - 1) if i >= 2 else hm.before(g, NH2 - 1 + i))
                    act.activation(gu_s[i % 2], ps[:, i % 2, :], ACT.Silu).then_inc(sl.sem, 1)
                    if i:
                        high(i - 1)
                high(NH2 - 1)

            act.wait_ge(dn.sem, dn.total(E // 2))
            for s in (w4_hi, c3_hi, na_hi, nb_hi, k1_ok, q1_ok, e1, p1_ok, l1c, r1e):
                s.credit(act)
            def split(g, i, a):
                act.wait_ge(s_raw4[i], 32 * g + 32)
                if not isinstance(g, int) or (g, i) != (0, 0):
                    act.wait_ge(d4.sem, d4.before(g, i + 1))
                act.activation(w4[i][0][:, a, :], raw4[i][:, a, :], ACT.Copy).then_inc(w4_hi.sem, 1)

            def turn3(ga, gb):
                if ga is not None:
                    act.wait_ge(s_c3, ga * 16 + 16)
                    act.wait_ge(pv3.sem, pv3.before(ga, 2))
                    act.activation(cT[0], c_in, ACT.Copy).then_inc(c3_hi.sem, 1)
                if gb is not None:
                    act.wait_ge(t1.sem, t1.now(gb, 1))
                    act.wait_ge(a1.sem, a1.before(gb, 2))
                    act.activation(p1T, ps[:, 4, :].rearrange("p (b q) -> p b q", b=GB), ACT.Copy).then_inc(p1_ok.sem, 1)
                    if ga is None:
                        act.wait_ge(a1.sem, a1.total(G))
                        split(0, 0, 0)
                if ga is not None:
                    for m in range(2):
                        act.wait_ge(pk3.sem, pk3.now(ga, m + 1))
                        act.wait_ge(s1.sem, s1.before(ga, 1))
                        act.activation(k1[:, m, :], ps[:, m, :], ACT.Identity, bias=biasc[:, 6 + m:7 + m]).then_inc(k1_ok.sem, 1)
                if gb is not None:
                    for c in range(2):
                        act.wait_ge(nbt.sem, nbt.now(gb, 2 * c + 2))
                        act.wait_ge(l1.sem, l1.before(gb, 1))
                        act.activation(two_seqs(xnT_b[0], c), in_bank(6 + c), ACT.Copy).then_inc(nb_hi.sem, 1)
                if ga is not None:
                    for c in range(2):
                        act.wait_ge(nat.sem, nat.now(ga, 2 * c + 2))
                        act.wait_ge(pq3.sem, pq3.before(ga, 2))
                        act.activation(two_seqs(xnT[0], c), in_bank(c), ACT.Copy).then_inc(na_hi.sem, 1)
                if gb is not None:
                    act.wait_ge(l1.sem, l1.now(gb, 1))
                    act.wait_ge(l1t.sem, l1t.before(gb, 1))
                    act.activation(lg1T[0:E, :], ps[0:E, 5, :], ACT.Copy).then_inc(l1c.sem, 1)
                if ga is not None:
                    for m in range(2):
                        act.wait_ge(pq3.sem, pq3.now(ga, m + 1))
                        act.activation(q1[:, m, :], ps[:, 2 + m, :], ACT.Identity, bias=bq1s[:, m:m + 1], scale=1.0 / 16
                                       ).then_inc(q1_ok.sem, 1)
                if ga is not None:
                    act.wait_ge(m1.sem, m1.now(ga, 1))
                    act.wait_ge(x3.sem, x3.before(ga, GB))
                    for b in range(GB):
                        act.activation(sc1[:, b, :], sc1[:, b, :], ACT.Exp, bias=nmax[:, b:b + 1], accum_out=sum1[:, b:b + 1]
                                       ).then_inc(e1.sem, 1)
                if gb is not None:
                    act.wait_ge(ex1.sem, ex1.now(gb, 1))
                    act.activation(r3[3], r3[2], ACT.Exp).then_inc(r1e.sem, 1)
            turn3(0, None)
            with act.Fori(0, G - 1) as g:
                turn3(g + 1, g)
            turn3(None, G - 1)

            for s in (di_hi, h1_hi):
                s.credit(act)

            def slots_high(g, i):
                act.wait_ge(xd_t.sem, xd_t.now(g, i + 1))
                act.wait_ge(h1.sem, h1.before(g, 8 * i + 8))
                act.activation(slot_cols(diT[i][0]), in_bank(6 + i), ACT.Copy).then_inc(di_hi.sem, 1)

            def hidden(g, i, f):
                if f == 0:
                    act.wait_ge(d4.sem, d4.before(g, i + 1))
                act.wait_ge(h1.sem, h1.now(g, 8 * i + f + 1))
                act.activation(h4[i][0][:, f, :], ps[:, f % 4, 0:CAP], ACT.Relu).then_inc(h1_hi.sem, 1)

            def turn(g, last):
                for i in range(2):
                    nxt = (g, 1) if i == 0 else (g + 1, 0)
                    more = i == 0 or not last
                    for f in range(8):
                        hidden(g, i, f)
                        if more and f == 1:
                            split(*nxt, 0)
                    if more:
                        slots_high(*nxt)
                        split(*nxt, 1)
            split(0, 0, 1)
            slots_high(0, 0)
            with act.Fori(0, E // 2 - 1) as g:
                turn(g, False)
            turn(E // 2 - 1, True)

        @block.vector
        def _(dve):
            su = s_setup
            for s in (ln0, xt_lo, k_lo, v_ok, q_lo, q_m, mx_ok, o_n, oT_lo, x1, ln1, x1_lo, vs):
                s.credit(dve)
            wraw = work[:, fmark:fmark + 4 * K2 * D].rearrange("p (m k n) -> p m k n", m=4, k=K2)
            dve.wait_ge(s_const, 16)
            su.done(dve.tensor_scalar(neg_ident[:, :], ident, -1.0, None, ALU.mult))
            su.done(dve.tensor_copy(parity[:, 1:2], cst[:, C_ODD:C_ODD + 1]))
            su.done(dve.tensor_scalar(parity[:, 0:1], cst[:, C_ODD:C_ODD + 1], -1.0, 1.0, ALU.mult, ALU.add))
            su.done(dve.memset(ones_b[:, :], 1.0))
            su.done(dve.tensor_scalar(ones_r[:, :], ident, 0.0, 1.0, ALU.mult, ALU.add))
            su.done(dve.tensor_copy(tri_b[:, :], cst[:, C_TRI:C_TRI + P]))
            dve.wait_ge(s_wa_hi, 1)
            dve.tensor_tensor(wa[1][:, :, :, :], wraw, wa[0][:, :, :, :], ALU.subtract).then_inc(s_wa_lo, 1)
            dve.wait_ge(s_wa_lo, 1)
            su.done(dve.memset(v0, 0.0))
            dve.wait_ge(su.sem, su.last)
            su.done(dve.memset(v0[:, :, :, DH:DH + 1], 1.0))
            dve.wait_ge(s_tanh, 1)
            dve.wait_ge(s_small, 16 * 8)
            for i in range(2):
                su.done(dve.memset(wr[i].bitcast(F32), 0.0))
            su.done(dve.memset(fill[:, 0:ROW - 1], 0.0))
            dve.memset(fill[:, ROW - 1:ROW], float(2 * T)).then_inc(s_fill, 1)
            dve.wait_ge(su.sem, su.last)
            su.done(dve.tensor_copy(wr[0][:, :, :, 0:E], wr_raw))
            su.done(dve.memset(ones_before[:, :], 0.0))
            su.done(dve.tensor_copy(tokn[:, :], cst[:, C_TOK:C_TOK + 2 * GB]))
            su.done(dve.tensor_scalar(bq1s[:, :], biasc[:, 4:6], 1.0 / 16, None, ALU.mult))
            su.done(dve.reciprocal(scal[:, 5:6], scal[:, 4:5]))
            dve.wait_ge(su.sem, su.last)
            su.done(dve.tensor_tensor(wr[1][:, :, :, 0:E], wr_raw, wr[0][:, :, :, 0:E], ALU.subtract))
            dve.tensor_scalar(bo0r, bo0r, tgate[:, 0:1], None, ALU.mult).then_inc(s_bo, 1)
            dve.wait_ge(su.sem, su.last)
            with dve.Fori(0, G) as g:
                vs.last = 0

                def own(n=None):
                    dve.wait_ge(vs.sem, vs.now(g, vs.last if n is None else n))

                def x_of(b):
                    return x_all[:, bass.ds(g * GB + b, 1), 0:D].rearrange("p a d -> p (a d)")

                def step(ins):
                    vs.done(ins)
                    own()

                def statistics(n, b):
                    alone(dve)
                    step(dve.bn_stats(stats[:, n, :], x_of(b)))
                    alone(dve)
                    step(dve.bn_aggr(mv[:, n, :], stats[:, n, :]))

                def normalise(n, b, dst, sig):
                    dve.tensor_scalar(dst, x_of(b), mv[:, n, 0:1], rstd[:, n:n + 1], ALU.subtract, ALU.mult
                                      ).then_inc(sig.sem, 1)

                dve.wait_ge(s_x, g * 16 + 16)
                dve.wait_ge(ln1.sem, ln1.before(g, GB))
                for b in range(GB):
                    statistics(b, b)
                reciprocal_root(dve, step, mv[:, 0:GB, 1:2].rearrange("p n o -> p (n o)"), rstd[:, 0:GB], newton[:, 0:GB])
                for b in range(GB):
                    if b >= 2:
                        dve.wait_ge(xt_tr.sem, xt_tr.now(g, b - 1))
                    else:
                        dve.wait_ge(x1t.sem, x1t.before(g, GB - 1 + b))
                    normalise(b, b, xn[b % 2], ln0)
                for c in range(2):
                    dve.wait_ge(xt_hi.sem, xt_hi.now(g, c + 1))
                    dve.tensor_tensor(two_seqs(xnT[1], c), in_bank(6 + c), two_seqs(xnT[0], c), ALU.subtract
                                      ).then_inc(xt_lo.sem, 1)
                for m in range(2):
                    dve.wait_ge(k_hi.sem, k_hi.now(g, m + 1))
                    dve.scalar_tensor_tensor(kT[1][:, m, :], ps[:, m, :], biasc[:, 2 + m:3 + m], kT[0][:, m, :],
                                             ALU.add, ALU.subtract).then_inc(k_lo.sem, 1)
                for c in range(2):
                    dve.wait_ge(pj_v.sem, pj_v.now(g, c + 1))
                    dve.wait_ge(pv.sem, pv.before(g, UNITS))
                    for i in range(2):
                        dve.tensor_tensor(v0[:, 2 * c + i, :, 0:DH],
                                          ps[:, 2 + c, i * D:(i + 1) * D].rearrange("p (h d) -> p h d", d=DH),
                                          bv0r.rearrange("p (h d) -> p h d", d=DH), ALU.add).then_inc(v_ok.sem, 1)
                for m in range(2):
                    dve.wait_ge(q_hi.sem, q_hi.now(g, m + 1))
                    dve.scalar_tensor_tensor(qT[1][:, m, :], ps[:, 4 + m, :], biasc[:, m:m + 1], qT[0][:, m, :],
                                             ALU.add, ALU.subtract).then_inc(q_lo.sem, 1)
                    dve.wait_ge(sc_k.sem, sc_k.before(g, UNITS))
                    dve.wait_ge(q_lo.sem, q_lo.now(g, m + 1))
                    for i in range(2):
                        for r in range(2):
                            dve.tensor_scalar(qM[i][:, m, r, :], qT[i][:, m, :], parity[:, r:r + 1], None, ALU.mult
                                              ).then_inc(q_m.sem, 1)

                def tail_a(b):
                    o_ps = ps[:, 7, :].rearrange("p (h d) -> p h d", d=32)
                    dve.wait_ge(o_tr.sem, o_tr.now(g, b + 1))
                    vs.done(dve.reciprocal(rden[:, :].rearrange("p (h o) -> p h o", o=1), o_ps[:, :, DH:DH + 1]))
                    own()
                    dve.tensor_tensor(o_tok.rearrange("p (h d) -> p h d", d=DH), o_ps[:, :, 0:DH],
                                      rden[:, :].rearrange("p (h o) -> p h o", o=1).to_broadcast([P, H, DH]), ALU.mult
                                      ).then_inc(o_n.sem, 1)

                def tail_b(b):
                    dve.wait_ge(oT_hi.sem, oT_hi.now(g, b + 1))
                    dve.tensor_tensor(oT[1], ps[:, 7, 0:256].rearrange("p (k t) -> p k t", k=K2), oT[0], ALU.subtract
                                      ).then_inc(oT_lo.sem, 1)

                def tail_c(b):
                    dve.wait_ge(wo.sem, wo.now(g, b + 1))
                    dve.wait_ge(xb_ok.sem, xb_ok.now(g, b + 1))
                    dve.scalar_tensor_tensor(x_of(b), ps[:, 7, 256:512], tgate[:, 0:1], x_of(b), ALU.mult, ALU.add
                                             ).then_inc(x1.sem, 1)
                    dve.wait_ge(x1.sem, x1.now(g, b + 1))
                    statistics(GB + b, b)
                    reciprocal_root(dve, step, mv[:, GB + b, 1:2], rstd[:, GB + b:GB + b + 1], newton[:, GB + b:GB + b + 1])
                    if b >= 2:
                        dve.wait_ge(x1t.sem, x1t.now(g, b - 1))
                    else:
                        dve.wait_ge(xt_tr.sem, xt_tr.now(g, 3 + b))
                    normalise(GB + b, b, xn[b % 2], ln1)

                def tail_d(b):
                    dve.wait_ge(x1_hi.sem, x1_hi.now(g, b + 1))
                    dve.tensor_tensor(xnT_all[1][:, :, bass.ds(g * GT + b * P, P)],
                                      ps[:, 7, 0:256].rearrange("p (k t) -> p k t", k=K2),
                                      xnT_all[0][:, :, bass.ds(g * GT + b * P, P)], ALU.subtract).then_inc(x1_lo.sem, 1)

                for u in range(UNITS):
                    dve.wait_ge(sc_q.sem, sc_q.now(g, u + 1))
                    dve.wait_ge(dg.sem, dg.now(g, u - 1) if u >= 2 else dg.before(g, UNITS - 1 + u))
                    dve.tensor_reduce(mx[u % 2], ps[:, 0:2, :].rearrange("p j (h k) -> p (j h) k", k=P), AX.X, ALU.max
                                      ).then_inc(mx_ok.sem, 1)
                    if u >= 3 and u % 2:
                        tail_a(u // 2 - 1)
                        tail_b(u // 2 - 1)
                    if u >= 4 and u % 2 == 0:
                        tail_c(u // 2 - 2)
                        tail_d(u // 2 - 2)
                tail_c(GB - 2)
                tail_d(GB - 2)
                tail_a(GB - 1)
                tail_b(GB - 1)
                tail_c(GB - 1)
                tail_d(GB - 1)
                assert vs.last == vs.per, vs.last

            r = [t.rearrange("p (t e) -> p t e", e=E) for t in rt]
            rev = cst[:, C_REV:C_REV + P].rearrange("p (t e) -> p t e", e=E)

            def over_e(col):
                return col.rearrange("p (t o) -> p t o", o=1).to_broadcast([P, B, E])

            def seq(ins):
                dve.wait_ge(re_step.sem, re_step.done(ins))

            dve.wait_ge(lgt, 1)
            dve.tensor_scalar(rt[1], ps[:, 4, 0:P], scal[:, 5:6], -80.0, ALU.mult, ALU.max).then_inc(s_inh, 1)
            dve.wait_ge(s_inh, 2)
            seq(dve.tensor_scalar(rt[2], rt[2], 1.0, None, ALU.add))
            seq(dve.reciprocal(rt[2], rt[2]))
            seq(dve.tensor_scalar(rt[2], rt[2], -GOLD, None, ALU.add))
            dve.scalar_tensor_tensor(rt[3], rt[2], -1.0, rt[2], ALU.mult, ALU.max).then_inc(s_fb, 1)
            seq(dve.tensor_scalar(rt[6], rt[1], Z_LO, None, ALU.is_ge))
            seq(dve.scalar_tensor_tensor(rt[6], rt[1], 0.0, rt[6], ALU.is_le, ALU.mult))
            dve.wait_ge(s_fb, 3)
            seq(dve.tensor_tensor(rt[4], rt[4], rt[6], ALU.mult))
            seq(dve.tensor_reduce(rs[0], r[4], AX.X, ALU.add))
            seq(dve.tensor_scalar(rs[1], rs[0], 1e-8, None, ALU.is_lt))

            def first_of_max(src, dst):
                seq(dve.tensor_reduce(rs[2], src, AX.X, ALU.max))
                seq(dve.tensor_tensor(dst, src, over_e(rs[2]), ALU.is_equal))
                seq(dve.tensor_tensor(dst, dst, rev, ALU.mult))
                seq(dve.tensor_reduce(rs[3], dst, AX.X, ALU.max))
                seq(dve.tensor_tensor(dst, dst, over_e(rs[3]), ALU.is_equal))

            first_of_max(r[5], r[8])
            seq(dve.scalar_tensor_tensor(rt[1], rt[8], -4.0, rt[5], ALU.mult, ALU.add))
            first_of_max(r[1], r[7])
            seq(dve.tensor_tensor(rt[7], rt[7], rt[8], ALU.add))
            seq(dve.tensor_tensor(rt[7], rt[7], rt[5], ALU.mult))

            def divide_by_sum(t, i):
                seq(dve.tensor_reduce(rs[2], r[i], AX.X, ALU.add))
                seq(dve.tensor_scalar(rs[2], rs[2], 1e-8, None, ALU.max))
                seq(dve.reciprocal(rs[2], rs[2]))
                seq(dve.tensor_tensor(r[i], r[i], over_e(rs[2]), ALU.mult))

            divide_by_sum(rt[7], 7)
            seq(dve.tensor_tensor(r[7], r[7], over_e(rs[1]), ALU.mult))
            seq(dve.tensor_tensor(rt[4], rt[4], rt[7], ALU.add))
            divide_by_sum(rt[4], 4)
            dve.tensor_scalar(w_exp.rearrange("p e t -> p t e"), r[4], tgate[:, 2:3], None, ALU.mult).then_inc(s_wexp, 1)
            dve.wait_ge(s_wexp, 1)

            for s in (hm, hl, ac, wcur, as2):
                s.credit(dve)
            with dve.Fori(0, E // 2) as g:
                as2.last = 0

                def multiply(i):
                    dve.wait_ge(sl.sem, sl.now(g, i + 1))
                    dve.wait_ge(up.sem, up.now(g, i + 1))
                    dve.wait_ge(hl.sem, hl.now(g, i - 1) if i >= 2 else hl.before(g, NH2 - 1 + i))
                    dve.tensor_tensor(gu_h[i % 2], gu_s[i % 2], ps[:, 2 + i % 2, :], ALU.mult).then_inc(hm.sem, 1)

                def low(i):
                    dve.wait_ge(hh.sem, hh.now(g, i + 1))
                    dve.tensor_tensor(hT[i // 2 % 2][1][:, i % 2, :], gu_h[i % 2], hT[i // 2 % 2][0][:, i % 2, :],
                                      ALU.subtract).then_inc(hl.sem, 1)

                def accumulate(c):
                    e, n = c // 4, c % 4
                    if n == 0:
                        dve.wait_ge(ac.sem, ac.before(g, 4 * e + 4))
                        dve.tensor_copy(w_cur[e][:, :], w_exp[:, bass.ds(2 * g + e, 1), :].rearrange("p e t -> p (e t)")
                                        ).then_inc(wcur.sem, 1)
                        dve.wait_ge(wcur.sem, wcur.now(g, e + 1))
                    dve.wait_ge(dn.sem, dn.now(g, c + 1))
                    dve.wait_ge(ac.sem, ac.now(g, c - 3) if c >= 4 else ac.before(g, NC2 - 3 + c))
                    if as2.last:
                        dve.wait_ge(as2.sem, as2.now(g, as2.last))
                    for j in range(4):
                        t = 4 * n + j
                        ins = dve.scalar_tensor_tensor(x_all[:, t, 0:D], ps[:, 4 + 2 * (c % 2) + j // 2, (j % 2) * D:(j % 2 + 1) * D],
                                                       w_cur[e][:, t:t + 1], x_all[:, t, 0:D], ALU.mult, ALU.add)
                        if j < 3:
                            as2.done(ins)
                        else:
                            ins.then_inc(ac.sem, 1)

                for i in range(NH2):
                    if i == 0:
                        dve.wait_ge(as2.sem, as2.before(g, as2.per))
                    multiply(i)
                    if i:
                        low(i - 1)
                    if i >= 4 and i % 2 == 0:
                        accumulate(i // 2 - 2)
                low(NH2 - 1)
                accumulate(NC2 - 2)
                accumulate(NC2 - 1)
                assert as2.last == as2.per

            for s in (na, nb, na_lo, nb_lo, v1_ok, s1m, m1, x3, ex1, oh1, dest, dsa, dsb, dsr):
                s.credit(dve)
            dve.wait_ge(as2.sem, as2.total(E // 2))
            dve.wait_ge(ac.sem, ac.total(E // 2))
            def turn3(ga, gb):
                dsa.last = dsb.last = dsr.last = 0

                def seqa(ins):
                    dve.wait_ge(dsa.sem, dsa.now(ga, dsa.done(ins)))

                def seqb(ins):
                    dve.wait_ge(dsb.sem, dsb.now(gb, dsb.done(ins)))

                def seqr(ins):
                    dve.wait_ge(dsr.sem, dsr.now(ga if ga is not None else G, dsr.done(ins)))

                def x_of(g, b):
                    return x_all[:, bass.ds(g * GB + b, 1), 0:D].rearrange("p a d -> p (a d)")

                def moments(steps, g, half, rows):
                    for b in range(GB):
                        alone(dve)
                        steps.done(dve.bn_stats(st3[:, half * GB + b, :], rows(b)))
                    dve.wait_ge(steps.sem, steps.now(g, steps.last))
                    for b in range(GB):
                        alone(dve)
                        steps.done(dve.bn_aggr(mv3[:, half * GB + b, :], st3[:, half * GB + b, :]))
                    dve.wait_ge(steps.sem, steps.now(g, steps.last))

                def normalise(g, b, half, xn3, turned, sig):
                    n = half * GB + b
                    if b == 0:
                        dve.wait_ge(turned.sem, turned.before(g, GB))
                    dve.tensor_scalar(xn3[b], x_of(g, b), mv3[:, n, 0:1], rstd3[:, n:n + 1], ALU.subtract, ALU.mult
                                      ).then_inc(sig.sem, 1)

                if ga is not None:
                    dve.wait_ge(na.sem, na.before(ga, GB))
                    moments(dsa, ga, 0, lambda b: x_of(ga, b))
                if gb is not None:
                    dve.wait_ge(e1.sem, e1.now(gb, GB))
                    seqb(dve.reciprocal(gsc, sum1))
                    seqb(dve.tensor_scalar(gsc, gsc, tgate[:, 1:2], None, ALU.mult))
                    for b in range(GB):
                        dve.wait_ge(a1.sem, a1.now(gb, b // 2 + 1))
                        dve.scalar_tensor_tensor(x_of(gb, b), ps[:, 6 + b // 2, (b % 2) * D:(b % 2 + 1) * D], gsc[:, b:b + 1],
                                                 x_of(gb, b), ALU.mult, ALU.add).then_inc(x3.sem, 1)
                    dve.wait_ge(x3.sem, x3.now(gb, GB))
                    moments(dsb, gb, 1, lambda b: x_of(gb, b))
                sel = slice(0 if ga is not None else GB, 2 * GB if gb is not None else GB)
                reciprocal_root(dve, seqr, mv3[:, sel, 1:2].rearrange("p n o -> p (n o)"), rstd3[:, sel], newton3[:, sel])
                if gb is not None:
                    for b in range(GB):
                        normalise(gb, b, 1, xn_b, nbt, nb)
                if ga is not None:
                    for b in range(GB):
                        normalise(ga, b, 0, xn_a, nat, na)
                    for c in range(2):
                        dve.wait_ge(pv3.sem, pv3.now(ga, c + 1))
                        dve.wait_ge(a1.sem, a1.before(ga, 2))
                        dve.tensor_tensor(v1[:, 2 * c:2 * c + 2, :], ps[:, 2 + c, :].rearrange("p (b n) -> p b n", b=2),
                                          bv1r.rearrange("p (o n) -> p o n", o=1).to_broadcast([P, 2, D]), ALU.add
                                          ).then_inc(v1_ok.sem, 1)
                if gb is not None:
                    seqb(dve.tensor_copy(x_all[:, bass.ds(gb * GB, GB), D:D + 1], rstd3[:, GB:2 * GB].rearrange("p (b o) -> p b o", o=1)))
                    seqb(dve.scalar_tensor_tensor(x_all[:, bass.ds(gb * GB, GB), D + 1:D + 2], mv3[:, GB:2 * GB, 0:1], -1.0,
                                                  rstd3[:, GB:2 * GB].rearrange("p (b o) -> p b o", o=1), ALU.mult, ALU.mult))
                    seqb(dve.tensor_copy(x_all[:, bass.ds(gb * GB, GB), D + 3:D + 4], tokn[:, 0:GB].rearrange("p (b o) -> p b o", o=1)))
                    for c in range(2):
                        dve.wait_ge(nb_hi.sem, nb_hi.now(gb, c + 1))
                        dve.tensor_tensor(two_seqs(xnT_b[1], c), in_bank(6 + c), two_seqs(xnT_b[0], c), ALU.subtract
                                          ).then_inc(nb_lo.sem, 1)
                if ga is not None:
                    for c in range(2):
                        dve.wait_ge(na_hi.sem, na_hi.now(ga, c + 1))
                        dve.tensor_tensor(two_seqs(xnT[1], c), in_bank(c), two_seqs(xnT[0], c), ALU.subtract
                                          ).then_inc(na_lo.sem, 1)

                def mask_and_max():
                    dve.wait_ge(s1.sem, s1.now(ga, 1))
                    dve.wait_ge(s_m3, 16 * ga + 16)
                    dve.wait_ge(t1.sem, t1.before(ga, 1))
                    dve.scalar_tensor_tensor(sc1, mask, NEG, ps[:, 4, :].rearrange("p (b k) -> p b k", b=GB), ALU.mult, ALU.add
                                             ).then_inc(s1m.sem, 1)
                    dve.wait_ge(s1m.sem, s1m.now(ga, 1))
                    dve.wait_ge(e1.sem, e1.before(ga, GB))
                    seqa(dve.tensor_reduce(nmax, sc1, AX.X, ALU.max))
                    dve.tensor_scalar(nmax, nmax, -1.0, None, ALU.mult).then_inc(m1.sem, 1)

                lp = ps[:, 5, 0:GB * E].rearrange("p (b e) -> p b e", e=E)
                top, rank, gate, row, place, own = (r3s[i] for i in range(6))

                def over8(col):
                    return col.rearrange("p (t o) -> p t o", o=1).to_broadcast([P, GB, E])

                def pick_expert():
                    dve.wait_ge(l1t.sem, l1t.now(gb, 1))
                    seqb(dve.tensor_reduce(top, lp, AX.X, ALU.max))
                    seqb(dve.tensor_tensor(r3[0], lp, over8(top), ALU.is_equal))
                    seqb(dve.tensor_tensor(r3[0], r3[0], cst[:, C_REV:C_REV + GB * E].rearrange("p (b e) -> p b e", e=E), ALU.mult))
                    seqb(dve.tensor_reduce(rank, r3[0], AX.X, ALU.max))
                    dve.wait_ge(loc1.sem, loc1.before(gb, 1))
                    dve.tensor_tensor(r3[2], lp, over8(top), ALU.subtract).then_inc(ex1.sem, 1)
                    dve.wait_ge(ex1.sem, ex1.now(gb, 1))
                    dve.tensor_tensor(oh_b[:, :, :], r3[0], over8(rank), ALU.is_equal).then_inc(oh1.sem, 1)

                def pick_place():
                    dve.wait_ge(oh1.sem, oh1.now(gb, 1))
                    seqb(dve.tensor_reduce(counted[:, :], oh_b[:, :, :].rearrange("p b e -> p e b"), AX.X, ALU.add))
                    seqb(dve.tensor_scalar(own, tokn[:, GB:2 * GB], -1.0, float(E * CAP), ALU.mult, ALU.add))
                    seqb(dve.scalar_tensor_tensor(row, rank, -float(CAP), own, ALU.mult, ALU.add))
                    dve.wait_ge(r1e.sem, r1e.now(gb, 1))
                    seqb(dve.tensor_reduce(gate, r3[3], AX.X, ALU.add))
                    seqb(dve.reciprocal(gate, gate))
                    seqb(dve.tensor_scalar(x_all[:, bass.ds(gb * GB, GB), D + 2:D + 3], gate.rearrange("p (b o) -> p b o", o=1),
                                           tgate[:, 3:4], None, ALU.mult))
                    dve.wait_ge(loc1.sem, loc1.now(gb, 1))
                    seqb(dve.tensor_tensor(r3[1], ps[:, 5, GB * E:2 * GB * E].rearrange("p (b e) -> p b e", e=E), oh_b[:, :, :], ALU.mult))
                    seqb(dve.tensor_reduce(place, r3[1], AX.X, ALU.add))
                    seqb(dve.tensor_tensor(row, row, place, ALU.add))
                    seqb(dve.scalar_tensor_tensor(row, place, float(CAP), row, ALU.is_lt, ALU.mult))
                    dve.tensor_tensor(tok_idx[:, bass.ds(gb * GB, GB)], row, tokn[:, GB:2 * GB], ALU.add).then_inc(dest.sem, 1)
                    dve.wait_ge(dest.sem, dest.now(gb, 1))
                    seqb(dve.tensor_tensor(ones_before[:, :], ones_before[:, :], counted[:, :], ALU.add))
                    seqb(dve.tensor_scalar(tokn[:, :], tokn[:, :], float(GT), None, ALU.add))

                if ga is not None:
                    mask_and_max()
                if gb is not None:
                    pick_expert()
                    pick_place()
                assert dsa.last in (0, DSA) and dsb.last in (0, DSB) and dsr.last == RSQ, (dsa.last, dsb.last)
            turn3(0, None)
            with dve.Fori(0, G - 1) as g:
                turn3(g + 1, g)
            turn3(None, G - 1)

            for s in (xd_ok, di_lo, w4_l2, h1_lo, y4, ds4, idx4):
                s.credit(dve)

            def slots_norm(g, i):
                for j in range(2):
                    row = xs[:, bass.ds(4 * g + 2 * i + j, 1), :].rearrange("p a c -> p (a c)") if not isinstance(g, int) \
                        else xs[:, 4 * g + 2 * i + j, :]
                    dve.wait_ge(xd_t.sem, xd_t.now(g, 1) if i else xd_t.before(g, 2))
                    dve.tensor_scalar(xd[j], row[:, 0:D], row[:, D:D + 1], row[:, D + 1:D + 2], ALU.mult, ALU.add
                                      ).then_inc(xd_ok.sem, 1)

            def slots_low(g, i):
                dve.wait_ge(di_hi.sem, di_hi.now(g, i + 1))
                dve.tensor_tensor(slot_cols(diT[i][1]), in_bank(6 + i), slot_cols(diT[i][0]), ALU.subtract
                                  ).then_inc(di_lo.sem, 1)

            def split_w2(g, i):
                dve.wait_ge(w4_hi.sem, w4_hi.now(g, 2 * i + 2))
                dve.tensor_tensor(w4[i][1][:, 1, :], raw4[i][:, 1, :], w4[i][0][:, 1, :], ALU.subtract).then_inc(w4_l2.sem, 1)

            def hidden_low(g, i, f):
                dve.wait_ge(h1_hi.sem, h1_hi.now(g, 8 * i + f + 1))
                dve.scalar_tensor_tensor(h4[i][1][:, f, :], ps[:, f % 4, 0:CAP], 0.0, h4[i][0][:, f, :], ALU.max, ALU.subtract
                                         ).then_inc(h1_lo.sem, 1)

            def rows_out(g, i):
                dve.wait_ge(d4.sem, d4.now(g, i + 1))
                dve.wait_ge(out_left.sem, out_left.before(g, i + 1))
                t = 4 * g + 2 * i
                sel = slice(t, t + 2) if isinstance(g, int) else bass.ds(t, 2)
                dve.tensor_copy(out_idx[i][:, :].rearrange("p (a o) -> p a o", o=1), xs[:, sel, D + 3:D + 4]).then_inc(idx4.sem, 1)
                for j in range(2):
                    row = xs[:, t + j, :] if isinstance(g, int) else xs[:, bass.ds(t + j, 1), :].rearrange("p a c -> p (a c)")
                    ins = dve.scalar_tensor_tensor(yo[i][j], ps[:, 4 + i, j * D:(j + 1) * D], row[:, D + 2:D + 3],
                                                   row[:, 0:D], ALU.mult, ALU.add)
                    ins.then_inc(y4.sem if j else ds4.sem, 1)

            def turn(g, last):
                for i in range(2):
                    nxt = (g, 1) if i == 0 else (g + 1, 0)
                    more = i == 0 or not last
                    if more:
                        if i == 1:
                            dve.wait_ge(s_xs[1], 16)
                        slots_norm(*nxt)
                    for f in range(8):
                        hidden_low(g, i, f)
                    if more:
                        slots_low(*nxt)
                        split_w2(*nxt)
                    rows_out(g, i)
            split_w2(0, 0)
            dve.wait_ge(s_xs[0], 16)
            slots_norm(0, 0)
            slots_low(0, 0)
            with dve.Fori(0, E // 2 - 1) as g:
                turn(g, False)
            turn(E // 2 - 1, True)

        @block.tensor
        def _(pe):
            for s in (xt_tr, pj_k, pj_v, pj_q, sc_q, sc_k, pv, o_tr, o_nt, wo, x1t):
                s.credit(pe)
            THREE = ((0, 0), (0, 1), (1, 0))

            def product(dst, left, right, last_of=None):
                n = 0
                for k in range(K2):
                    for i, j in THREE:
                        mm = pe.matmul(dst, left(i, k), right(j, k), start=(n == 0), stop=(n == 3 * K2 - 1))
                        n += 1
                return mm

            pe.wait_ge(s_const, 16)
            pe.wait_ge(s_wa_hi, 1)
            pe.wait_ge(s_wa_lo, 1)
            with pe.Fori(0, G) as g:
                pe.wait_ge(c_hi.sem, c_hi.now(g, 1))
                pe.wait_ge(c_lo.sem, c_lo.now(g, 1))
                pe.wait_ge(mx_ok.sem, mx_ok.before(g, UNITS))
                for m in range(2):
                    product(ps[:, m, :], lambda i, k: wa[i][:, 1, k, m * P:(m + 1) * P], lambda j, k: cT[j][:, k, :]
                            ).then_inc(pj_k.sem, 1)
                pe.wait_ge(ex.sem, ex.before(g, UNITS))
                for c in range(2):
                    for i in range(2):
                        b = 2 * c + i
                        mm = product(ps[:, 2 + c, i * D:(i + 1) * D], lambda i, k: cT[i][:, k, b * P:(b + 1) * P],
                                     lambda j, k: wa[j][:, 2, k, :])
                    mm.then_inc(pj_v.sem, 1)
                for b in range(GB):
                    pe.wait_ge(ln0.sem, ln0.now(g, b + 1))
                    if b == 0:
                        pe.wait_ge(x1_lo.sem, x1_lo.before(g, GB))
                        pe.wait_ge(x1_hi.sem, x1_hi.before(g, GB))
                    for k in range(K2):
                        mm = pe.transpose(ps[:, 6 + b // 2, (b % 2) * 256 + k * P:(b % 2) * 256 + (k + 1) * P],
                                          xn[b % 2][:, k * P:(k + 1) * P], ident)
                    mm.then_inc(xt_tr.sem, 1)
                pe.wait_ge(xt_hi.sem, xt_hi.now(g, 2))
                pe.wait_ge(xt_lo.sem, xt_lo.now(g, 2))
                for m in range(2):
                    product(ps[:, 4 + m, :], lambda i, k: wa[i][:, 0, k, m * P:(m + 1) * P], lambda j, k: xnT[j][:, k, :]
                            ).then_inc(pj_q.sem, 1)

                def scores_for_max(u):
                    b, gp = u // 2, u % 2
                    if u == 0:
                        pe.wait_ge(k_m.sem, k_m.now(g, 2))
                        pe.wait_ge(k_lo.sem, k_lo.now(g, 2))
                        pe.wait_ge(q_hi.sem, q_hi.now(g, 2))
                    else:
                        pe.wait_ge(mx_ok.sem, mx_ok.now(g, u))
                    for m in range(2):
                        for j in range(2):
                            r = 32 * (2 * gp + j)
                            mm = pe.matmul(ps[:, j, m * 256:(m + 1) * 256], qT[0][r:r + 32, m, b * P:(b + 1) * P],
                                           kM[r:r + 32, m, :, b * P:(b + 1) * P], start=True, stop=True,
                                           skip_group_check=True)
                    mm.then_inc(sc_q.sem, 1)

                def scores_shifted(u):
                    b, gp, bank = u // 2, u % 2, 2 + 2 * (u % 2)
                    if u == 0:
                        pe.wait_ge(q_m.sem, q_m.now(g, 8))
                        pe.wait_ge(v_ok.sem, v_ok.now(g, 4))
                    if u == 1:
                        pe.wait_ge(q_lo.sem, q_lo.now(g, 2))
                    if u >= 2:
                        pe.wait_ge(ex.sem, ex.now(g, u - 1))
                    n = 0
                    for i, jj in THREE:
                        for m in range(2):
                            for j in range(2):
                                r = 32 * (2 * gp + j)
                                pe.matmul(ps[:, bank + j, m * 256:(m + 1) * 256], kT[i][r:r + 32, m, b * P:(b + 1) * P],
                                          qM[jj][r:r + 32, m, :, b * P:(b + 1) * P], start=(n < 2), stop=False,
                                          skip_group_check=True)
                                n += 1

                def shift(u):
                    bank = 2 + 2 * (u % 2)
                    pe.wait_ge(dg.sem, dg.now(g, u + 1))
                    for j in range(2):
                        mm = pe.matmul(ps[:, bank + j, :], ones_r[:, :], diag[u % 2][:, 4 * j:4 * j + 4, :],
                                       start=False, stop=True, skip_group_check=True)
                    mm.then_inc(sc_k.sem, 1)

                def values(u):
                    b, gp = u // 2, u % 2
                    pe.wait_ge(ex.sem, ex.now(g, u + 1))
                    if gp == 0:
                        if b == 0:
                            pe.wait_ge(o_raw.sem, o_raw.before(g, GB))
                        else:
                            pe.wait_ge(o_raw.sem, o_raw.now(g, b))
                    for j in range(2):
                        c = 2 * gp + j
                        for s in range(4):
                            h = (s // 2) * 8 + c * 2 + s % 2
                            mm = pe.matmul(ps[32 * s:32 * s + 32, 6, c * P:(c + 1) * P], v0[:, b, h, :],
                                           probs[u % 2][:, 4 * j + s, :], start=True, stop=True, skip_group_check=True)
                    mm.then_inc(pv.sem, 1)

                def tail(b, step):
                    if step == 0:
                        pe.wait_ge(o_raw.sem, o_raw.now(g, b + 1))
                        pe.wait_ge(x1_lo.sem, x1_lo.now(g, b) if b else x1_lo.before(g, GB))
                        if b == 0:
                            pe.wait_ge(xt_lo.sem, xt_lo.now(g, 2))
                        for c in range(4):
                            mm = pe.transpose(ps[:, 7, c * P:(c + 1) * P], oT_raw[:, c, :], ident)
                        mm.then_inc(o_tr.sem, 1)
                    if step == 1:
                        pe.wait_ge(o_n.sem, o_n.now(g, b + 1))
                        for k in range(K2):
                            mm = pe.transpose(ps[:, 7, k * P:(k + 1) * P], o_tok[:, k * P:(k + 1) * P], ident)
                        mm.then_inc(o_nt.sem, 1)
                    if step == 2:
                        pe.wait_ge(oT_hi.sem, oT_hi.now(g, b + 1))
                        pe.wait_ge(oT_lo.sem, oT_lo.now(g, b + 1))
                        product(ps[:, 7, 256:512], lambda i, k: oT[i][:, k, :], lambda j, k: wa[j][:, 3, k, :]
                                ).then_inc(wo.sem, 1)
                    if step == 3:
                        pe.wait_ge(ln1.sem, ln1.now(g, b + 1))
                        for k in range(K2):
                            mm = pe.transpose(ps[:, 7, k * P:(k + 1) * P], xn[b % 2][:, k * P:(k + 1) * P], ident)
                        mm.then_inc(x1t.sem, 1)

                steps = []
                scores_for_max(0)
                for u in range(UNITS):
                    if u + 1 < UNITS:
                        scores_for_max(u + 1)
                    if steps:
                        tail(*steps.pop(0))
                    scores_shifted(u)
                    if steps:
                        tail(*steps.pop(0))
                    shift(u)
                    if u >= 1:
                        values(u - 1)
                        if u % 2 == 0:
                            steps += [(u // 2 - 1, i) for i in range(4)]
                values(UNITS - 1)
                steps += [(GB - 1, i) for i in range(4)]
                for s in steps:
                    tail(*s)

            pe.wait_ge(mx_ok.sem, mx_ok.total(G))
            pe.wait_ge(ex.sem, ex.total(G))
            pe.wait_ge(x1_lo.sem, x1_lo.total(G))
            for n in range(G):
                product(ps[:, n, :], lambda i, k: wr[i][:, 0, k, :], lambda j, k: xnT_all[j][:, k, n * GT:(n + 1) * GT]
                        ).then_inc(lg, 1)
            pe.wait_ge(lgc, G)
            for t in range(B):
                mm = pe.transpose(ps[:, 4, t * E:(t + 1) * E], lgT[0:E, t * P:(t + 1) * P], ident[0:E, 0:E])
            mm.then_inc(lgt, 1)
            pe.wait_ge(s_inh, 1)

            for s in (gt, up, dn):
                s.credit(pe)
            with pe.Fori(0, E // 2) as g:
                def gate_up(i):
                    e, n, m = i // 8, i // 2 % 4, i % 2
                    if i % 8 == 0:
                        pe.wait_ge(w2_hi.sem, w2_hi.now(g, e + 1))
                        pe.wait_ge(w2_lo.sem, w2_lo.now(g, e + 1))
                    for bank, at0, prior, done in ((0, 0, sl, gt), (2, 2 * I0, hm, up)):
                        pe.wait_ge(prior.sem, prior.now(g, i - 1) if i >= 2 else prior.before(g, NH2 - 1 + i))
                        product(ps[:, bank + i % 2, :],
                                lambda a, k: w2s[e][a][:, at0 + k * I0 + m * P:at0 + k * I0 + (m + 1) * P],
                                lambda b, k: xnT_all[b][:, k, n * GT:(n + 1) * GT]).then_inc(done.sem, 1)

                def down(c):
                    e = c // 4
                    pe.wait_ge(hh.sem, hh.now(g, 2 * c + 2))
                    pe.wait_ge(hl.sem, hl.now(g, 2 * c + 2))
                    pe.wait_ge(ac.sem, ac.now(g, c - 1) if c >= 2 else ac.before(g, NC2 - 1 + c))
                    for j in range(4):
                        mm = product(ps[:, 4 + 2 * (c % 2) + j // 2, (j % 2) * D:(j % 2 + 1) * D],
                                     lambda a, k: hT[c % 2][a][:, k, j * P:(j + 1) * P],
                                     lambda b, k: w2s[e][b][:, 4 * I0 + k * D:4 * I0 + (k + 1) * D])
                    mm.then_inc(dn.sem, 1)

                for c in range(NC2):
                    gate_up(2 * c)
                    gate_up(2 * c + 1)
                    if c:
                        down(c - 1)
                down(NC2 - 1)

            for s in (nat, nbt, pk3, pv3, pq3, s1, t1, a1, l1, l1t, loc1):
                s.credit(pe)
            pe.wait_ge(ac.sem, ac.total(E // 2))
            pe.wait_ge(s_wa1_lo, 1)
            def turn3(ga, gb):
                def transposes3(g, b, xn3, bank, sig, done):
                    pe.wait_ge(sig.sem, sig.now(g, b + 1))
                    for k in range(K2):
                        mm = pe.transpose(ps[:, bank + b // 2, (b % 2) * 256 + k * P:(b % 2) * 256 + (k + 1) * P],
                                          xn3[b][:, k * P:(k + 1) * P], ident)
                    mm.then_inc(done.sem, 1)

                if gb is not None:
                    for b in range(GB):
                        pe.wait_ge(e1.sem, e1.now(gb, b + 1))
                        mm = pe.transpose(ps[:, 4, b * P:(b + 1) * P], sc1[:, b, :], ident)
                    mm.then_inc(t1.sem, 1)
                if gb is not None:
                    pe.wait_ge(p1_ok.sem, p1_ok.now(gb, 1))
                    pe.wait_ge(v1_ok.sem, v1_ok.now(gb, 2))
                    pe.wait_ge(nb_hi.sem, nb_hi.before(gb, 2))
                    pe.wait_ge(nb_lo.sem, nb_lo.before(gb, 2))
                    for b in range(GB):
                        mm = pe.matmul(ps[:, 6 + b // 2, (b % 2) * D:(b % 2 + 1) * D], p1T[:, b, :], v1[:, b, :], start=True, stop=True)
                        if b % 2:
                            mm.then_inc(a1.sem, 1)
                if ga is not None:
                    pe.wait_ge(c3_hi.sem, c3_hi.now(ga, 1))
                    pe.wait_ge(c3_lo.sem, c3_lo.now(ga, 1))
                    pe.wait_ge(na_hi.sem, na_hi.before(ga, 2))
                    pe.wait_ge(na_lo.sem, na_lo.before(ga, 2))
                    for m in range(2):
                        product(ps[:, m, :], lambda i, k: wa[i][:, 1, k, m * P:(m + 1) * P], lambda j, k: cT[j][:, k, :]
                                ).then_inc(pk3.sem, 1)
                    pe.wait_ge(q1_ok.sem, q1_ok.before(ga, 2))
                    for c in range(2):
                        for i in range(2):
                            b = 2 * c + i
                            mm = product(ps[:, 2 + c, i * D:(i + 1) * D], lambda i, k: cT[i][:, k, b * P:(b + 1) * P],
                                         lambda j, k: wa[j][:, 2, k, :])
                        mm.then_inc(pv3.sem, 1)
                if gb is not None:
                    for b in range(GB):
                        transposes3(gb, b, xn_b, 6, nb, nbt)
                if ga is not None:
                    pe.wait_ge(k1_ok.sem, k1_ok.now(ga, 2))
                    for b in range(GB):
                        transposes3(ga, b, xn_a, 0, na, nat)
                if gb is not None:
                    pe.wait_ge(nb_hi.sem, nb_hi.now(gb, 2))
                    pe.wait_ge(nb_lo.sem, nb_lo.now(gb, 2))
                    pe.wait_ge(dest.sem, dest.before(gb, 1))
                    product(ps[:, 5, :], lambda i, k: wr[i][:, 1, k, :], lambda j, k: xnT_b[j][:, k, :]).then_inc(l1.sem, 1)
                if ga is not None:
                    pe.wait_ge(na_hi.sem, na_hi.now(ga, 2))
                    pe.wait_ge(na_lo.sem, na_lo.now(ga, 2))
                    pe.wait_ge(v1_ok.sem, v1_ok.now(ga, 2))
                    for m in range(2):
                        product(ps[:, 2 + m, :], lambda i, k: wa[i][:, 0, k, m * P:(m + 1) * P], lambda j, k: xnT[j][:, k, :]
                                ).then_inc(pq3.sem, 1)
                if gb is not None:
                    pe.wait_ge(l1c.sem, l1c.now(gb, 1))
                    alone(pe)
                    for b in range(GB):
                        mm = pe.transpose(ps[:, 5, b * E:(b + 1) * E], lg1T[0:E, b * P:(b + 1) * P], ident[0:E, 0:E])
                    mm.then_inc(l1t.sem, 1)
                if ga is not None:
                    pe.wait_ge(q1_ok.sem, q1_ok.now(ga, 2))
                    pe.wait_ge(p1_ok.sem, p1_ok.before(ga, 1))
                    for b in range(GB):
                        for k in range(2):
                            mm = pe.matmul(ps[:, 4, b * P:(b + 1) * P], q1[:, k, b * P:(b + 1) * P], k1[:, k, b * P:(b + 1) * P],
                                           start=(k == 0), stop=(k == 1))
                    mm.then_inc(s1.sem, 1)
                if gb is not None:
                    pe.wait_ge(oh1.sem, oh1.now(gb, 1))
                    place = ps[:, 5, GB * E:2 * GB * E].rearrange("p (b e) -> p b e", e=E)
                    pe.matmul(place, tri_b[:, :], oh_b[:, :, :], start=True, stop=False)
                    for b in range(GB - 1):
                        pe.matmul(place[:, b + 1:GB, :], ones_b[:, :], oh_b[:, b:b + 1, :].to_broadcast([P, GB - 1 - b, E]),
                                  start=False, stop=False, skip_group_check=True)
                    pe.matmul(place, ones_b[:, :], ones_before[:, :].rearrange("p (o e) -> p o e", o=1).to_broadcast([P, GB, E]),
                              start=False, stop=True).then_inc(loc1.sem, 1)
            turn3(0, None)
            with pe.Fori(0, G - 1) as g:
                turn3(g + 1, g)
            turn3(None, G - 1)

            for s in (xd_t, h1, d4):
                s.credit(pe)

            def slots_transposed(g, i):
                pe.wait_ge(xd_ok.sem, xd_ok.now(g, 2 * i + 2))
                pe.wait_ge(di_lo.sem, di_lo.before(g, i + 1))
                for j in range(2):
                    for k in range(K2):
                        mm = pe.transpose(ps[:, 6 + i, j * 256 + k * P:j * 256 + (k + 1) * P], xd[j][:, k * P:(k + 1) * P], ident)
                mm.then_inc(xd_t.sem, 1)

            def hidden(g, i, f):
                n = 8 * i + f
                if f == 0:
                    pe.wait_ge(di_hi.sem, di_hi.now(g, i + 1))
                    pe.wait_ge(di_lo.sem, di_lo.now(g, i + 1))
                    pe.wait_ge(w4_hi.sem, w4_hi.now(g, 2 * i + 1))
                    pe.wait_ge(w4_l1.sem, w4_l1.now(g, i + 1))
                pe.wait_ge(h1_lo.sem, h1_lo.now(g, n - 3) if n >= 4 else h1_lo.before(g, 16 - 3 + n))
                product(ps[:, f % 4, 0:CAP], lambda a, k: w4[i][a][:, 0, k * F1 + f * P:k * F1 + (f + 1) * P],
                        lambda b, k: diT[i][b][:, k, :]).then_inc(h1.sem, 1)

            def down4(g, i):
                pe.wait_ge(w4_hi.sem, w4_hi.now(g, 2 * i + 2))
                pe.wait_ge(w4_l2.sem, w4_l2.now(g, i + 1))
                pe.wait_ge(y4.sem, y4.before(g, i + 1))
                for j in range(2):
                    for f in range(8):
                        if j == 0:
                            pe.wait_ge(h1_lo.sem, h1_lo.now(g, 8 * i + f + 1))
                        for n, (a, b) in enumerate(THREE):
                            mm = pe.matmul(ps[:, 4 + i, j * D:(j + 1) * D], h4[i][a][:, f, j * P:(j + 1) * P],
                                           w4[i][b][:, 1, f * D:(f + 1) * D], start=(f == 0 and n == 0), stop=(f == 7 and n == 2))
                mm.then_inc(d4.sem, 1)

            def turn(g, last):
                for i in range(2):
                    for f in range(8):
                        hidden(g, i, f)
                    if i == 0 or not last:
                        slots_transposed(*((g, 1) if i == 0 else (g + 1, 0)))
                    down4(g, i)
            slots_transposed(0, 0)
            with pe.Fori(0, E // 2 - 1) as g:
                turn(g, False)
            turn(E // 2 - 1, True)

        @block.gpsimd
        def _(pool):
            for s in (c_lo, k_m, dg, xb_ok, w2q_hi, w2q_lo, w2_hi, w2_lo, c3_lo, w4_l1, out_left):
                s.credit(pool)
            pool.wait_ge(s_fill, 1)
            pool.dma_start(slots[0:T, :].rearrange("(t p) c -> p t c", p=P),
                           fill[:, :].rearrange("p (o c) -> p o c", o=1).to_broadcast([P, T // P, ROW])).then_inc(s_disp, 16)
            pool.wait_ge(s_bo, 1)
            pool.wait_ge(s_setup.sem, s_setup.last)
            for i in range(2):
                pool.wait_ge(s_raw2[i], 16)
            with pool.Fori(0, G) as g:
                pool.wait_ge(c_hi.sem, c_hi.now(g, 1))
                pool.tensor_tensor(cT[1], c_in, cT[0], ALU.subtract).then_inc(c_lo.sem, 1)
                quarter = bass.ds(g * (W2C // 2), W2C // 2)
                pool.tensor_copy(w2_both[0][:, quarter], raw_both[:, quarter]).then_inc(w2q_hi.sem, 1)
                for m in range(2):
                    pool.wait_ge(k_hi.sem, k_hi.now(g, m + 1))
                    pool.tensor_tensor(kM[:, m, :, :], kT[0][:, m:m + 1, :].to_broadcast([P, 2, GT]),
                                       parity[:, :].rearrange("p (r o) -> p r o", o=1).to_broadcast([P, 2, GT]), ALU.mult
                                       ).then_inc(k_m.sem, 1)
                pool.wait_ge(w2q_hi.sem, w2q_hi.now(g, 1))
                alone(pool)
                pool.tensor_tensor(w2_both[1][:, quarter], raw_both[:, quarter], w2_both[0][:, quarter], ALU.subtract
                                   ).then_inc(w2q_lo.sem, 1)
                for u in range(UNITS):
                    pool.wait_ge(mx_ok.sem, mx_ok.now(g, u + 1))
                    pool.wait_ge(sc_k.sem, sc_k.now(g, u - 1) if u >= 2 else sc_k.before(g, UNITS - 1 + u))
                    pool.tensor_tensor(diag[u % 2], neg_ident[:, :].rearrange("p (o q) -> p o q", o=1).to_broadcast([P, 8, P]),
                                       mx[u % 2].rearrange("p (h o) -> p h o", o=1).to_broadcast([P, 8, P]), ALU.mult
                                       ).then_inc(dg.sem, 1)
                    if u % 2:
                        b = u // 2
                        pool.wait_ge(ln0.sem, ln0.now(g, b + 1))
                        alone(pool)
                        xo = x_all[:, bass.ds(g * GB + b, 1), 0:D].rearrange("p a d -> p (a d)")
                        pool.tensor_tensor(xo, xo, bo0r, ALU.add).then_inc(xb_ok.sem, 1)
            pool.wait_ge(w2q_lo.sem, w2q_lo.total(G))
            pool.sem_inc(w2_hi.sem, 2)
            pool.sem_inc(w2_lo.sem, 2)
            with pool.Fori(1, E // 2) as g:
                for i in range(2):
                    pool.wait_ge(s_raw2[i], 16 * g + 16)
                    pool.wait_ge(dn.sem, dn.before(g, 4 * i + 4))
                    alone(pool)
                    pool.tensor_copy(w2s[i][0], raw[i]).then_inc(w2_hi.sem, 1)
                    pool.wait_ge(w2_hi.sem, w2_hi.now(g, i + 1))
                    pool.tensor_tensor(w2s[i][1], raw[i], w2s[i][0], ALU.subtract).then_inc(w2_lo.sem, 1)
            pool.wait_ge(s_wa1, 16)
            pool.wait_ge(wo.sem, wo.total(G))
            pool.tensor_copy(wa[0][:, 0:3, :, :], wa1_raw).then_inc(s_wa1_hi, 1)
            pool.wait_ge(s_wa1_hi, 1)
            pool.tensor_tensor(wa[1][:, 0:3, :, :], wa1_raw, wa[0][:, 0:3, :, :], ALU.subtract).then_inc(s_wa1_lo, 1)
            def split_w1(g, i):
                pool.wait_ge(w4_hi.sem, w4_hi.now(g, 2 * i + 1))
                pool.tensor_tensor(w4[i][1][:, 0, :], raw4[i][:, 0, :], w4[i][0][:, 0, :], ALU.subtract).then_inc(w4_l1.sem, 1)

            def ctx_low(g):
                pool.wait_ge(c3_hi.sem, c3_hi.now(g, 1))
                pool.tensor_tensor(cT[1], c_in, cT[0], ALU.subtract).then_inc(c3_lo.sem, 1)

            def dispatch(g):
                pool.wait_ge(dest.sem, dest.now(g, 1))
                for t in range(g * GB, g * GB + GB):
                    pool.indirect_dma_start(out=slots[:, :], out_offset=bass.IndirectOffsetOnAxis(ap=tok_idx[:, t:t + 1], axis=0),
                                            in_=x_all[:, t, :], in_offset=None).then_inc(s_disp, 16)
            ctx_low(0)
            pool.wait_ge(s_disp, 16)
            for g in range(1, G):
                ctx_low(g)
                if g >= 2:
                    dispatch(g - 2)
            dispatch(G - 2)
            split_w1(0, 0)
            dispatch(G - 1)

            def scatter(g, i):
                pool.wait_ge(y4.sem, y4.now(g, i + 1))
                pool.wait_ge(ds4.sem, ds4.now(g, i + 1))
                pool.wait_ge(idx4.sem, idx4.now(g, i + 1))
                alone(pool)
                for j in range(2):
                    pool.indirect_dma_start(out=out.rearrange("b s d -> (b s) d"),
                                            out_offset=bass.IndirectOffsetOnAxis(ap=out_idx[i][:, j:j + 1], axis=0),
                                            in_=yo[i][j], in_offset=None, bounds_check=T - 1, oob_is_err=False
                                            ).then_inc(s_sc[i], 16)

            def rows_have_left(g, i):
                pool.wait_ge(s_sc[i], 32 * g + 32)
                alone(pool)
                pool.sem_inc(out_left.sem, 1)

            def turn(g, last):
                for i in range(2):
                    scatter(g, i)
                    if not last:
                        split_w1(g + 1, i)
                    rows_have_left(g, i)
            split_w1(0, 1)
            with pool.Fori(0, E // 2 - 1) as g:
                turn(g, False)
            turn(E // 2 - 1, True)
            for i in range(2):
                pool.wait_ge(s_sc[i], 32 * (E // 2))


def layout(inputs):
    a = {k: np.asarray(v) for k, v in inputs.items()}
    rows = np.arange(D).reshape(2, 4, 2, DH).transpose(1, 0, 2, 3).reshape(-1)
    return {
        "x": a["x"], "ctxT": np.ascontiguousarray(a["ctx_1024"].reshape(T, D).T), "maskf": a["mask_BxSxS2_fk0"],
        "gx": a["g_xattn"], "gf": a["g_ffn"],
        "wa0": np.stack([a["L0_xattn_Wq"].T, a["L0_xattn_Wk"].T, a["L0_xattn_Wv"].T, a["L0_xattn_Wo"].T[rows]]),
        "bcols": np.concatenate([a[n].reshape(2, P).T for n in ("L0_xattn_bq", "L0_xattn_bk", "L1_xattn_bq", "L1_xattn_bk")], axis=1),
        "bv0": a["L0_xattn_bv"], "bo0": a["L0_xattn_bo"],
        "w0": np.concatenate([a[f"L0_ffn_{n}"].reshape(E, K2, P, 256).transpose(0, 2, 1, 3).reshape(E, P, 512)
                              for n in ("Wg", "Wu", "Wd")], axis=2),
        "wrs": np.stack([a["L0_ffn_Wr"], a["L1_ffn_wg"]]), "temp": a["L0_ffn_temperature"],
        "wa1": np.stack([a["L1_xattn_Wq"], a["L1_xattn_Wk"], a["L1_xattn_Wv"]]),
        "bv1": a["L1_xattn_bv"],
        "w1": a["L1_ffn_w1"], "w2": a["L1_ffn_w2"], "const": constants(),
    }


def kernel(**inputs):
    from concourse import bacc
    from concourse.bass_utils import run_bass_kernel_spmd

    nc = bacc.Bacc("TRN2", target_bir_lowering=False, num_devices=1)
    arrays, args = {}, []
    for name, a in layout(inputs).items():
        a = np.ascontiguousarray(a)
        arrays[f"in_{name}"] = a
        args.append(nc.dram_tensor(f"in_{name}", a.shape, mybir.dt.from_np(a.dtype), kind="ExternalInput").ap())
    out = nc.dram_tensor("out", (B, S, D), F32, kind="ExternalOutput").ap()
    slots = nc.dram_tensor("slots", (2 * T, ROW), F32, kind="Internal").ap()
    block_kernel(nc, *args, out, slots)
    r = run_bass_kernel_spmd(nc, [arrays], core_ids=[0])
    return r.results[0]["out"]
```

```python
import math
from contextlib import ExitStack

import numpy as np

import concourse.bass as bass
from concourse import mybir

ALU = mybir.AluOpType
ACT = mybir.ActivationFunctionType
AX = mybir.AxisListType
F32 = mybir.dt.float32
F32R = mybir.dt.float32r
BF16 = mybir.dt.bfloat16
I32 = mybir.dt.int32

P = 128
B, S, D = 16, 128, 256
K2 = D // P
H, DH = 16, 16
T = B * S
GB = 4
G = B // GB
GT = GB * S
UNITS = 2 * GB
E = 8
I0 = 256
W2C = 6 * I0
F1 = 1024
CAP = T // E
ROW = D + 4
EPS = 1e-5
ARENA = 34304
RSQ = 11
VS0, VS1 = 2 * GB + RSQ, (2 + RSQ + 1) * GB
DSA, DSB = 2 * GB + RSQ, 29 + RSQ
GOLD = 1.0 / math.e
GOLD_LO = 0.5 - math.log(4.0 / 3.0)
Z_LO = math.log(GOLD_LO / (1.0 - GOLD_LO))
NEG = -1000000000.0
HIDDEN = -float(2 ** 40)
C_ID, C_TRI, C_ODD, C_IDX, C_REV, C_TOK, C_OWN = 0, 128, 256, 257, 257 + 128, 257 + 256, 257 + 260
C_N = 257 + 264


def constants():
    p = np.arange(P)
    c = np.zeros((P, C_N), np.float32)
    c[:, C_ID:C_ID + P] = np.eye(P)
    c[:, C_TRI:C_TRI + P] = p[:, None] < p[None, :]
    c[:, C_ODD] = (p // DH) % 2
    c[:, C_IDX:C_IDX + P] = np.tile(np.arange(E), P // E)
    c[:, C_REV:C_REV + P] = E - np.tile(np.arange(E), P // E)
    c[:, C_TOK:C_TOK + GB] = p[:, None] + S * np.arange(GB)
    c[:, C_OWN:C_OWN + GB] = T + p[:, None] + S * np.arange(GB)
    return c


class Signal:

    def __init__(self, sem, per):
        self.sem, self.per = sem, per

    def credit(self, eng):
        eng.sem_inc(self.sem, self.per)

    def now(self, g, n):
        return g * self.per + (self.per + n)

    def before(self, g, n):
        return g * self.per + n

    def total(self, turns):
        return (turns + 1) * self.per


class Steps(Signal):

    def __init__(self, sem, per):
        super().__init__(sem, per)
        self.last = 0

    def done(self, ins):
        ins.then_inc(self.sem, 1)
        self.last += 1
        return self.last


def block_kernel(nc, x, ctxT, maskf, mask0, gx, gf, wa0, bcols, bv0, bo0, w0, wrs, temp, wa1, bv1,
                 w1, w2, const, out, slots):
    with ExitStack() as ctx:
        def sem(name):
            return ctx.enter_context(nc.semaphore(name))

        def sb(name, cols, dt=F32):
            return ctx.enter_context(nc.sbuf_tensor(name, [P, cols], dt))

        psum = ctx.enter_context(nc.psum_tensor("psum", [P, 8, 512], F32))

        x_all = sb("x_all", B * ROW).rearrange("p (t c) -> p t c", c=ROW)
        cst = sb("cst", C_N)
        ident = cst[:, C_ID:C_ID + P]
        neg_ident = sb("neg_ident", P)
        parity = sb("parity", 2)
        ones_r = sb("ones_r", P, F32R)
        ones_b = sb("ones_b", P, BF16)
        tri_b = sb("tri_b", P, BF16)
        ident_b = sb("ident_b", P, BF16)
        hide = sb("hide", 2 * P, BF16).rearrange("p (a n) -> p a n", a=2)
        biasc = sb("biasc", 8)
        biasr = sb("biasr", 3 * D)
        bv0r, bo0r, bv1r = (biasr[:, i * D:(i + 1) * D] for i in range(3))
        scal = sb("scal", 8)
        scratch = sb("scratch", 2 * GB)
        wr_raw = sb("wr_raw", 2 * K2 * E).rearrange("p (l k n) -> p l k n", l=2, k=K2)
        fill = sb("fill", ROW)
        bq1s = sb("bq1s", 2)
        w_exp = sb("w_exp", E * B).rearrange("p (e t) -> p e t", e=E)
        w_cur = [sb(f"w_cur{i}", B) for i in range(2)]
        tgate = sb("tgate", 4)
        arena = sb("arena", ARENA, F32R)
        at = [0]

        def cut(cols):
            at[0] += cols
            assert at[0] <= ARENA
            return arena[:, at[0] - cols:at[0]]

        def pair(cols):
            return cut(cols), cut(cols)

        wa = pair(4 * K2 * D)
        wa = [w.rearrange("p (m k n) -> p m k n", m=4, k=K2) for w in wa]
        xnT_all = [w.rearrange("p (k t) -> p k t", k=K2) for w in pair(K2 * T)]
        w2_both = pair(2 * W2C)
        w2s = [[w[:, i * W2C:(i + 1) * W2C] for w in w2_both] for i in range(2)]
        wr = [w.rearrange("p (l k n) -> p l k n", l=2, k=K2) for w in pair(2 * K2 * P)]
        cT = [w.rearrange("p (k t) -> p k t", k=K2) for w in pair(K2 * GT)]
        xnT = [w.rearrange("p (k t) -> p k t", k=K2) for w in pair(K2 * GT)]
        kT_at = at[0]
        kT = [w.rearrange("p (m t) -> p m t", m=2) for w in pair(2 * GT)]
        kM = cut(4 * GT).rearrange("p (m r t) -> p m r t", m=2, r=2)
        qT = [w.rearrange("p (m t) -> p m t", m=2) for w in pair(2 * GT)]
        qM_at = at[0]
        qM = [w.rearrange("p (m r t) -> p m r t", m=2, r=2) for w in pair(4 * GT)]
        oT = [w.rearrange("p (k t) -> p k t", k=K2) for w in pair(K2 * P)]
        at[0] = kT_at
        xnT_b = [w.rearrange("p (k t) -> p k t", k=K2) for w in pair(K2 * GT)]
        at[0] = qM_at
        hT = [[w.rearrange("p (k t) -> p k t", k=2) for w in pair(2 * GT)] for _ in range(2)]
        at[0] = 0
        w4 = [[w.rearrange("p (a n) -> p a n", a=2) for w in pair(2 * 2048)] for _ in range(2)]
        diT = [[w.rearrange("p (k c) -> p k c", k=K2) for w in pair(K2 * CAP)] for _ in range(2)]
        h4 = [[w.rearrange("p (f c) -> p f c", f=8) for w in pair(8 * CAP)] for _ in range(2)]

        diag = [sb(f"diag{i}", 8 * P, F32R).rearrange("p (h q) -> p h q", h=8) for i in range(2)]

        work = sb("work", 9728)
        wat = [0]

        def fcut(cols):
            wat[0] += cols
            assert wat[0] <= 9728, wat
            return work[:, wat[0] - cols:wat[0]]

        raw_both = fcut(2 * W2C)
        raw = [raw_both[:, i * W2C:(i + 1) * W2C] for i in range(2)]
        c_in = fcut(K2 * GT).rearrange("p (k t) -> p k t", k=K2)
        fmark = wat[0]
        wa0_raw = fcut(4 * K2 * D).rearrange("p (m k n) -> p m k n", m=4, k=K2)
        wat[0] = fmark
        v0 = fcut(GB * H * 32).rearrange("p (b h d) -> p b h d", b=GB, h=H)
        probs = [fcut(8 * P).rearrange("p (h q) -> p h q", h=8) for _ in range(2)]
        oT_raw = fcut(512).rearrange("p (c q) -> p c q", c=4)
        mask0_raw = oT_raw[:, 0:2, :].bitcast(I32)
        o_tok = fcut(D)
        xn = [fcut(D) for _ in range(2)]
        stats = fcut(2 * 6 * GB).rearrange("p (n s) -> p n s", s=6)
        mv = fcut(2 * 2 * GB).rearrange("p (n s) -> p n s", s=2)
        rstd, newton = fcut(2 * GB), fcut(2 * GB)
        mx = [fcut(8) for _ in range(2)]
        rden = fcut(H)

        wat[0] = fmark
        lgT = fcut(T)
        gu_s = [fcut(GT) for _ in range(2)]
        gu_h = [fcut(GT) for _ in range(2)]
        rt = [fcut(P) for _ in range(9)]
        rs = [fcut(B) for _ in range(4)]
        wat[0] = 0
        k1 = fcut(2 * GT).rearrange("p (m t) -> p m t", m=2)
        q1 = fcut(2 * GT).rearrange("p (m t) -> p m t", m=2)
        mask = fcut(GT).rearrange("p (b k) -> p b k", b=GB)
        assert wat[0] <= 2 * W2C
        wat[0] = fmark
        wa1_raw = fcut(3 * K2 * D).rearrange("p (m k n) -> p m k n", m=3, k=K2)
        wat[0] = fmark
        v1 = fcut(GB * D).rearrange("p (b n) -> p b n", b=GB)
        sc1 = fcut(GT).rearrange("p (b k) -> p b k", b=GB)
        p1T = fcut(GT).rearrange("p (b q) -> p b q", b=GB)
        lg1T = fcut(GT)
        r3 = [fcut(GB * E).rearrange("p (b e) -> p b e", b=GB) for _ in range(4)]
        r3s = [fcut(GB) for _ in range(6)]
        counted = fcut(E)
        xn_b = [fcut(D) for _ in range(GB)]
        nmax, sum1, gsc = fcut(GB), fcut(GB), fcut(GB)
        assert wat[0] <= fmark + 4096
        wat[0] = fmark + 4096
        xn_a = [fcut(D) for _ in range(GB)]
        st3 = fcut(2 * 6 * GB).rearrange("p (n s) -> p n s", s=6)
        mv3 = fcut(2 * 2 * GB).rearrange("p (n s) -> p n s", s=2)
        rstd3, newton3 = fcut(2 * GB), fcut(2 * GB)
        tok_idx = sb("tok_idx", B, I32)
        ones_before = sb("ones_before", E, BF16)
        oh_b = sb("oh_b", GB * E, BF16).rearrange("p (b e) -> p b e", b=GB)
        tokn = sb("tokn", 2 * GB)
        wat[0] = 0
        raw4 = [fcut(4096).rearrange("p (a n) -> p a n", a=2) for _ in range(2)]
        xd = [fcut(D) for _ in range(2)]
        yo = [[fcut(D) for j in range(2)] for i in range(2)]
        out_idx = [sb(f"out_idx{i}", 2, I32) for i in range(2)]
        xs = x_all

        ps = psum

        s_passed = sem("wait_passed")
        ORDER0 = (1, 2, 0, 3)

        def reciprocal_root(dve, step, var, r, t):
            step(dve.tensor_scalar(t, var, EPS, None, ALU.add))
            step(dve.tensor_scalar(r.bitcast(I32), t.bitcast(I32), -0.5, float(0x5f3759df), ALU.mult, ALU.add))
            for _ in range(3):
                step(dve.tensor_tensor(u := scratch[:, 0:r.shape[1]], r, r, ALU.mult))
                step(dve.scalar_tensor_tensor(u, u, -0.5, t, ALU.mult, ALU.mult))
                step(dve.scalar_tensor_tensor(r, u, 1.5, r, ALU.add, ALU.mult))

        def alone(eng):
            eng.sem_inc(s_passed, 1)

        s_mask0 = sem("mask0_loaded")
        s_const, s_small = sem("const_loaded"), sem("small_loaded")
        s_waraw = [sem(f"attn_weights_loaded{m}") for m in range(4)]
        s_x, s_c = [sem("first_x_loaded"), sem("other_x_loaded")], sem("ctx_loaded")
        s_setup = Steps(sem("vector_setup_step"), 0)
        s_wa_hi, s_wa_lo = sem("attn_weights_high"), sem("attn_weights_low")
        s_bo = sem("bias_gated")
        s_tanh, s_fill = sem("tanh_ready"), sem("fill_ready")
        sg = {}

        def signal(name, per):
            sg[name] = Signal(sem(name), per)
            return sg[name]

        c_hi, c_lo = signal("ctx_high", 1), signal("ctx_low", 1)
        ln0 = signal("xn_ready", GB)
        xt_tr = signal("xn_transposed", GB)
        xt_hi, xt_lo = signal("xnT_high", 2), signal("xnT_low", 2)
        pj_k, pj_v, pj_q = signal("k_projected", 2), signal("v_projected", 2), signal("q_projected", 2)
        k_hi, k_lo, k_m = signal("k_high", 2), signal("k_low", 2), signal("k_masked", 2)
        v_ok = signal("v_ready", 2 * 2)
        q_hi, q_lo = signal("q_high", 2), signal("q_low", 2)
        q_mh, q_m = signal("q_high_masked", 4), signal("q_low_masked", 4)
        sc_q = signal("scores_for_max", UNITS)
        mx_ok, dg = signal("max_ready", UNITS), signal("diag_ready", UNITS)
        sc_k = signal("scores_shifted", UNITS)
        ex = signal("exp_ready", UNITS)
        pv = signal("pv_done", UNITS)
        o_raw = signal("oT_copied", GB)
        o_tr = signal("o_transposed", GB)
        o_n = signal("o_normalised", GB)
        o_nt = signal("o_back", GB)
        oT_hi, oT_lo = signal("oT_high", GB), signal("oT_low", GB)
        wo = signal("wo_done", GB)
        x1 = signal("x_after_attn", GB)
        ln1 = signal("xn1_ready", GB)
        x1t = signal("xn1_transposed", GB)
        x1_hi, x1_lo = signal("xn1T_high", GB), signal("xn1T_low", GB)
        xb_ok = signal("x_with_bias", GB)
        vs0, vs = Steps(sem("vector_norm_step"), VS0), Steps(sem("vector_step"), VS1)


        NC2, NH2 = 2 * G, 4 * G
        lg, lgc, lgt = sem("logits_ready"), sem("logits_copied"), sem("logits_transposed")
        s_wexp = sem("routing_weights_ready")
        re_step = Steps(sem("routing_step"), 0)
        s_inh, s_fb = sem("sigmoid_exp_ready"), sem("zone_exp_ready")
        s_raw2 = [sem(f"expert_weights_loaded{i}") for i in range(2)]
        w2q_hi, w2q_lo = signal("first_experts_high", 1), signal("first_experts_low", 1)
        w2_hi, w2_lo = signal("expert_high", 2), signal("expert_low", 2)
        gt, up = signal("gate_ready", NH2), signal("up_ready", NH2)
        sl, hm = signal("silu_ready", NH2), signal("h_ready", NH2)
        hh, hl = signal("h_high", NH2), signal("h_low", NH2)
        dn, ac = signal("down_ready", NC2), signal("x_accumulated", NC2)
        wcur = signal("expert_weight_picked", 2)
        as2 = Steps(sem("vector_step2"), 3 * NC2)

        s_c3, s_m3, s_wa1, s_base = sem("ctx3_loaded"), sem("mask_loaded"), sem("wa1_loaded"), sem("base_out_written")
        s_wa1_hi, s_wa1_lo = sem("wa1_high"), sem("wa1_low")
        s_disp = sem("rows_dispatched")
        c3_hi, c3_lo = signal("ctx3_high", 1), signal("ctx3_low", 1)
        na, nat = signal("xn2_ready", GB), signal("xn2_transposed", GB)
        na_hi, na_lo = signal("xn2T_high", 2), signal("xn2T_low", 2)
        nb, nbt = signal("xn3_ready", GB), signal("xn3_transposed", GB)
        nb_hi, nb_lo = signal("xn3T_high", 2), signal("xn3T_low", 2)
        pk3, pv3, pq3 = signal("k1_projected", 2), signal("v1_projected", 2), signal("q1_projected", 2)
        k1_ok, v1_ok, q1_ok = signal("k1_ready", 2), signal("v1_ready", 2), signal("q1_ready", 2)
        s1 = signal("scores1_ready", 1)
        s1m, m1 = signal("scores1_masked", 1), signal("max1_ready", 1)
        e1 = signal("probs1_ready", GB)
        t1 = signal("probs1_transposed", 1)
        p1_ok = signal("probs1T_ready", 1)
        a1 = signal("attn1_ready", 2)
        x3 = signal("x3_ready", GB)
        l1, l1c, l1t = signal("logits1_ready", 1), signal("logits1_copied", 1), signal("logits1_transposed", 1)
        ex1, r1e = signal("gate_shift_ready", 1), signal("gate_exp_ready", 1)
        oh1, loc1 = signal("onehot_ready", 1), signal("places_ready", 1)
        dest = signal("rows_ready", 1)
        dsa, dsb = Steps(sem("vector_step3a"), DSA), Steps(sem("vector_step3b"), DSB)
        dsm = Steps(sem("vector_max_step3"), 1)

        s_xs = [sem("first_slots_loaded"), sem("other_slots_loaded")]
        s_raw4 = [sem(f"expert1_weights_loaded{i}") for i in range(2)]
        w4_hi, w4_l1, w4_l2 = signal("expert1_high", 4), signal("expert1_w1_low", 2), signal("expert1_w2_low", 2)
        xd_ok = signal("slots_normalised", 4)
        xd_t = signal("slots_transposed", 2)
        di_hi, di_lo = signal("slotsT_high", 2), signal("slotsT_low", 2)
        h1, h1_hi, h1_lo = signal("hidden_ready", 16), signal("hidden_high", 16), signal("hidden_low", 16)
        d4 = signal("expert1_out_ready", 2)
        y4 = signal("rows_out_ready", 2)
        idx4 = signal("row_numbers_ready", 2)
        out_left = signal("rows_out_left", 2)
        s_sc = [sem(f"rows_scattered{i}") for i in range(2)]
        ds4 = Steps(sem("vector_step4"), 2)

        block = ctx.enter_context(nc.Block())

        def two_seqs(t, c):
            return t[:, :, 2 * c * P:(2 * c + 2) * P].rearrange("p k (b t) -> p b k t", b=2)

        def slot_cols(t):
            return t.rearrange("p k (b t) -> p b k t", b=2)

        def in_bank(i):
            return ps[:, i, :].rearrange("p (b k t) -> p b k t", b=2, k=K2)

        @block.sync
        def _(sp):
            sp.dma_start(c_in, ctxT[:, 0:GT].rearrange("(k p) t -> p k t", p=P)).then_inc(s_c, 16)

            def weights(m):
                sp.dma_start(wa0_raw[:, m, :, :], wa0[m].rearrange("(k p) n -> p k n", p=P)).then_inc(s_waraw[m], 16)
            weights(1)
            sp.dma_start(x_all[:, 0:GB, 0:D], x[0:GB].rearrange("b s d -> s b d")).then_inc(s_x[0], 16)
            weights(2)
            sp.dma_start(cst[:, :], const).then_inc(s_const, 16)
            sp.dma_start(mask0_raw, mask0.rearrange("a p n -> p a n")).then_inc(s_mask0, 16)
            weights(0)
            weights(3)
            sp.dma_start(biasc[:, :], bcols).then_inc(s_small, 16)
            for i, b in enumerate((bv0, bo0, bv1)):
                sp.dma_start(biasr[:, i * D:(i + 1) * D], b.rearrange("(a d) -> a d", a=1).to_broadcast([P, D])
                             ).then_inc(s_small, 16)
            sp.dma_start(wr_raw, wrs.rearrange("l (k p) e -> p l k e", p=P)).then_inc(s_small, 16)
            for a, i, n in ((gx, 0, 2), (gf, 2, 2), (temp, 4, 1)):
                sp.dma_start(scal[:, i:i + n], a.rearrange("(a d) -> a d", a=1).to_broadcast([P, n])
                             ).then_inc(s_small, 16)
            for i in range(2):
                sp.dma_start(raw[i], w0[i:i + 1].rearrange("e p n -> p (e n)")).then_inc(s_raw2[i], 16)
            sp.dma_start(x_all[:, GB:B, 0:D], x[GB:B].rearrange("b s d -> s b d")).then_inc(s_x[1], 16)
            with sp.Fori(0, G - 1) as g:
                sp.wait_ge(c_hi.sem, c_hi.now(g, 1))
                alone(sp)
                sp.wait_ge(c_lo.sem, c_lo.now(g, 1))
                alone(sp)
                sp.dma_start(c_in, ctxT[:, bass.ds(g * GT + GT, GT)].rearrange("(k p) t -> p k t", p=P)
                             ).then_inc(s_c, 16)
            with sp.Fori(1, E // 2) as g:
                for i in range(2):
                    sp.wait_ge(w2_lo.sem, w2_lo.before(g, i + 1))
                    alone(sp)
                    sp.dma_start(raw[i], w0[bass.ds(2 * g + i, 1)].rearrange("e p n -> p (e n)")).then_inc(s_raw2[i], 16)
            sp.wait_ge(s_wexp, 1)
            sp.dma_start(wa1_raw, wa1.rearrange("m (k p) n -> p m k n", p=P)).then_inc(s_wa1, 16)
            def ctx_load(g):
                sp.wait_ge(c3_lo.sem, c3_lo.before(g, 1))
                alone(sp)
                sp.wait_ge(c3_hi.sem, c3_hi.before(g, 1))
                alone(sp)
                sp.dma_start(c_in, ctxT[:, bass.ds(g * GT, GT)].rearrange("(k p) t -> p k t", p=P)).then_inc(s_c3, 16)

            def mask_load(g):
                sp.wait_ge(s1m.sem, s1m.before(g, 1))
                alone(sp)
                sp.dma_start(mask, maskf[bass.ds(g * GB, GB)].rearrange("b q k -> q b k")).then_inc(s_m3, 16)

            def base_out(g):
                sp.wait_ge(x3.sem, x3.now(g, GB))
                alone(sp)
                sp.dma_start(out[bass.ds(g * GB, GB)].rearrange("b s d -> s b d"), x_all[:, bass.ds(g * GB, GB), 0:D]
                             ).then_inc(s_base, 16)

            def load4(i, e):
                sp.dma_start(raw4[i][:, 0, :].rearrange("p (k n) -> p k n", k=K2),
                             w1[e].rearrange("e (k p) n -> p (e k) n", p=P)).then_inc(s_raw4[i], 16)
                sp.dma_start(raw4[i][:, 1, :].rearrange("p (f n) -> p f n", f=8),
                             w2[e].rearrange("e (f p) n -> p (e f) n", p=P)).then_inc(s_raw4[i], 16)

            sp.wait_ge(c_lo.sem, c_lo.total(G))
            ctx_load(0)
            sp.wait_ge(w2_lo.sem, w2_lo.total(E // 2))
            mask_load(0)
            with sp.Fori(0, G - 1) as g:
                ctx_load(g + 1)
                mask_load(g + 1)
                base_out(g)
            sp.wait_ge(c3_lo.sem, c3_lo.total(G))
            sp.wait_ge(s1m.sem, s1m.total(G))
            load4(0, slice(0, 1))
            base_out(G - 1)
            sp.wait_ge(s_disp, 16 * B + 16)
            sp.wait_ge(s_base, 16 * G)
            sp.wait_ge(dsb.sem, dsb.total(G))

            for n, tiles in enumerate((slice(0, 4), slice(4, B))):
                sp.dma_start(xs[:, tiles, :], slots[tiles.start * P:tiles.stop * P, :].rearrange("(t p) c -> p t c", p=P)
                             ).then_inc(s_xs[n], 16)
                if n == 0:
                    load4(1, slice(1, 2))
            with sp.Fori(0, E // 2 - 1) as g:
                for i in range(2):
                    sp.wait_ge(w4_hi.sem, w4_hi.now(g, 2 * i + 2))
                    alone(sp)
                    sp.wait_ge(w4_l1.sem, w4_l1.now(g, i + 1))
                    alone(sp)
                    sp.wait_ge(w4_l2.sem, w4_l2.now(g, i + 1))
                    alone(sp)
                    load4(i, bass.ds(2 * g + 2 + i, 1))

        @block.scalar
        def _(act):
            for s in (c_hi, xt_hi, k_hi, q_hi, ex, o_raw, oT_hi, x1_hi, sl, hh, c3_hi, q_mh):
                s.credit(act)

            def logits_copy(n):
                act.wait_ge(pv.sem, pv.total(G))
                act.wait_ge(lg, n + 1)
                act.activation(lgT[0:E, n * GT:(n + 1) * GT], ps[0:E, 4 + n % 2, :], ACT.Copy).then_inc(lgc, 1)

            def hidden2(g, i):
                act.wait_ge(gt.sem, gt.now(g, i + 1))
                act.wait_ge(hm.sem, hm.now(g, i - 1))
                act.activation(gu_s[i % 2], ps[:, i % 2, :], ACT.Silu).then_inc(sl.sem, 1)
                act.wait_ge(hm.sem, hm.now(g, i + 1))
                c = i // 2
                act.wait_ge(dn.sem, dn.now(g, c - 1))
                act.activation(hT[c % 2][0][:, i % 2, :], gu_h[i % 2], ACT.Copy).then_inc(hh.sem, 1)

            def ctx_high(g):
                act.wait_ge(s_c, g * 16 + 16)
                act.wait_ge(pj_k.sem, pj_k.before(g, 2))
                act.wait_ge(pj_v.sem, pj_v.before(g, 2))
                act.activation(cT[0], c_in, ACT.Copy).then_inc(c_hi.sem, 1)

            def xn_high(g, c):
                act.wait_ge(xt_tr.sem, xt_tr.now(g, 2 * c + 2))
                act.wait_ge(pj_q.sem, pj_q.before(g, 2))
                act.activation(two_seqs(xnT[0], c), in_bank(7), ACT.Copy).then_inc(xt_hi.sem, 1)

            def k_high(g, m):
                act.wait_ge(pj_k.sem, pj_k.now(g, m + 1))
                act.wait_ge(sc_k.sem, sc_k.before(g, UNITS))
                act.wait_ge(k_m.sem, k_m.before(g, 2))
                act.activation(kT[0][:, m, :], ps[:, m, :], ACT.Identity, bias=biasc[:, 2 + m:3 + m]
                               ).then_inc(k_hi.sem, 1)

            def q_high(g, m):
                act.wait_ge(pj_q.sem, pj_q.now(g, m + 1))
                act.wait_ge(q_m.sem, q_m.before(g, 4))
                act.activation(qT[0][:, m, :], ps[:, 4 + m, :], ACT.Identity, bias=biasc[:, m:m + 1]
                               ).then_inc(q_hi.sem, 1)

            def q_mask(g, m):
                act.wait_ge(sc_k.sem, sc_k.before(g, UNITS))
                act.wait_ge(q_hi.sem, q_hi.now(g, m + 1))
                for r in range(2):
                    act.activation(qM[0][:, m, r, :], qT[0][:, m, :], ACT.Copy, scale=parity[:, r:r + 1]).then_inc(q_mh.sem, 1)

            def exponential(g, u):
                act.wait_ge(sc_k.sem, sc_k.now(g, u + 1))
                act.wait_ge(pv.sem, pv.now(g, u - 1) if u >= 2 else pv.before(g, UNITS - 1 + u))
                act.activation(probs[u % 2], ps[:, 2 + 2 * (u % 2):4 + 2 * (u % 2), :].rearrange("p j (h q) -> p (j h) q", q=P),
                               ACT.Exp, scale=DH ** -0.5).then_inc(ex.sem, 1)

            def units(g, ga):
                def o_copy(b):
                    act.wait_ge(pv.sem, pv.now(g, 2 * b + 2))
                    act.wait_ge(o_tr.sem, o_tr.now(g, b) if b else o_tr.before(g, GB))
                    act.activation(oT_raw, ps[:, 6, :].rearrange("p (c q) -> p c q", c=4), ACT.Copy).then_inc(o_raw.sem, 1)

                def o_high(b):
                    act.wait_ge(o_nt.sem, o_nt.now(g, b + 1))
                    act.wait_ge(wo.sem, wo.now(g, b) if b else wo.before(g, GB))
                    act.activation(oT[0], ps[:, 7, 0:256].rearrange("p (k t) -> p k t", k=K2), ACT.Copy
                                   ).then_inc(oT_hi.sem, 1)

                def x1_high(b):
                    act.wait_ge(x1t.sem, x1t.now(g, b + 1))
                    act.activation(xnT_all[0][:, :, bass.ds(g * GT + b * P, P)],
                                   ps[:, 7, 0:256].rearrange("p (k t) -> p k t", k=K2), ACT.Copy).then_inc(x1_hi.sem, 1)

                for u in range(1, UNITS):
                    if ga is not None and u == 1:
                        ctx_high(ga)
                    if u >= 5 and u % 2:
                        x1_high((u - 5) // 2)
                    if ga is not None and u == 2:
                        xn_high(ga, 0)
                    exponential(g, u)
                    if ga is not None and u == 2:
                        xn_high(ga, 1)
                    if u % 2 == 0:
                        o_copy(u // 2 - 1)
                    elif u >= 3:
                        o_high((u - 3) // 2)
                if ga is not None:
                    for m in range(2):
                        k_high(ga, m)
                o_copy(GB - 1)
                if ga is None:
                    hidden2(0, 0)
                    logits_copy(0)
                    logits_copy(1)
                x1_high(GB - 2)
                if ga is not None:
                    for m in range(2):
                        q_high(ga, m)
                    q_mask(ga, 0)
                else:
                    hidden2(0, 1)
                    logits_copy(2)
                o_high(GB - 1)
                if ga is not None:
                    q_mask(ga, 1)
                    exponential(ga, 0)
                else:
                    hidden2(0, 2)
                    hidden2(0, 3)
                x1_high(GB - 1)

            ctx_high(0)
            for m in ORDER0:
                act.wait_ge(s_waraw[m], 16)
                act.activation(wa[0][:, m, :, :], wa0_raw[:, m, :, :], ACT.Copy).then_inc(s_wa_hi, 1)
            act.wait_ge(s_small, 16 * 8)
            act.activation(tgate[:, :], scal[:, 0:4], ACT.Tanh).then_inc(s_tanh, 1)
            for m in range(2):
                k_high(0, m)
            for c in range(2):
                xn_high(0, c)
            for m in range(2):
                q_high(0, m)
            act.wait_ge(s_setup.sem, 6)
            for m in range(2):
                q_mask(0, m)
            exponential(0, 0)
            with act.Fori(0, G - 1) as g:
                units(g, g + 1)
            units(G - 1, None)

            logits_copy(3)
            act.wait_ge(s_inh, 1)
            act.activation(rt[2], rt[1], ACT.Exp, scale=-1.0).then_inc(s_inh, 1)
            act.wait_ge(s_fb, 1)
            act.activation(rt[4], rt[3], ACT.Exp, scale=-1.0 / 0.1).then_inc(s_fb, 1)
            act.wait_ge(s_fb, 2)
            act.activation(rt[5], rt[3], ACT.Exp, scale=-1.0 / 0.3).then_inc(s_fb, 1)

            def pair2(g, last):
                for c in range(NC2 - 2 if last else NC2):
                    hidden2(g, 2 * c + 4)
                    hidden2(g, 2 * c + 5)

            def ctx3_high(g):
                act.wait_ge(s_c3, g * 16 + 16)
                act.wait_ge(pv3.sem, pv3.before(g, 2))
                act.activation(cT[0], c_in, ACT.Copy).then_inc(c3_hi.sem, 1)
            with act.Fori(0, E // 2 - 1) as g:
                pair2(g, False)
            ctx3_high(0)
            pair2(E // 2 - 1, True)

            for s in (w4_hi, na_hi, nb_hi, k1_ok, q1_ok, e1, p1_ok, l1c, r1e):
                s.credit(act)

            def split(g, i, a):
                act.wait_ge(s_raw4[i], 32 * g + 32)
                if not isinstance(g, int) or (g, i) != (0, 0):
                    act.wait_ge(d4.sem, d4.before(g, i + 1))
                act.activation(w4[i][0][:, a, :], raw4[i][:, a, :], ACT.Copy).then_inc(w4_hi.sem, 1)

            def turn3(ga, gb, gn):
                if gb is not None:
                    act.wait_ge(t1.sem, t1.now(gb, 1))
                    act.wait_ge(a1.sem, a1.before(gb, 2))
                    act.activation(p1T, ps[:, 4, :].rearrange("p (b q) -> p b q", b=GB), ACT.Copy).then_inc(p1_ok.sem, 1)
                    if ga is None:
                        act.wait_ge(a1.sem, a1.total(G))
                        split(0, 0, 0)
                if ga is not None:
                    for c in range(2):
                        act.wait_ge(nat.sem, nat.now(ga, 2 * c + 2))
                        act.wait_ge(pq3.sem, pq3.before(ga, 2))
                        act.activation(two_seqs(xnT[0], c), in_bank(2 + c), ACT.Copy).then_inc(na_hi.sem, 1)
                    for m in range(2):
                        act.wait_ge(pk3.sem, pk3.now(ga, m + 1))
                        act.wait_ge(s1.sem, s1.before(ga, 1))
                        act.activation(k1[:, m, :], ps[:, m, :], ACT.Identity, bias=biasc[:, 6 + m:7 + m]).then_inc(k1_ok.sem, 1)
                    for m in range(2):
                        act.wait_ge(pq3.sem, pq3.now(ga, m + 1))
                        act.activation(q1[:, m, :], ps[:, m, :], ACT.Identity, bias=bq1s[:, m:m + 1], scale=1.0 / 16
                                       ).then_inc(q1_ok.sem, 1)
                if gb is not None:
                    for c in range(2):
                        act.wait_ge(nbt.sem, nbt.now(gb, 2 * c + 2))
                        act.wait_ge(l1.sem, l1.before(gb, 1))
                        act.activation(two_seqs(xnT_b[0], c), in_bank(6 + c), ACT.Copy).then_inc(nb_hi.sem, 1)
                if gn is not None:
                    ctx3_high(gn)
                if gb is not None:
                    act.wait_ge(l1.sem, l1.now(gb, 1))
                    act.wait_ge(l1t.sem, l1t.before(gb, 1))
                    act.activation(lg1T[0:E, :], ps[0:E, 5, :], ACT.Copy).then_inc(l1c.sem, 1)
                if ga is not None:
                    act.wait_ge(m1.sem, m1.now(ga, 1))
                    act.wait_ge(x3.sem, x3.before(ga, GB))
                    for b in range(GB):
                        act.activation(sc1[:, b, :], sc1[:, b, :], ACT.Exp, bias=nmax[:, b:b + 1], accum_out=sum1[:, b:b + 1]
                                       ).then_inc(e1.sem, 1)
                if gb is not None:
                    act.wait_ge(ex1.sem, ex1.now(gb, 1))
                    act.activation(r3[3], r3[2], ACT.Exp).then_inc(r1e.sem, 1)
            turn3(0, None, 1)
            with act.Fori(0, G - 2) as g:
                turn3(g + 1, g, g + 2)
            turn3(G - 1, G - 2, None)
            turn3(None, G - 1, None)

            for s in (di_hi, h1_hi):
                s.credit(act)

            def slots_high(g, i):
                act.wait_ge(xd_t.sem, xd_t.now(g, i + 1))
                act.wait_ge(h1.sem, h1.before(g, 8 * i + 8))
                act.activation(slot_cols(diT[i][0]), in_bank(6 + i), ACT.Copy).then_inc(di_hi.sem, 1)

            def hidden(g, i, f):
                if f == 0:
                    act.wait_ge(d4.sem, d4.before(g, i + 1))
                act.wait_ge(h1.sem, h1.now(g, 8 * i + f + 1))
                act.activation(h4[i][0][:, f, :], ps[:, f % 4, 0:CAP], ACT.Relu).then_inc(h1_hi.sem, 1)

            def turn(g, last):
                for i in range(2):
                    nxt = (g, 1) if i == 0 else (g + 1, 0)
                    more = i == 0 or not last
                    for f in range(8):
                        hidden(g, i, f)
                        if more and f == 1:
                            split(*nxt, 0)
                    if more:
                        slots_high(*nxt)
                        split(*nxt, 1)
            split(0, 0, 1)
            slots_high(0, 0)
            with act.Fori(0, E // 2 - 1) as g:
                turn(g, False)
            turn(E // 2 - 1, True)

        @block.vector
        def _(dve):
            su = s_setup
            for s in (ln0, xt_lo, k_lo, v_ok, q_lo, q_m, mx_ok, o_n, oT_lo, x1, ln1, x1_lo, vs0, vs,
                      hm, hl, ac, wcur, as2, na, dsa):
                s.credit(dve)

            def weights_low(n):
                m = ORDER0[n]
                dve.wait_ge(s_wa_hi, n + 1)
                dve.tensor_tensor(wa[1][:, m, :, :], wa0_raw[:, m, :, :], wa[0][:, m, :, :], ALU.subtract).then_inc(s_wa_lo, 1)

            def constants_ready():
                dve.wait_ge(s_const, 16)
                su.done(dve.tensor_scalar(neg_ident[:, :], ident, -1.0, None, ALU.mult))
                su.done(dve.tensor_copy(parity[:, 1:2], cst[:, C_ODD:C_ODD + 1]))
                su.done(dve.tensor_scalar(parity[:, 0:1], cst[:, C_ODD:C_ODD + 1], -1.0, 1.0, ALU.mult, ALU.add))
                su.done(dve.memset(ones_b[:, :], 1.0))
                su.done(dve.tensor_scalar(ones_r[:, :], ident, 0.0, 1.0, ALU.mult, ALU.add))
                su.done(dve.tensor_copy(tri_b[:, :], cst[:, C_TRI:C_TRI + P]))
                su.done(dve.tensor_copy(ident_b[:, :], ident))
                dve.wait_ge(s_mask0, 16)
                su.done(dve.tensor_scalar(hide, mask0_raw, 0.0, HIDDEN, ALU.is_equal, ALU.mult))

            def values_ready():
                dve.wait_ge(s_wa_lo, 4)
                su.done(dve.memset(v0[:, :, :, DH + 1:32], 0.0))
                su.done(dve.memset(v0[:, :, :, DH:DH + 1], 1.0))
                dve.wait_ge(su.sem, su.last)

            def small_ready():
                dve.wait_ge(s_tanh, 1)
                dve.wait_ge(s_small, 16 * 8)
                for i in range(2):
                    su.done(dve.memset(wr[i].bitcast(F32), 0.0))
                su.done(dve.memset(fill[:, 0:ROW - 1], 0.0))
                dve.memset(fill[:, ROW - 1:ROW], float(2 * T)).then_inc(s_fill, 1)
                dve.wait_ge(su.sem, su.last)
                su.done(dve.tensor_copy(wr[0][:, :, :, 0:E], wr_raw))
                su.done(dve.memset(ones_before[:, :], 0.0))
                su.done(dve.tensor_copy(tokn[:, :], cst[:, C_TOK:C_TOK + 2 * GB]))
                su.done(dve.tensor_scalar(bq1s[:, :], biasc[:, 4:6], 1.0 / 16, None, ALU.mult))
                su.done(dve.reciprocal(scal[:, 5:6], scal[:, 4:5]))
                dve.wait_ge(su.sem, su.last)
                su.done(dve.tensor_tensor(wr[1][:, :, :, 0:E], wr_raw, wr[0][:, :, :, 0:E], ALU.subtract))
                dve.tensor_scalar(bo0r, bo0r, tgate[:, 0:1], None, ALU.mult).then_inc(s_bo, 1)
                dve.wait_ge(su.sem, su.last)

            def hidden2(g, i):
                dve.wait_ge(sl.sem, sl.now(g, i + 1))
                dve.wait_ge(up.sem, up.now(g, i + 1))
                dve.wait_ge(hl.sem, hl.now(g, i - 1))
                dve.tensor_tensor(gu_h[i % 2], gu_s[i % 2], ps[:, 2 + i % 2, :], ALU.mult).then_inc(hm.sem, 1)
                dve.wait_ge(hh.sem, hh.now(g, i + 1))
                dve.tensor_tensor(hT[i // 2 % 2][1][:, i % 2, :], gu_h[i % 2], hT[i // 2 % 2][0][:, i % 2, :],
                                  ALU.subtract).then_inc(hl.sem, 1)

            def x_of(g, b):
                return x_all[:, bass.ds(g * GB + b, 1), 0:D].rearrange("p a d -> p (a d)")

            def normalise(g, n, dst, sig):
                dve.tensor_scalar(dst, x_of(g, n % GB), mv[:, n, 0:1], rstd[:, n:n + 1], ALU.subtract, ALU.mult
                                  ).then_inc(sig.sem, 1)

            def moments(g):
                vs0.last = 0
                dve.wait_ge(s_x[0] if isinstance(g, int) else s_x[1], 16)
                dve.wait_ge(ln0.sem, ln0.before(g, GB))
                for b in range(GB):
                    alone(dve)
                    vs0.done(dve.bn_stats(stats[:, b, :], x_of(g, b)))
                dve.wait_ge(vs0.sem, vs0.now(g, vs0.last))
                for b in range(GB):
                    alone(dve)
                    vs0.done(dve.bn_aggr(mv[:, b, :], stats[:, b, :]))
                dve.wait_ge(vs0.sem, vs0.now(g, vs0.last))

            def root(g):
                reciprocal_root(dve, lambda ins: dve.wait_ge(vs0.sem, vs0.now(g, vs0.done(ins))),
                                mv[:, 0:GB, 1:2].rearrange("p n o -> p (n o)"), rstd[:, 0:GB], newton[:, 0:GB])
                assert vs0.last == VS0, vs0.last

            def norm0(g, c):
                for b in (2 * c, 2 * c + 1):
                    if b >= 2:
                        dve.wait_ge(xt_tr.sem, xt_tr.now(g, b - 1))
                    else:
                        dve.wait_ge(x1t.sem, x1t.before(g, GB) if isinstance(g, int) else x1t.before(g - 1, GB))
                    normalise(g, b, xn[b % 2], ln0)

            def xn_low(g, c):
                dve.wait_ge(xt_hi.sem, xt_hi.now(g, c + 1))
                dve.tensor_tensor(two_seqs(xnT[1], c), in_bank(7), two_seqs(xnT[0], c), ALU.subtract
                                  ).then_inc(xt_lo.sem, 1)

            def k_low(g, m):
                dve.wait_ge(k_hi.sem, k_hi.now(g, m + 1))
                dve.scalar_tensor_tensor(kT[1][:, m, :], ps[:, m, :], biasc[:, 2 + m:3 + m], kT[0][:, m, :],
                                         ALU.add, ALU.subtract).then_inc(k_lo.sem, 1)

            def v_add(g, c):
                dve.wait_ge(pj_v.sem, pj_v.now(g, c + 1))
                dve.wait_ge(pv.sem, pv.before(g, UNITS))
                for i in range(2):
                    dve.tensor_tensor(v0[:, 2 * c + i, :, 0:DH],
                                      ps[:, 2 + c, i * D:(i + 1) * D].rearrange("p (h d) -> p h d", d=DH),
                                      bv0r.rearrange("p (h d) -> p h d", d=DH), ALU.add).then_inc(v_ok.sem, 1)

            def q_low(g, m):
                dve.wait_ge(q_hi.sem, q_hi.now(g, m + 1))
                dve.scalar_tensor_tensor(qT[1][:, m, :], ps[:, 4 + m, :], biasc[:, m:m + 1], qT[0][:, m, :],
                                         ALU.add, ALU.subtract).then_inc(q_lo.sem, 1)
                dve.wait_ge(sc_k.sem, sc_k.before(g, UNITS))
                dve.wait_ge(q_lo.sem, q_lo.now(g, m + 1))
                for r in range(2):
                    dve.tensor_scalar(qM[1][:, m, r, :], qT[1][:, m, :], parity[:, r:r + 1], None, ALU.mult
                                      ).then_inc(q_m.sem, 1)

            def maximum(g, u):
                dve.wait_ge(sc_q.sem, sc_q.now(g, u + 1))
                dve.wait_ge(dg.sem, dg.now(g, u - 1) if u >= 2 else dg.before(g, UNITS - 1 + u))
                dve.tensor_reduce(mx[u % 2], ps[:, 0:2, :].rearrange("p j (h k) -> p (j h) k", k=P), AX.X, ALU.max
                                  ).then_inc(mx_ok.sem, 1)

            def units(g, ga):
                vs.last = 0

                def step(ins):
                    dve.wait_ge(vs.sem, vs.now(g, vs.done(ins)))

                def o_normalise(b):
                    o_ps = ps[:, 7, :].rearrange("p (h d) -> p h d", d=32)
                    dve.wait_ge(o_tr.sem, o_tr.now(g, b + 1))
                    step(dve.reciprocal(rden[:, :].rearrange("p (h o) -> p h o", o=1), o_ps[:, :, DH:DH + 1]))
                    dve.tensor_tensor(o_tok.rearrange("p (h d) -> p h d", d=DH), o_ps[:, :, 0:DH],
                                      rden[:, :].rearrange("p (h o) -> p h o", o=1).to_broadcast([P, H, DH]), ALU.mult
                                      ).then_inc(o_n.sem, 1)

                def o_low(b):
                    dve.wait_ge(oT_hi.sem, oT_hi.now(g, b + 1))
                    dve.tensor_tensor(oT[1], ps[:, 7, 0:256].rearrange("p (k t) -> p k t", k=K2), oT[0], ALU.subtract
                                      ).then_inc(oT_lo.sem, 1)

                def residual(b):
                    dve.wait_ge(wo.sem, wo.now(g, b + 1))
                    dve.wait_ge(xb_ok.sem, xb_ok.now(g, b + 1))
                    dve.scalar_tensor_tensor(x_of(g, b), ps[:, 7, 256:512], tgate[:, 0:1], x_of(g, b), ALU.mult, ALU.add
                                             ).then_inc(x1.sem, 1)
                    dve.wait_ge(x1.sem, x1.now(g, b + 1))
                    n = GB + b
                    alone(dve)
                    step(dve.bn_stats(stats[:, n, :], x_of(g, b)))
                    alone(dve)
                    step(dve.bn_aggr(mv[:, n, :], stats[:, n, :]))
                    reciprocal_root(dve, step, mv[:, n, 1:2], rstd[:, n:n + 1], newton[:, n:n + 1])
                    if b >= 2:
                        dve.wait_ge(x1t.sem, x1t.now(g, b - 1))
                    elif ga is not None:
                        dve.wait_ge(xt_tr.sem, xt_tr.now(ga, 3 + b))
                    normalise(g, n, xn[b % 2], ln1)

                def x1_low(b):
                    dve.wait_ge(x1_hi.sem, x1_hi.now(g, b + 1))
                    dve.tensor_tensor(xnT_all[1][:, :, bass.ds(g * GT + b * P, P)],
                                      ps[:, 7, 0:256].rearrange("p (k t) -> p k t", k=K2),
                                      xnT_all[0][:, :, bass.ds(g * GT + b * P, P)], ALU.subtract).then_inc(x1_lo.sem, 1)

                for u in range(1, UNITS):
                    if u > 1:
                        maximum(g, u)
                    if ga is not None:
                        if u == 1:
                            moments(ga)
                        if u == 2:
                            root(ga)
                            norm0(ga, 0)
                        if u == 3:
                            xn_low(ga, 0)
                            norm0(ga, 1)
                            xn_low(ga, 1)
                    if u >= 6 and u % 2 == 0:
                        x1_low((u - 6) // 2)
                    if u >= 4 and u % 2 == 0:
                        o_normalise((u - 4) // 2)
                        o_low((u - 4) // 2)
                    if u >= 5 and u % 2:
                        residual((u - 5) // 2)
                x1_low(1)
                o_normalise(2)
                o_low(2)
                residual(2)
                if ga is not None:
                    for m in range(2):
                        k_low(ga, m)
                    for c in range(2):
                        v_add(ga, c)
                else:
                    hidden2(0, 0)
                x1_low(2)
                if ga is not None:
                    q_low(ga, 0)
                else:
                    hidden2(0, 1)
                o_normalise(3)
                if ga is not None:
                    q_low(ga, 1)
                o_low(3)
                if ga is not None:
                    maximum(ga, 0)
                else:
                    hidden2(0, 2)
                residual(3)
                if ga is not None:
                    maximum(ga, 1)
                else:
                    hidden2(0, 3)
                x1_low(3)
                assert vs.last == vs.per, vs.last

            dve.wait_ge(c_hi.sem, c_hi.now(0, 1))
            dve.tensor_tensor(cT[1], c_in, cT[0], ALU.subtract).then_inc(c_lo.sem, 1)
            weights_low(0)
            weights_low(1)
            moments(0)
            root(0)
            norm0(0, 0)
            constants_ready()
            weights_low(2)
            xn_low(0, 0)
            norm0(0, 1)
            weights_low(3)
            for m in range(2):
                k_low(0, m)
            xn_low(0, 1)
            values_ready()
            for c in range(2):
                v_add(0, c)
            for m in range(2):
                q_low(0, m)
            for u in range(2):
                maximum(0, u)
            small_ready()
            with dve.Fori(0, G - 1) as g:
                units(g, g + 1)
            units(G - 1, None)

            r = [t.rearrange("p (t e) -> p t e", e=E) for t in rt]
            rev = cst[:, C_REV:C_REV + P].rearrange("p (t e) -> p t e", e=E)

            def over_e(col):
                return col.rearrange("p (t o) -> p t o", o=1).to_broadcast([P, B, E])

            def seq(ins):
                dve.wait_ge(re_step.sem, re_step.done(ins))

            dve.wait_ge(lgt, 1)
            dve.tensor_scalar(rt[1], ps[:, 7, 0:P], scal[:, 5:6], -80.0, ALU.mult, ALU.max).then_inc(s_inh, 1)
            dve.wait_ge(s_inh, 2)
            seq(dve.tensor_scalar(rt[2], rt[2], 1.0, None, ALU.add))
            seq(dve.reciprocal(rt[2], rt[2]))
            seq(dve.tensor_scalar(rt[2], rt[2], -GOLD, None, ALU.add))
            dve.scalar_tensor_tensor(rt[3], rt[2], -1.0, rt[2], ALU.mult, ALU.max).then_inc(s_fb, 1)
            seq(dve.tensor_scalar(rt[6], rt[1], Z_LO, None, ALU.is_ge))
            seq(dve.scalar_tensor_tensor(rt[6], rt[1], 0.0, rt[6], ALU.is_le, ALU.mult))
            dve.wait_ge(s_fb, 3)
            seq(dve.tensor_tensor(rt[4], rt[4], rt[6], ALU.mult))
            seq(dve.tensor_reduce(rs[0], r[4], AX.X, ALU.add))
            seq(dve.tensor_scalar(rs[1], rs[0], 1e-8, None, ALU.is_lt))

            def first_of_max(src, dst):
                seq(dve.tensor_reduce(rs[2], src, AX.X, ALU.max))
                seq(dve.tensor_tensor(dst, src, over_e(rs[2]), ALU.is_equal))
                seq(dve.tensor_tensor(dst, dst, rev, ALU.mult))
                seq(dve.tensor_reduce(rs[3], dst, AX.X, ALU.max))
                seq(dve.tensor_tensor(dst, dst, over_e(rs[3]), ALU.is_equal))

            first_of_max(r[5], r[8])
            seq(dve.scalar_tensor_tensor(rt[1], rt[8], -4.0, rt[5], ALU.mult, ALU.add))
            first_of_max(r[1], r[7])
            seq(dve.tensor_tensor(rt[7], rt[7], rt[8], ALU.add))
            seq(dve.tensor_tensor(rt[7], rt[7], rt[5], ALU.mult))

            def divide_by_sum(t, i):
                seq(dve.tensor_reduce(rs[2], r[i], AX.X, ALU.add))
                seq(dve.tensor_scalar(rs[2], rs[2], 1e-8, None, ALU.max))
                seq(dve.reciprocal(rs[2], rs[2]))
                seq(dve.tensor_tensor(r[i], r[i], over_e(rs[2]), ALU.mult))

            divide_by_sum(rt[7], 7)
            seq(dve.tensor_tensor(r[7], r[7], over_e(rs[1]), ALU.mult))
            seq(dve.tensor_tensor(rt[4], rt[4], rt[7], ALU.add))
            divide_by_sum(rt[4], 4)
            dve.tensor_scalar(w_exp.rearrange("p e t -> p t e"), r[4], tgate[:, 2:3], None, ALU.mult).then_inc(s_wexp, 1)
            dve.wait_ge(s_wexp, 1)

            def pair2(g, last):
                as2.last = 0

                def accumulate(c):
                    e, n = c // 4, c % 4
                    if n == 0:
                        dve.wait_ge(ac.sem, ac.before(g, 4 * e + 4))
                        dve.tensor_copy(w_cur[e][:, :], w_exp[:, bass.ds(2 * g + e, 1), :].rearrange("p e t -> p (e t)")
                                        ).then_inc(wcur.sem, 1)
                        dve.wait_ge(wcur.sem, wcur.now(g, e + 1))
                    dve.wait_ge(dn.sem, dn.now(g, c + 1))
                    dve.wait_ge(ac.sem, ac.now(g, c - 3) if c >= 4 else ac.before(g, NC2 - 3 + c))
                    if as2.last:
                        dve.wait_ge(as2.sem, as2.now(g, as2.last))
                    for j in range(4):
                        t = 4 * n + j
                        ins = dve.scalar_tensor_tensor(x_all[:, t, 0:D], ps[:, 4 + 2 * (c % 2) + j // 2, (j % 2) * D:(j % 2 + 1) * D],
                                                       w_cur[e][:, t:t + 1], x_all[:, t, 0:D], ALU.mult, ALU.add)
                        if j < 3:
                            as2.done(ins)
                        else:
                            ins.then_inc(ac.sem, 1)

                dve.wait_ge(as2.sem, as2.before(g, as2.per))
                for c in range(NC2):
                    if last and c == NC2 - 2:
                        x_norm3(0)
                    accumulate(c)
                    if c < NC2 - 2 or not last:
                        hidden2(g, 2 * c + 4)
                        hidden2(g, 2 * c + 5)
                assert as2.last == as2.per

            def x_norm3(g):
                dsa.last = 0
                if isinstance(g, int):
                    dve.wait_ge(ac.sem, ac.now(E // 2 - 1, 5))
                dve.wait_ge(na.sem, na.before(g, GB))
                moments3(dsa, g, 0)
                root3(dsa, g, 0)
                for b in range(GB):
                    normalise3(g, b, 0, xn_a, nat, na)

            def moments3(steps, g, half):
                for b in range(GB):
                    alone(dve)
                    steps.done(dve.bn_stats(st3[:, half * GB + b, :], x_of(g, b)))
                dve.wait_ge(steps.sem, steps.now(g, steps.last))
                for b in range(GB):
                    alone(dve)
                    steps.done(dve.bn_aggr(mv3[:, half * GB + b, :], st3[:, half * GB + b, :]))
                dve.wait_ge(steps.sem, steps.now(g, steps.last))

            def root3(steps, g, half):
                sel = slice(half * GB, (half + 1) * GB)
                reciprocal_root(dve, lambda ins: dve.wait_ge(steps.sem, steps.now(g, steps.done(ins))),
                                mv3[:, sel, 1:2].rearrange("p n o -> p (n o)"), rstd3[:, sel], newton3[:, sel])

            def normalise3(g, b, half, xn3, turned, sig):
                n = half * GB + b
                if b == 0:
                    dve.wait_ge(turned.sem, turned.before(g, GB))
                dve.tensor_scalar(xn3[b], x_of(g, b), mv3[:, n, 0:1], rstd3[:, n:n + 1], ALU.subtract, ALU.mult
                                  ).then_inc(sig.sem, 1)
            with dve.Fori(0, E // 2 - 1) as g:
                pair2(g, False)
            pair2(E // 2 - 1, True)

            for s in (nb, na_lo, nb_lo, v1_ok, s1m, m1, x3, ex1, oh1, dest, dsm, dsb):
                s.credit(dve)
            dve.wait_ge(as2.sem, as2.total(E // 2))
            dve.wait_ge(ac.sem, ac.total(E // 2))

            def turn3(ga, gb, gn):
                dsb.last = 0

                def seqb(ins):
                    dve.wait_ge(dsb.sem, dsb.now(gb, dsb.done(ins)))

                if gb is not None:
                    dve.wait_ge(e1.sem, e1.now(gb, GB))
                    seqb(dve.reciprocal(gsc, sum1))
                    seqb(dve.tensor_scalar(gsc, gsc, tgate[:, 1:2], None, ALU.mult))
                if ga is not None:
                    for c in range(2):
                        dve.wait_ge(na_hi.sem, na_hi.now(ga, c + 1))
                        dve.tensor_tensor(two_seqs(xnT[1], c), in_bank(2 + c), two_seqs(xnT[0], c), ALU.subtract
                                          ).then_inc(na_lo.sem, 1)
                if gb is not None:
                    for b in range(GB):
                        dve.wait_ge(a1.sem, a1.now(gb, b // 2 + 1))
                        dve.scalar_tensor_tensor(x_of(gb, b), ps[:, 6 + b // 2, (b % 2) * D:(b % 2 + 1) * D], gsc[:, b:b + 1],
                                                 x_of(gb, b), ALU.mult, ALU.add).then_inc(x3.sem, 1)
                    dve.wait_ge(x3.sem, x3.now(gb, GB))
                    moments3(dsb, gb, 1)
                    root3(dsb, gb, 1)
                    for b in range(GB):
                        normalise3(gb, b, 1, xn_b, nbt, nb)
                if ga is not None:
                    for c in range(2):
                        dve.wait_ge(pv3.sem, pv3.now(ga, c + 1))
                        dve.wait_ge(a1.sem, a1.before(ga, 2))
                        dve.tensor_tensor(v1[:, 2 * c:2 * c + 2, :], ps[:, 2 + c, :].rearrange("p (b n) -> p b n", b=2),
                                          bv1r.rearrange("p (o n) -> p o n", o=1).to_broadcast([P, 2, D]), ALU.add
                                          ).then_inc(v1_ok.sem, 1)
                if gb is not None:
                    seqb(dve.tensor_copy(x_all[:, bass.ds(gb * GB, GB), D:D + 1], rstd3[:, GB:2 * GB].rearrange("p (b o) -> p b o", o=1)))
                    seqb(dve.scalar_tensor_tensor(x_all[:, bass.ds(gb * GB, GB), D + 1:D + 2], mv3[:, GB:2 * GB, 0:1], -1.0,
                                                  rstd3[:, GB:2 * GB].rearrange("p (b o) -> p b o", o=1), ALU.mult, ALU.mult))
                    seqb(dve.tensor_copy(x_all[:, bass.ds(gb * GB, GB), D + 3:D + 4], tokn[:, 0:GB].rearrange("p (b o) -> p b o", o=1)))
                    for c in range(2):
                        dve.wait_ge(nb_hi.sem, nb_hi.now(gb, c + 1))
                        dve.tensor_tensor(two_seqs(xnT_b[1], c), in_bank(6 + c), two_seqs(xnT_b[0], c), ALU.subtract
                                          ).then_inc(nb_lo.sem, 1)

                def mask_and_max():
                    dve.wait_ge(s1.sem, s1.now(ga, 1))
                    dve.wait_ge(s_m3, 16 * ga + 16)
                    dve.wait_ge(t1.sem, t1.before(ga, 1))
                    dve.scalar_tensor_tensor(sc1, mask, NEG, ps[:, 4, :].rearrange("p (b k) -> p b k", b=GB), ALU.mult, ALU.add
                                             ).then_inc(s1m.sem, 1)
                    dve.wait_ge(s1m.sem, s1m.now(ga, 1))
                    dve.wait_ge(e1.sem, e1.before(ga, GB))
                    dve.tensor_reduce(nmax, sc1, AX.X, ALU.max).then_inc(dsm.sem, 1)
                    dve.wait_ge(dsm.sem, dsm.now(ga, 1))
                    dve.tensor_scalar(nmax, nmax, -1.0, None, ALU.mult).then_inc(m1.sem, 1)

                lp = ps[:, 5, 0:GB * E].rearrange("p (b e) -> p b e", e=E)
                top, rank, gate, row, place, own = (r3s[i] for i in range(6))

                def over8(col):
                    return col.rearrange("p (t o) -> p t o", o=1).to_broadcast([P, GB, E])

                def pick_expert():
                    dve.wait_ge(l1t.sem, l1t.now(gb, 1))
                    seqb(dve.tensor_reduce(top, lp, AX.X, ALU.max))
                    seqb(dve.tensor_tensor(r3[0], lp, over8(top), ALU.is_equal))
                    seqb(dve.tensor_tensor(r3[0], r3[0], cst[:, C_REV:C_REV + GB * E].rearrange("p (b e) -> p b e", e=E), ALU.mult))
                    seqb(dve.tensor_reduce(rank, r3[0], AX.X, ALU.max))
                    dve.wait_ge(loc1.sem, loc1.before(gb, 1))
                    dve.tensor_tensor(r3[2], lp, over8(top), ALU.subtract).then_inc(ex1.sem, 1)
                    dve.wait_ge(ex1.sem, ex1.now(gb, 1))
                    dve.tensor_tensor(oh_b[:, :, :], r3[0], over8(rank), ALU.is_equal).then_inc(oh1.sem, 1)

                def pick_place():
                    dve.wait_ge(oh1.sem, oh1.now(gb, 1))
                    seqb(dve.tensor_reduce(counted[:, :], oh_b[:, :, :].rearrange("p b e -> p e b"), AX.X, ALU.add))
                    seqb(dve.tensor_scalar(own, tokn[:, GB:2 * GB], -1.0, float(E * CAP), ALU.mult, ALU.add))
                    seqb(dve.scalar_tensor_tensor(row, rank, -float(CAP), own, ALU.mult, ALU.add))
                    dve.wait_ge(r1e.sem, r1e.now(gb, 1))
                    seqb(dve.tensor_reduce(gate, r3[3], AX.X, ALU.add))
                    seqb(dve.reciprocal(gate, gate))
                    seqb(dve.tensor_scalar(x_all[:, bass.ds(gb * GB, GB), D + 2:D + 3], gate.rearrange("p (b o) -> p b o", o=1),
                                           tgate[:, 3:4], None, ALU.mult))
                    dve.wait_ge(loc1.sem, loc1.now(gb, 1))
                    seqb(dve.tensor_tensor(r3[1], ps[:, 5, GB * E:2 * GB * E].rearrange("p (b e) -> p b e", e=E), oh_b[:, :, :], ALU.mult))
                    seqb(dve.tensor_reduce(place, r3[1], AX.X, ALU.add))
                    seqb(dve.tensor_tensor(row, row, place, ALU.add))
                    seqb(dve.scalar_tensor_tensor(row, place, float(CAP), row, ALU.is_lt, ALU.mult))
                    dve.tensor_tensor(tok_idx[:, bass.ds(gb * GB, GB)], row, tokn[:, GB:2 * GB], ALU.add).then_inc(dest.sem, 1)
                    dve.wait_ge(dest.sem, dest.now(gb, 1))
                    seqb(dve.tensor_tensor(ones_before[:, :], ones_before[:, :], counted[:, :], ALU.add))
                    seqb(dve.tensor_scalar(tokn[:, :], tokn[:, :], float(GT), None, ALU.add))

                if ga is not None:
                    mask_and_max()
                if gn is not None:
                    x_norm3(gn)
                if gb is not None:
                    pick_expert()
                    pick_place()
                assert dsb.last in (0, DSB), dsb.last
            turn3(0, None, 1)
            with dve.Fori(0, G - 2) as g:
                turn3(g + 1, g, g + 2)
            turn3(G - 1, G - 2, None)
            turn3(None, G - 1, None)

            for s in (xd_ok, di_lo, w4_l2, h1_lo, y4, ds4, idx4):
                s.credit(dve)

            def slots_norm(g, i):
                for j in range(2):
                    row = xs[:, bass.ds(4 * g + 2 * i + j, 1), :].rearrange("p a c -> p (a c)") if not isinstance(g, int) \
                        else xs[:, 4 * g + 2 * i + j, :]
                    dve.wait_ge(xd_t.sem, xd_t.now(g, 1) if i else xd_t.before(g, 2))
                    dve.tensor_scalar(xd[j], row[:, 0:D], row[:, D:D + 1], row[:, D + 1:D + 2], ALU.mult, ALU.add
                                      ).then_inc(xd_ok.sem, 1)

            def slots_low(g, i):
                dve.wait_ge(di_hi.sem, di_hi.now(g, i + 1))
                dve.tensor_tensor(slot_cols(diT[i][1]), in_bank(6 + i), slot_cols(diT[i][0]), ALU.subtract
                                  ).then_inc(di_lo.sem, 1)

            def split_w2(g, i):
                dve.wait_ge(w4_hi.sem, w4_hi.now(g, 2 * i + 2))
                dve.tensor_tensor(w4[i][1][:, 1, :], raw4[i][:, 1, :], w4[i][0][:, 1, :], ALU.subtract).then_inc(w4_l2.sem, 1)

            def hidden_low(g, i, f):
                dve.wait_ge(h1_hi.sem, h1_hi.now(g, 8 * i + f + 1))
                dve.scalar_tensor_tensor(h4[i][1][:, f, :], ps[:, f % 4, 0:CAP], 0.0, h4[i][0][:, f, :], ALU.max, ALU.subtract
                                         ).then_inc(h1_lo.sem, 1)

            def rows_out(g, i):
                dve.wait_ge(d4.sem, d4.now(g, i + 1))
                dve.wait_ge(out_left.sem, out_left.before(g, i + 1))
                t = 4 * g + 2 * i
                sel = slice(t, t + 2) if isinstance(g, int) else bass.ds(t, 2)
                dve.tensor_copy(out_idx[i][:, :].rearrange("p (a o) -> p a o", o=1), xs[:, sel, D + 3:D + 4]).then_inc(idx4.sem, 1)
                for j in range(2):
                    row = xs[:, t + j, :] if isinstance(g, int) else xs[:, bass.ds(t + j, 1), :].rearrange("p a c -> p (a c)")
                    ins = dve.scalar_tensor_tensor(yo[i][j], ps[:, 4 + i, j * D:(j + 1) * D], row[:, D + 2:D + 3],
                                                   row[:, 0:D], ALU.mult, ALU.add)
                    ins.then_inc(y4.sem if j else ds4.sem, 1)

            def turn(g, last):
                for i in range(2):
                    nxt = (g, 1) if i == 0 else (g + 1, 0)
                    more = i == 0 or not last
                    if more:
                        if i == 1:
                            dve.wait_ge(s_xs[1], 16)
                        slots_norm(*nxt)
                    for f in range(8):
                        hidden_low(g, i, f)
                    if more:
                        slots_low(*nxt)
                        split_w2(*nxt)
                    rows_out(g, i)
            split_w2(0, 0)
            dve.wait_ge(s_xs[0], 16)
            slots_norm(0, 0)
            slots_low(0, 0)
            with dve.Fori(0, E // 2 - 1) as g:
                turn(g, False)
            turn(E // 2 - 1, True)

        @block.tensor
        def _(pe):
            for s in (xt_tr, pj_k, pj_v, pj_q, sc_q, sc_k, pv, o_tr, o_nt, wo, x1t, gt, up, dn,
                      nat, pv3):
                s.credit(pe)
            THREE = ((0, 0), (0, 1), (1, 0))

            def product(dst, left, right, last_of=None):
                n = 0
                for k in range(K2):
                    for i, j in THREE:
                        mm = pe.matmul(dst, left(i, k), right(j, k), start=(n == 0), stop=(n == 3 * K2 - 1))
                        n += 1
                return mm

            def logits0(n):
                if n >= 2:
                    pe.wait_ge(lgc, n - 1)
                product(ps[:, 4 + n % 2, :], lambda i, k: wr[i][:, 0, k, :], lambda j, k: xnT_all[j][:, k, n * GT:(n + 1) * GT]
                        ).then_inc(lg, 1)

            def gate_up(g, i):
                e, n, m = i // 8, i // 2 % 4, i % 2
                if i % 8 == 0:
                    pe.wait_ge(w2_hi.sem, w2_hi.now(g, e + 1))
                    pe.wait_ge(w2_lo.sem, w2_lo.now(g, e + 1))
                for bank, at0, prior, done in ((0, 0, sl, gt), (2, 2 * I0, hm, up)):
                    pe.wait_ge(prior.sem, prior.now(g, i - 1))
                    product(ps[:, bank + i % 2, :],
                            lambda a, k: w2s[e % 2][a][:, at0 + k * I0 + m * P:at0 + k * I0 + (m + 1) * P],
                            lambda b, k: xnT_all[b][:, k, n * GT:(n + 1) * GT]).then_inc(done.sem, 1)

            def k_project(g, m):
                if m == 0:
                    pe.wait_ge(c_hi.sem, c_hi.now(g, 1))
                    pe.wait_ge(c_lo.sem, c_lo.now(g, 1))
                    pe.wait_ge(mx_ok.sem, mx_ok.before(g, UNITS))
                product(ps[:, m, :], lambda i, k: wa[i][:, 1, k, m * P:(m + 1) * P], lambda j, k: cT[j][:, k, :]
                        ).then_inc(pj_k.sem, 1)

            def v_project(g, c):
                pe.wait_ge(ex.sem, ex.before(g, UNITS - 1))
                for i in range(2):
                    b = 2 * c + i
                    mm = product(ps[:, 2 + c, i * D:(i + 1) * D], lambda i, k: cT[i][:, k, b * P:(b + 1) * P],
                                 lambda j, k: wa[j][:, 2, k, :])
                mm.then_inc(pj_v.sem, 1)

            def q_project(g, m):
                if m == 0:
                    pe.wait_ge(xt_hi.sem, xt_hi.now(g, 2))
                    pe.wait_ge(xt_lo.sem, xt_lo.now(g, 2))
                    pe.wait_ge(ex.sem, ex.before(g, UNITS))
                product(ps[:, 4 + m, :], lambda i, k: wa[i][:, 0, k, m * P:(m + 1) * P], lambda j, k: xnT[j][:, k, :]
                        ).then_inc(pj_q.sem, 1)

            def xn_transpose(g, c):
                if c:
                    pe.wait_ge(xt_hi.sem, xt_hi.now(g, 1))
                    pe.wait_ge(xt_lo.sem, xt_lo.now(g, 1))
                elif not isinstance(g, int):
                    pe.wait_ge(x1_hi.sem, x1_hi.before(g - 1, GB))
                    pe.wait_ge(x1_lo.sem, x1_lo.before(g - 1, GB))
                for b in (2 * c, 2 * c + 1):
                    pe.wait_ge(ln0.sem, ln0.now(g, b + 1))
                    for k in range(K2):
                        mm = pe.transpose(ps[:, 7, (b % 2) * 256 + k * P:(b % 2) * 256 + (k + 1) * P],
                                          xn[b % 2][:, k * P:(k + 1) * P], ident)
                    mm.then_inc(xt_tr.sem, 1)

            def scores_for_max(g, u):
                b, gp = u // 2, u % 2
                if u == 0:
                    pe.wait_ge(k_m.sem, k_m.now(g, 2))
                    pe.wait_ge(k_lo.sem, k_lo.now(g, 2))
                    pe.wait_ge(q_hi.sem, q_hi.now(g, 2))
                else:
                    pe.wait_ge(mx_ok.sem, mx_ok.now(g, u))
                for j in range(2):
                    pe.matmul(ps[:, j, :], ident_b[:, :], hide[:, 0:1, :].to_broadcast([P, 4, P]), start=True, stop=False,
                              skip_group_check=True)
                for m in range(2):
                    for j in range(2):
                        r = 32 * (2 * gp + j)
                        mm = pe.matmul(ps[:, j, m * 256:(m + 1) * 256], qT[0][r:r + 32, m, b * P:(b + 1) * P],
                                       kM[r:r + 32, m, :, b * P:(b + 1) * P], start=False, stop=True,
                                       skip_group_check=True)
                mm.then_inc(sc_q.sem, 1)

            def scores_shifted(g, u):
                b, gp, bank = u // 2, u % 2, 2 + 2 * (u % 2)
                if u == 0:
                    pe.wait_ge(q_m.sem, q_m.now(g, 4))
                    pe.wait_ge(q_mh.sem, q_mh.now(g, 4))
                    pe.wait_ge(v_ok.sem, v_ok.now(g, 4))
                if u == 1:
                    pe.wait_ge(q_lo.sem, q_lo.now(g, 2))
                if u >= 2:
                    pe.wait_ge(ex.sem, ex.now(g, u - 1))
                for j in range(2):
                    pe.matmul(ps[:, bank + j, :], ident_b[:, :], hide[:, 1:2, :].to_broadcast([P, 4, P]), start=True, stop=False,
                              skip_group_check=True)
                for i, jj in THREE:
                    for m in range(2):
                        for j in range(2):
                            r = 32 * (2 * gp + j)
                            pe.matmul(ps[:, bank + j, m * 256:(m + 1) * 256], kT[i][r:r + 32, m, b * P:(b + 1) * P],
                                      qM[jj][r:r + 32, m, :, b * P:(b + 1) * P], start=False, stop=False,
                                      skip_group_check=True)

            def shift(g, u):
                bank = 2 + 2 * (u % 2)
                pe.wait_ge(dg.sem, dg.now(g, u + 1))
                for j in range(2):
                    mm = pe.matmul(ps[:, bank + j, :], ones_r[:, :], diag[u % 2][:, 4 * j:4 * j + 4, :],
                                   start=False, stop=True, skip_group_check=True)
                mm.then_inc(sc_k.sem, 1)

            def units(g, ga):
                def values(u):
                    b, gp = u // 2, u % 2
                    pe.wait_ge(ex.sem, ex.now(g, u + 1))
                    if gp == 0:
                        if b == 0:
                            pe.wait_ge(o_raw.sem, o_raw.before(g, GB))
                        else:
                            pe.wait_ge(o_raw.sem, o_raw.now(g, b))
                    for j in range(2):
                        c = 2 * gp + j
                        for s in range(4):
                            h = (s // 2) * 8 + c * 2 + s % 2
                            mm = pe.matmul(ps[32 * s:32 * s + 32, 6, c * P:(c + 1) * P], v0[:, b, h, :],
                                           probs[u % 2][:, 4 * j + s, :], start=True, stop=True, skip_group_check=True)
                    mm.then_inc(pv.sem, 1)

                def tail(b, step):
                    if step == 0:
                        pe.wait_ge(o_raw.sem, o_raw.now(g, b + 1))
                        pe.wait_ge(x1_lo.sem, x1_lo.now(g, b) if b else x1_lo.before(g, GB))
                        if b == 0 and ga is not None:
                            pe.wait_ge(xt_lo.sem, xt_lo.now(ga, 2))
                        for c in range(4):
                            mm = pe.transpose(ps[:, 7, c * P:(c + 1) * P], oT_raw[:, c, :], ident)
                        mm.then_inc(o_tr.sem, 1)
                    if step == 1:
                        pe.wait_ge(o_n.sem, o_n.now(g, b + 1))
                        for k in range(K2):
                            mm = pe.transpose(ps[:, 7, k * P:(k + 1) * P], o_tok[:, k * P:(k + 1) * P], ident)
                        mm.then_inc(o_nt.sem, 1)
                    if step == 2:
                        pe.wait_ge(oT_hi.sem, oT_hi.now(g, b + 1))
                        pe.wait_ge(oT_lo.sem, oT_lo.now(g, b + 1))
                        product(ps[:, 7, 256:512], lambda i, k: oT[i][:, k, :], lambda j, k: wa[j][:, 3, k, :]
                                ).then_inc(wo.sem, 1)
                    if step == 3:
                        pe.wait_ge(ln1.sem, ln1.now(g, b + 1))
                        for k in range(K2):
                            mm = pe.transpose(ps[:, 7, k * P:(k + 1) * P], xn[b % 2][:, k * P:(k + 1) * P], ident)
                        mm.then_inc(x1t.sem, 1)

                for u in range(1, UNITS):
                    if u + 1 < UNITS:
                        scores_for_max(g, u + 1)
                    if u >= 5 and u % 2:
                        tail((u - 5) // 2, 3)
                    if u >= 4 and u % 2 == 0:
                        tail((u - 4) // 2, 2)
                    if ga is not None and u == 2:
                        xn_transpose(ga, 0)
                    scores_shifted(g, u)
                    if u >= 3 and u % 2:
                        tail((u - 3) // 2, 0)
                    shift(g, u)
                    values(u - 1)
                    if ga is not None and u == 2:
                        xn_transpose(ga, 1)
                    if u >= 3 and u % 2:
                        tail((u - 3) // 2, 1)
                if ga is not None:
                    k_project(ga, 0)
                    values(UNITS - 1)
                    tail(2, 2)
                    k_project(ga, 1)
                    v_project(ga, 0)
                    v_project(ga, 1)
                    tail(2, 3)
                    q_project(ga, 0)
                    q_project(ga, 1)
                    tail(3, 0)
                    scores_for_max(ga, 0)
                    tail(3, 1)
                    tail(3, 2)
                    scores_shifted(ga, 0)
                    scores_for_max(ga, 1)
                    shift(ga, 0)
                    tail(3, 3)
                else:
                    values(UNITS - 1)
                    tail(2, 2)
                    pe.wait_ge(mx_ok.sem, mx_ok.total(G))
                    pe.wait_ge(ex.sem, ex.total(G))
                    gate_up(0, 0)
                    logits0(0)
                    logits0(1)
                    tail(2, 3)
                    gate_up(0, 1)
                    tail(3, 0)
                    logits0(2)
                    tail(3, 1)
                    gate_up(0, 2)
                    tail(3, 2)
                    gate_up(0, 3)
                    tail(3, 3)

            pe.wait_ge(s_wa_lo, 1)
            for m in range(2):
                k_project(0, m)
            pe.wait_ge(s_const, 16)
            xn_transpose(0, 0)
            pe.wait_ge(s_wa_lo, 2)
            for c in range(2):
                v_project(0, c)
            xn_transpose(0, 1)
            pe.wait_ge(s_wa_lo, 4)
            for m in range(2):
                q_project(0, m)
            pe.wait_ge(s_setup.sem, 8)
            scores_for_max(0, 0)
            scores_shifted(0, 0)
            scores_for_max(0, 1)
            shift(0, 0)
            with pe.Fori(0, G - 1) as g:
                units(g, g + 1)
            units(G - 1, None)

            pe.wait_ge(x1_lo.sem, x1_lo.total(G))
            logits0(3)
            pe.wait_ge(lgc, G)
            for t in range(B):
                mm = pe.transpose(ps[:, 7, t * E:(t + 1) * E], lgT[0:E, t * P:(t + 1) * P], ident[0:E, 0:E])
            mm.then_inc(lgt, 1)

            def down(g, c):
                e = c // 4
                pe.wait_ge(hh.sem, hh.now(g, 2 * c + 2))
                pe.wait_ge(hl.sem, hl.now(g, 2 * c + 2))
                pe.wait_ge(ac.sem, ac.now(g, c - 1))
                for j in range(4):
                    mm = product(ps[:, 4 + 2 * (c % 2) + j // 2, (j % 2) * D:(j % 2 + 1) * D],
                                 lambda a, k: hT[c % 2][a][:, k, j * P:(j + 1) * P],
                                 lambda b, k: w2s[e][b][:, 4 * I0 + k * D:4 * I0 + (k + 1) * D])
                mm.then_inc(dn.sem, 1)

            def pair2(g, last):
                for c in range(NC2):
                    down(g, c)
                    if c < NC2 - 2 or not last:
                        gate_up(g, 2 * c + 4)
                        gate_up(g, 2 * c + 5)
            pe.wait_ge(s_inh, 1)
            with pe.Fori(0, E // 2 - 1) as g:
                pair2(g, False)
            pair2(E // 2 - 1, True)

            for s in (nbt, pk3, pq3, s1, t1, a1, l1, l1t, loc1):
                s.credit(pe)
            pe.wait_ge(sl.sem, sl.total(E // 2))
            pe.wait_ge(hm.sem, hm.total(E // 2))
            pe.wait_ge(s_wa1_lo, 1)

            def turn3(ga, gb):
                def transposes3(g, b, xn3, bank, sig, done):
                    pe.wait_ge(sig.sem, sig.now(g, b + 1))
                    for k in range(K2):
                        mm = pe.transpose(ps[:, bank + b // 2, (b % 2) * 256 + k * P:(b % 2) * 256 + (k + 1) * P],
                                          xn3[b][:, k * P:(k + 1) * P], ident)
                    mm.then_inc(done.sem, 1)

                if gb is not None:
                    for b in range(GB):
                        pe.wait_ge(e1.sem, e1.now(gb, b + 1))
                        mm = pe.transpose(ps[:, 4, b * P:(b + 1) * P], sc1[:, b, :], ident)
                    mm.then_inc(t1.sem, 1)
                def k1_project():
                    pe.wait_ge(c3_hi.sem, c3_hi.now(ga, 1))
                    pe.wait_ge(c3_lo.sem, c3_lo.now(ga, 1))
                    pe.wait_ge(q1_ok.sem, q1_ok.before(ga, 2))
                    for m in range(2):
                        product(ps[:, m, :], lambda i, k: wa[i][:, 1, k, m * P:(m + 1) * P], lambda j, k: cT[j][:, k, :]
                                ).then_inc(pk3.sem, 1)
                if gb is None:
                    k1_project()
                if ga is not None:
                    pe.wait_ge(v1_ok.sem, v1_ok.before(ga, 2))
                    for b in range(GB):
                        transposes3(ga, b, xn_a, 2, na, nat)
                if gb is not None:
                    pe.wait_ge(p1_ok.sem, p1_ok.now(gb, 1))
                    pe.wait_ge(v1_ok.sem, v1_ok.now(gb, 2))
                    pe.wait_ge(nb_hi.sem, nb_hi.before(gb, 2))
                    pe.wait_ge(nb_lo.sem, nb_lo.before(gb, 2))
                    for b in range(GB):
                        mm = pe.matmul(ps[:, 6 + b // 2, (b % 2) * D:(b % 2 + 1) * D], p1T[:, b, :], v1[:, b, :], start=True, stop=True)
                        if b % 2:
                            mm.then_inc(a1.sem, 1)
                if ga is not None:
                    if gb is not None:
                        k1_project()
                    pe.wait_ge(na_hi.sem, na_hi.now(ga, 2))
                    pe.wait_ge(na_lo.sem, na_lo.now(ga, 2))
                    for c in range(2):
                        for i in range(2):
                            b = 2 * c + i
                            mm = product(ps[:, 2 + c, i * D:(i + 1) * D], lambda i, k: cT[i][:, k, b * P:(b + 1) * P],
                                         lambda j, k: wa[j][:, 2, k, :])
                        mm.then_inc(pv3.sem, 1)
                    pe.wait_ge(k1_ok.sem, k1_ok.now(ga, 2))
                    for m in range(2):
                        product(ps[:, m, :], lambda i, k: wa[i][:, 0, k, m * P:(m + 1) * P], lambda j, k: xnT[j][:, k, :]
                                ).then_inc(pq3.sem, 1)
                if gb is not None:
                    for b in range(GB):
                        transposes3(gb, b, xn_b, 6, nb, nbt)
                if ga is not None:
                    pe.wait_ge(q1_ok.sem, q1_ok.now(ga, 2))
                    if gb is None:
                        pe.wait_ge(ac.sem, ac.total(E // 2))
                    else:
                        pe.wait_ge(p1_ok.sem, p1_ok.before(ga, 1))
                    for b in range(GB):
                        for k in range(2):
                            mm = pe.matmul(ps[:, 4, b * P:(b + 1) * P], q1[:, k, b * P:(b + 1) * P], k1[:, k, b * P:(b + 1) * P],
                                           start=(k == 0), stop=(k == 1))
                    mm.then_inc(s1.sem, 1)
                if gb is not None:
                    pe.wait_ge(nb_hi.sem, nb_hi.now(gb, 2))
                    pe.wait_ge(nb_lo.sem, nb_lo.now(gb, 2))
                    pe.wait_ge(dest.sem, dest.before(gb, 1))
                    product(ps[:, 5, :], lambda i, k: wr[i][:, 1, k, :], lambda j, k: xnT_b[j][:, k, :]).then_inc(l1.sem, 1)
                if gb is not None:
                    pe.wait_ge(l1c.sem, l1c.now(gb, 1))
                    alone(pe)
                    for b in range(GB):
                        mm = pe.transpose(ps[:, 5, b * E:(b + 1) * E], lg1T[0:E, b * P:(b + 1) * P], ident[0:E, 0:E])
                    mm.then_inc(l1t.sem, 1)
                if gb is not None:
                    pe.wait_ge(oh1.sem, oh1.now(gb, 1))
                    place = ps[:, 5, GB * E:2 * GB * E].rearrange("p (b e) -> p b e", e=E)
                    pe.matmul(place, tri_b[:, :], oh_b[:, :, :], start=True, stop=False)
                    for b in range(GB - 1):
                        pe.matmul(place[:, b + 1:GB, :], ones_b[:, :], oh_b[:, b:b + 1, :].to_broadcast([P, GB - 1 - b, E]),
                                  start=False, stop=False, skip_group_check=True)
                    pe.matmul(place, ones_b[:, :], ones_before[:, :].rearrange("p (o e) -> p o e", o=1).to_broadcast([P, GB, E]),
                              start=False, stop=True).then_inc(loc1.sem, 1)
            turn3(0, None)
            with pe.Fori(0, G - 1) as g:
                turn3(g + 1, g)
            turn3(None, G - 1)

            for s in (xd_t, h1, d4):
                s.credit(pe)

            def slots_transposed(g, i):
                pe.wait_ge(xd_ok.sem, xd_ok.now(g, 2 * i + 2))
                pe.wait_ge(di_lo.sem, di_lo.before(g, i + 1))
                for j in range(2):
                    for k in range(K2):
                        mm = pe.transpose(ps[:, 6 + i, j * 256 + k * P:j * 256 + (k + 1) * P], xd[j][:, k * P:(k + 1) * P], ident)
                mm.then_inc(xd_t.sem, 1)

            def hidden(g, i, f):
                n = 8 * i + f
                if f == 0:
                    pe.wait_ge(di_hi.sem, di_hi.now(g, i + 1))
                    pe.wait_ge(di_lo.sem, di_lo.now(g, i + 1))
                    pe.wait_ge(w4_hi.sem, w4_hi.now(g, 2 * i + 1))
                    pe.wait_ge(w4_l1.sem, w4_l1.now(g, i + 1))
                pe.wait_ge(h1_lo.sem, h1_lo.now(g, n - 3) if n >= 4 else h1_lo.before(g, 16 - 3 + n))
                product(ps[:, f % 4, 0:CAP], lambda a, k: w4[i][a][:, 0, k * F1 + f * P:k * F1 + (f + 1) * P],
                        lambda b, k: diT[i][b][:, k, :]).then_inc(h1.sem, 1)

            def down4(g, i):
                pe.wait_ge(w4_hi.sem, w4_hi.now(g, 2 * i + 2))
                pe.wait_ge(w4_l2.sem, w4_l2.now(g, i + 1))
                pe.wait_ge(y4.sem, y4.before(g, i + 1))
                for j in range(2):
                    for f in range(8):
                        if j == 0:
                            pe.wait_ge(h1_lo.sem, h1_lo.now(g, 8 * i + f + 1))
                        for n, (a, b) in enumerate(THREE):
                            mm = pe.matmul(ps[:, 4 + i, j * D:(j + 1) * D], h4[i][a][:, f, j * P:(j + 1) * P],
                                           w4[i][b][:, 1, f * D:(f + 1) * D], start=(f == 0 and n == 0), stop=(f == 7 and n == 2))
                mm.then_inc(d4.sem, 1)

            def turn(g, last):
                for i in range(2):
                    for f in range(8):
                        hidden(g, i, f)
                    if i == 0 or not last:
                        slots_transposed(*((g, 1) if i == 0 else (g + 1, 0)))
                    down4(g, i)
            slots_transposed(0, 0)
            with pe.Fori(0, E // 2 - 1) as g:
                turn(g, False)
            turn(E // 2 - 1, True)

        @block.gpsimd
        def _(pool):
            for s in (c_lo, k_m, dg, xb_ok, w2q_hi, w2q_lo, w2_hi, w2_lo, c3_lo, w4_l1, out_left):
                s.credit(pool)

            def ctx0_low(g):
                pool.wait_ge(c_hi.sem, c_hi.now(g, 1))
                pool.tensor_tensor(cT[1], c_in, cT[0], ALU.subtract).then_inc(c_lo.sem, 1)

            def k_masks(g):
                for m in range(2):
                    pool.wait_ge(k_hi.sem, k_hi.now(g, m + 1))
                    pool.tensor_tensor(kM[:, m, :, :], kT[0][:, m:m + 1, :].to_broadcast([P, 2, GT]),
                                       parity[:, :].rearrange("p (r o) -> p r o", o=1).to_broadcast([P, 2, GT]), ALU.mult
                                       ).then_inc(k_m.sem, 1)

            def diagonals(g, u):
                pool.wait_ge(mx_ok.sem, mx_ok.now(g, u + 1))
                pool.wait_ge(sc_k.sem, sc_k.now(g, u - 1) if u >= 2 else sc_k.before(g, UNITS - 1 + u))
                pool.tensor_tensor(diag[u % 2], neg_ident[:, :].rearrange("p (o q) -> p o q", o=1).to_broadcast([P, 8, P]),
                                   mx[u % 2].rearrange("p (h o) -> p h o", o=1).to_broadcast([P, 8, P]), ALU.mult
                                   ).then_inc(dg.sem, 1)

            def units(g, ga):
                for u in range(1, UNITS):
                    if u > 1:
                        diagonals(g, u)
                    if ga is not None and u == 1:
                        ctx0_low(ga)
                    quarter = bass.ds(g * (W2C // 2), W2C // 2)
                    if u == 2:
                        pool.tensor_copy(w2_both[0][:, quarter], raw_both[:, quarter]).then_inc(w2q_hi.sem, 1)
                    if u == 3:
                        pool.wait_ge(w2q_hi.sem, w2q_hi.now(g, 1))
                        alone(pool)
                        pool.tensor_tensor(w2_both[1][:, quarter], raw_both[:, quarter], w2_both[0][:, quarter], ALU.subtract
                                           ).then_inc(w2q_lo.sem, 1)
                    if u >= 4:
                        b = u - 4
                        pool.wait_ge(ln0.sem, ln0.now(g, b + 1))
                        alone(pool)
                        xo = x_all[:, bass.ds(g * GB + b, 1), 0:D].rearrange("p a d -> p (a d)")
                        pool.tensor_tensor(xo, xo, bo0r, ALU.add).then_inc(xb_ok.sem, 1)
                if ga is not None:
                    k_masks(ga)
                    diagonals(ga, 0)
                    diagonals(ga, 1)

            pool.wait_ge(s_const, 16)
            pool.wait_ge(s_setup.sem, 6)
            k_masks(0)
            diagonals(0, 0)
            diagonals(0, 1)
            pool.wait_ge(s_fill, 1)
            pool.dma_start(slots[0:T, :].rearrange("(t p) c -> p t c", p=P),
                           fill[:, :].rearrange("p (o c) -> p o c", o=1).to_broadcast([P, T // P, ROW])).then_inc(s_disp, 16)
            pool.wait_ge(s_bo, 1)
            for i in range(2):
                pool.wait_ge(s_raw2[i], 16)
            with pool.Fori(0, G - 1) as g:
                units(g, g + 1)
            units(G - 1, None)
            pool.wait_ge(w2q_lo.sem, w2q_lo.total(G))
            pool.sem_inc(w2_hi.sem, 2)
            pool.sem_inc(w2_lo.sem, 2)
            with pool.Fori(1, E // 2) as g:
                for i in range(2):
                    pool.wait_ge(s_raw2[i], 16 * g + 16)
                    pool.wait_ge(dn.sem, dn.before(g, 4 * i + 4))
                    alone(pool)
                    pool.tensor_copy(w2s[i][0], raw[i]).then_inc(w2_hi.sem, 1)
                    pool.wait_ge(w2_hi.sem, w2_hi.now(g, i + 1))
                    pool.tensor_tensor(w2s[i][1], raw[i], w2s[i][0], ALU.subtract).then_inc(w2_lo.sem, 1)
            pool.wait_ge(s_wa1, 16)
            pool.wait_ge(wo.sem, wo.total(G))
            pool.tensor_copy(wa[0][:, 0:3, :, :], wa1_raw).then_inc(s_wa1_hi, 1)
            pool.wait_ge(s_wa1_hi, 1)
            pool.tensor_tensor(wa[1][:, 0:3, :, :], wa1_raw, wa[0][:, 0:3, :, :], ALU.subtract).then_inc(s_wa1_lo, 1)

            def split_w1(g, i):
                pool.wait_ge(w4_hi.sem, w4_hi.now(g, 2 * i + 1))
                pool.tensor_tensor(w4[i][1][:, 0, :], raw4[i][:, 0, :], w4[i][0][:, 0, :], ALU.subtract).then_inc(w4_l1.sem, 1)

            def ctx_low(g):
                pool.wait_ge(c3_hi.sem, c3_hi.now(g, 1))
                pool.tensor_tensor(cT[1], c_in, cT[0], ALU.subtract).then_inc(c3_lo.sem, 1)

            def dispatch(g):
                pool.wait_ge(dest.sem, dest.now(g, 1))
                for t in range(g * GB, g * GB + GB):
                    pool.indirect_dma_start(out=slots[:, :], out_offset=bass.IndirectOffsetOnAxis(ap=tok_idx[:, t:t + 1], axis=0),
                                            in_=x_all[:, t, :], in_offset=None).then_inc(s_disp, 16)
            ctx_low(0)
            pool.wait_ge(s_disp, 16)
            for g in range(1, G):
                ctx_low(g)
                if g >= 2:
                    dispatch(g - 2)
            dispatch(G - 2)
            split_w1(0, 0)
            dispatch(G - 1)

            def scatter(g, i):
                pool.wait_ge(y4.sem, y4.now(g, i + 1))
                pool.wait_ge(ds4.sem, ds4.now(g, i + 1))
                pool.wait_ge(idx4.sem, idx4.now(g, i + 1))
                alone(pool)
                for j in range(2):
                    pool.indirect_dma_start(out=out.rearrange("b s d -> (b s) d"),
                                            out_offset=bass.IndirectOffsetOnAxis(ap=out_idx[i][:, j:j + 1], axis=0),
                                            in_=yo[i][j], in_offset=None, bounds_check=T - 1, oob_is_err=False
                                            ).then_inc(s_sc[i], 16)

            def rows_have_left(g, i):
                pool.wait_ge(s_sc[i], 32 * g + 32)
                alone(pool)
                pool.sem_inc(out_left.sem, 1)

            def turn(g, last):
                for i in range(2):
                    scatter(g, i)
                    if not last:
                        split_w1(g + 1, i)
                    rows_have_left(g, i)
            split_w1(0, 1)
            with pool.Fori(0, E // 2 - 1) as g:
                turn(g, False)
            turn(E // 2 - 1, True)
            for i in range(2):
                pool.wait_ge(s_sc[i], 32 * (E // 2))


def layout(inputs):
    a = {k: np.asarray(v) for k, v in inputs.items()}
    mask0 = a["mask_1x1xSxS2_if1"][0, 0]
    rows = np.arange(D).reshape(2, 4, 2, DH).transpose(1, 0, 2, 3).reshape(-1)
    return {
        "x": a["x"], "ctxT": np.ascontiguousarray(a["ctx_1024"].reshape(T, D).T), "maskf": a["mask_BxSxS2_fk0"],
        "mask0": np.stack([mask0, mask0.T]),
        "gx": a["g_xattn"], "gf": a["g_ffn"],
        "wa0": np.stack([a["L0_xattn_Wq"].T, a["L0_xattn_Wk"].T, a["L0_xattn_Wv"].T, a["L0_xattn_Wo"].T[rows]]),
        "bcols": np.concatenate([a[n].reshape(2, P).T for n in ("L0_xattn_bq", "L0_xattn_bk", "L1_xattn_bq", "L1_xattn_bk")], axis=1),
        "bv0": a["L0_xattn_bv"], "bo0": a["L0_xattn_bo"],
        "w0": np.concatenate([a[f"L0_ffn_{n}"].reshape(E, K2, P, 256).transpose(0, 2, 1, 3).reshape(E, P, 512)
                              for n in ("Wg", "Wu", "Wd")], axis=2),
        "wrs": np.stack([a["L0_ffn_Wr"], a["L1_ffn_wg"]]), "temp": a["L0_ffn_temperature"],
        "wa1": np.stack([a["L1_xattn_Wq"], a["L1_xattn_Wk"], a["L1_xattn_Wv"]]),
        "bv1": a["L1_xattn_bv"],
        "w1": a["L1_ffn_w1"], "w2": a["L1_ffn_w2"], "const": constants(),
    }


def kernel(**inputs):
    from concourse import bacc
    from concourse.bass_utils import run_bass_kernel_spmd

    nc = bacc.Bacc("TRN2", target_bir_lowering=False, num_devices=1)
    arrays, args = {}, []
    for name, a in layout(inputs).items():
        a = np.ascontiguousarray(a)
        arrays[f"in_{name}"] = a
        args.append(nc.dram_tensor(f"in_{name}", a.shape, mybir.dt.from_np(a.dtype), kind="ExternalInput").ap())
    out = nc.dram_tensor("out", (B, S, D), F32, kind="ExternalOutput").ap()
    slots = nc.dram_tensor("slots", (2 * T, ROW), F32, kind="Internal").ap()
    block_kernel(nc, *args, out, slots)
    r = run_bass_kernel_spmd(nc, [arrays], core_ids=[0])
    return r.results[0]["out"]
```
